# Optimizing a Trainium2 kernel written in Bass

```python
import numpy as np
import jax
import jax.numpy as jnp

def _softmax(x, axis=-1):
    return jax.nn.softmax(x, axis=axis)

def _gelu(x):
    return jax.nn.gelu(x, approximate=True)

def _silu(x):
    return jax.nn.silu(x)

def _sigmoid(x):
    return jax.nn.sigmoid(x)

def _layernorm(x, axis=-1, eps=1e-05):
    m = jnp.mean(x, axis=axis, keepdims=True)
    v = jnp.var(x, axis=axis, keepdims=True)
    return (x - m) / jnp.sqrt(v + eps)

def _scatter_add(tgt, idx, src, axis=0):
    return tgt.at[idx].add(src)

def _segment_sum(src, seg, n):
    return jax.ops.segment_sum(src, seg, n)
kernel_name = 'mk_decoder_postln_d2_seqx_r8_7922b2'

def setup_inputs(seed: int=0):
    np.random.seed(seed)
    _w = jnp.asarray

    def _rec_inputs():
        import jax
        import jax.numpy as jnp
        _rk = jax.random.key(seed)
        x = -0.000125 + 0.9999 * jax.random.normal(jax.random.fold_in(_rk, 1), (4, 256, 256), jnp.float32)
        _lenS = 256 - jax.random.randint(jax.random.fold_in(_rk, 7), (4,), 0, max(1, 256 // 4) + 1, jnp.int32)
        _lenS2 = 256 - jax.random.randint(jax.random.fold_in(_rk, 8), (4,), 0, max(1, 256 // 4) + 1, jnp.int32)
        itok_BxS_13_99985 = jax.random.randint(jax.random.fold_in(_rk, 11), (4, 256), 13, 99986, jnp.int32)
        _ctx_2048P = jax.random.normal(jax.random.fold_in(_rk, 12), (4, 16, 256), jnp.float32)
        _ctx_2048c = jax.random.dirichlet(jax.random.fold_in(_rk, 512), 0.3 * jnp.ones((16,), jnp.float32), (4, 256))
        _ctx_2048t = jnp.einsum('bsk,bkd->bsd', _ctx_2048c, _ctx_2048P)
        _ctx_2048t = _ctx_2048t * jax.lax.rsqrt(jnp.mean(jnp.square(_ctx_2048t)) + 1e-12) * 0.953939
        ctx_2048 = 6.82029e-06 + 0.0200006 * (_ctx_2048t + 0.3 * jax.random.normal(jax.random.fold_in(_rk, 612), (4, 256, 256), jnp.float32))
        pos_BxS2 = jnp.broadcast_to(jnp.arange(256, dtype=jnp.int32), (4, 256))
        itok_BxS_4096_4607 = jax.random.randint(jax.random.fold_in(_rk, 14), (4, 256), 512, 576, jnp.int32)
        return (x, itok_BxS_13_99985, ctx_2048, pos_BxS2, itok_BxS_4096_4607)
    x, itok_BxS_13_99985, ctx_2048, pos_BxS2, itok_BxS_4096_4607 = _rec_inputs()

    def _L0_attn_setup():
        import jax, jax.numpy as jnp
        import numpy as np
        from jax import lax
        key = jax.random.key(seed)
        ks = jax.random.split(key, 8)
        B, L, H = (2, 128, 256)
        E = 2
        d = H * E
        S = 16
        R = 128
        sc = lambda fan_in: 1.0 / np.sqrt(fan_in)
        return {'x': jax.random.normal(ks[0], (B, L, H), jnp.float32), 'W_in': jax.random.normal(ks[1], (H, 2 * d), jnp.float32) * sc(H), 'conv_w': jax.random.normal(ks[2], (d, 1, 3), jnp.float32) * sc(3), 'conv_b': jnp.zeros((d,), jnp.float32), 'W_x': jax.random.normal(ks[3], (d, R + 2 * S), jnp.float32) * sc(d), 'W_dt': jax.random.normal(ks[4], (R, d), jnp.float32) * sc(R), 'b_dt': jnp.zeros((d,), jnp.float32), 'A_log': jnp.log(jnp.tile(jnp.arange(1, S + 1, dtype=jnp.float32), (d, 1))), 'D': jnp.ones((d,), jnp.float32), 'W_out': jax.random.normal(ks[5], (d, H), jnp.float32) * sc(d)}
    _L0_attn_all = _L0_attn_setup()
    _L0_attn_in = {k: v for k, v in _L0_attn_all.items() if k in ('W_in', 'conv_w', 'conv_b', 'W_x', 'W_dt', 'b_dt', 'A_log', 'D', 'W_out')}
    del _L0_attn_all

    def _L0_xattn_setup():
        import jax, jax.numpy as jnp
        import numpy as np
        B, S, D = (4, 512, 256)
        E = 4
        F = 1024 // E
        VOCAB = 12500
        key = jax.random.key(seed)
        k1, k2, k3, k4, k5 = jax.random.split(key, 5)
        hidden_states = jax.random.normal(k1, (B, S, D), dtype=jnp.float32)
        token_ids = jax.random.randint(k2, (B, S), 0, VOCAB, dtype=jnp.int64)
        Wg = jax.random.normal(k3, (E, F, D), dtype=jnp.float32) * 0.02
        Wu = jax.random.normal(k4, (E, F, D), dtype=jnp.float32) * 0.02
        Wd = jax.random.normal(k5, (E, D, F), dtype=jnp.float32) * 0.02
        return {'hidden_states': hidden_states, 'token_ids': token_ids, 'Wg': Wg, 'Wu': Wu, 'Wd': Wd}
    _L0_xattn_all = _L0_xattn_setup()
    _L0_xattn_in = {k: v for k, v in _L0_xattn_all.items() if k in ()}
    del _L0_xattn_all

    def _L0_ffn_setup():
        import jax, jax.numpy as jnp
        import numpy as np
        EPS = 1e-06
        K_STEPS = 4
        USE_GATING = True

        def layer_norm(x, gamma, beta):
            mu = jnp.mean(x, axis=-1, keepdims=True)
            var = jnp.mean(jnp.square(x - mu), axis=-1, keepdims=True)
            return (x - mu) * jax.lax.rsqrt(var + EPS) * gamma + beta
        key = jax.random.key(seed)
        B, L, D, H = (4, 512, 256, 1024)
        ks = jax.random.split(key, 16)
        s = 0.02
        return {'x': jax.random.normal(ks[0], (B, L, D), dtype=jnp.float32), 'in_gamma': jnp.ones((D,), jnp.float32), 'in_beta': jnp.zeros((D,), jnp.float32), 'agg_w': jax.random.normal(ks[1], (D, D), jnp.float32) * s, 'agg_b': jnp.zeros((D,), jnp.float32), 'pn_gamma': jnp.ones((D,), jnp.float32), 'pn_beta': jnp.zeros((D,), jnp.float32), 'd1_w': jax.random.normal(ks[2], (D, H), jnp.float32) * s, 'd1_b': jnp.zeros((H,), jnp.float32), 'd2_w': jax.random.normal(ks[3], (H, D), jnp.float32) * s, 'd2_b': jnp.zeros((D,), jnp.float32), 'bc_w': jax.random.normal(ks[4], (D, D), jnp.float32) * s, 'bc_b': jnp.zeros((D,), jnp.float32), 'gate_w': jax.random.normal(ks[5], (D, D), jnp.float32) * s, 'gate_b': jnp.zeros((D,), jnp.float32), 'out_gamma': jnp.ones((D,), jnp.float32), 'out_beta': jnp.zeros((D,), jnp.float32)}
    _L0_ffn_all = _L0_ffn_setup()
    _L0_ffn_in = {k: v for k, v in _L0_ffn_all.items() if k in ('in_gamma', 'in_beta', 'agg_w', 'agg_b', 'pn_gamma', 'pn_beta', 'd1_w', 'd1_b', 'd2_w', 'd2_b', 'bc_w', 'bc_b', 'gate_w', 'gate_b', 'out_gamma', 'out_beta')}
    del _L0_ffn_all

    def _L1_attn_setup():
        import jax, jax.numpy as jnp
        import numpy as np
        H, P, N, G, K, CS = (64, 64, 128, 8, 4, 32)
        EMB = 256
        INTER = H * P
        CONV_DIM = INTER + 2 * G * N
        PROJ = INTER + CONV_DIM + H
        EPS = 1e-06

        def _segsum(x):
            L = x.shape[-1]
            lo = jnp.tril(jnp.ones((L, L), bool), -1)
            cum = jnp.cumsum(jnp.where(lo, x[..., None], 0.0), axis=-2)
            return jnp.where(jnp.tril(jnp.ones((L, L), bool)), cum, -jnp.inf)

        def _ssd(input_states, in_proj_w, conv_w, conv_b, dt_bias, A_log, D, norm_w, out_proj_w):
            b, s, _ = input_states.shape
            proj = input_states @ in_proj_w.T
            gate = proj[..., :INTER]
            h_BC = proj[..., INTER:INTER + CONV_DIM]
            dt = proj[..., INTER + CONV_DIM:]
            xc = jnp.transpose(h_BC, (0, 2, 1))
            yc = jax.lax.conv_general_dilated(xc, conv_w, (1,), [(K - 1, 0)], feature_group_count=CONV_DIM, dimension_numbers=('NCH', 'OIH', 'NCH'))
            h_BC = jax.nn.silu(jnp.transpose(yc + conv_b[None, :, None], (0, 2, 1)))
            hidden = h_BC[..., :INTER]
            Bx = h_BC[..., INTER:INTER + G * N]
            Cx = h_BC[..., INTER + G * N:]
            A = -jnp.exp(A_log)
            dt2 = jax.nn.softplus(dt + dt_bias)
            hid = hidden.reshape(b, s, H, P)
            pad = (CS - s % CS) % CS
            total = s + pad
            n_c = total // CS

            def padseq(t):
                return jnp.pad(t, [(0, 0), (0, pad)] + [(0, 0)] * (t.ndim - 2))
            D_res = padseq(hid) * D[None, None, :, None]
            hid_c = padseq(hid * dt2[..., None]).reshape(b, n_c, CS, H, P)
            rep = H // G
            B_c = padseq(jnp.tile(Bx.reshape(b, s, G, N), (1, 1, rep, 1))).reshape(b, n_c, CS, H, N)
            C_c = padseq(jnp.tile(Cx.reshape(b, s, G, N), (1, 1, rep, 1))).reshape(b, n_c, CS, H, N)
            A_c = jnp.transpose(padseq(A * dt2).reshape(b, n_c, CS, H), (0, 3, 1, 2))
            A_cum = jnp.cumsum(A_c, axis=-1)
            L = jnp.exp(_segsum(A_c))
            Gm = jnp.einsum('bcihn,bcjhn->bcijh', C_c, B_c)
            M = Gm * jnp.transpose(L, (0, 2, 3, 4, 1))
            Yd = jnp.einsum('bcijh,bcjhp->bcihp', M, hid_c)
            decay = jnp.exp(A_cum[..., -1:] - A_cum)
            B_dec = B_c * jnp.transpose(decay, (0, 2, 3, 1))[..., None]
            state = jnp.einsum('bclhn,bclhp->bchpn', B_dec, hid_c)
            Sd_out = jnp.exp(A_cum)
            Yoff = jnp.einsum('bclhn,bchpn->bclhp', C_c, state) * jnp.transpose(Sd_out, (0, 2, 3, 1))[..., None]
            y = (Yd + Yoff + D_res.reshape(b, n_c, CS, H, P)).reshape(b, total, H, P)[:, :s]
            y = y.reshape(b, s, INTER)
            yg = y * jax.nn.silu(gate)
            var = jnp.mean(yg * yg, axis=-1, keepdims=True)
            normed = norm_w * (yg * jax.lax.rsqrt(var + EPS))
            return normed @ out_proj_w.T
        key = jax.random.key(seed)
        ks = jax.random.split(key, 4)
        return {'input_states': jax.random.normal(ks[0], (1, 512, EMB), jnp.float32), 'in_proj_w': jax.random.normal(ks[1], (PROJ, EMB), jnp.float32) * 0.02, 'conv_w': jax.random.normal(ks[2], (CONV_DIM, 1, K), jnp.float32) * 0.1, 'conv_b': jnp.zeros((CONV_DIM,), jnp.float32), 'dt_bias': jnp.ones((H,), jnp.float32), 'A_log': jnp.log(jnp.arange(1, H + 1, dtype=jnp.float32)), 'D': jnp.ones((H,), jnp.float32), 'norm_w': jnp.ones((INTER,), jnp.float32), 'out_proj_w': jax.random.normal(ks[3], (EMB, INTER), jnp.float32) * 0.02}
    _L1_attn_all = _L1_attn_setup()
    _L1_attn_in = {k: v for k, v in _L1_attn_all.items() if k in ('in_proj_w', 'conv_w', 'conv_b', 'dt_bias', 'A_log', 'D', 'norm_w', 'out_proj_w')}
    del _L1_attn_all

    def _L1_xattn_setup():
        import jax, jax.numpy as jnp
        import numpy as np
        B, CTX, DRAFT, D = (2, 512, 64, 256)
        H, KVH, HD = (16, 4, 128)
        N_REP = H // KVH
        EPS = 1e-06
        THETA = 10000.0
        SCALE = 1.0 / np.sqrt(HD).astype(np.float32)

        def _rms_norm(x, w):
            v = jnp.mean(jnp.square(x.astype(jnp.float32)), axis=-1, keepdims=True)
            return (w * (x.astype(jnp.float32) * jax.lax.rsqrt(v + EPS))).astype(x.dtype)

        def _rotate_half(x):
            x1, x2 = jnp.split(x, 2, axis=-1)
            return jnp.concatenate((-x2, x1), axis=-1)

        def _rope(x, pos):
            inv_freq = 1.0 / THETA ** (jnp.arange(0, HD, 2, dtype=jnp.float32) / HD)
            freqs = pos.astype(jnp.float32)[:, None, :, None] * inv_freq
            emb = jnp.concatenate((freqs, freqs), axis=-1)
            return x * jnp.cos(emb) + _rotate_half(x) * jnp.sin(emb)
        key = jax.random.key(seed)
        ks = jax.random.split(key, 6)
        return {'draft_hidden': jax.random.normal(ks[0], (B, DRAFT, D), jnp.float32), 'context_hidden': jax.random.normal(ks[1], (B, CTX, D), jnp.float32), 'Wq': jax.random.normal(ks[2], (H * HD, D), jnp.float32) * 0.02, 'Wk': jax.random.normal(ks[3], (KVH * HD, D), jnp.float32) * 0.02, 'Wv': jax.random.normal(ks[4], (KVH * HD, D), jnp.float32) * 0.02, 'Wo': jax.random.normal(ks[5], (D, H * HD), jnp.float32) * 0.02, 'q_norm_w': jnp.ones((HD,), jnp.float32), 'k_norm_w': jnp.ones((HD,), jnp.float32), 'context_position_ids': jnp.broadcast_to(jnp.arange(CTX, dtype=jnp.int32), (B, CTX)), 'draft_position_ids': jnp.broadcast_to(CTX + jnp.arange(DRAFT, dtype=jnp.int32), (B, DRAFT))}
    _L1_xattn_all = _L1_xattn_setup()
    _L1_xattn_in = {k: v for k, v in _L1_xattn_all.items() if k in ('Wq', 'Wk', 'Wv', 'Wo', 'q_norm_w', 'k_norm_w')}
    del _L1_xattn_all

    def _L1_ffn_setup():
        import jax, jax.numpy as jnp
        import numpy as np
        E = 8
        TOP_K = 2
        H = 256
        I_MOE = 176
        I_SH = 704
        B, S = (2, 256)

        def _moe_forward(hidden_states, router_weight, gate_up_proj, down_proj, sh_gate_w, sh_up_w, sh_down_w, shared_gate_w):
            b, s, h = hidden_states.shape
            x = hidden_states.reshape(-1, h)
            shared = jnp.einsum('ti,hi->th', jax.nn.silu(x @ sh_gate_w.T) * (x @ sh_up_w.T), sh_down_w)
            logits = x @ router_weight.T
            probs = jax.nn.softmax(logits.astype(jnp.float32), axis=-1)
            top_v, top_i = jax.lax.top_k(probs, TOP_K)
            top_v = top_v / top_v.sum(axis=-1, keepdims=True)
            combine = (jax.nn.one_hot(top_i, E, dtype=top_v.dtype) * top_v[..., None]).sum(axis=1)
            out = jnp.zeros_like(x)
            for e in range(E):
                gu = x @ gate_up_proj[e].T
                gate, up = (gu[:, :I_MOE], gu[:, I_MOE:])
                cur = jax.nn.silu(gate) * up @ down_proj[e].T
                out = out + cur * combine[:, e:e + 1]
            out = out + jax.nn.sigmoid(x @ shared_gate_w.T) * shared
            return out.reshape(b, s, h)
        key = jax.random.key(seed)
        ks = jax.random.split(key, 8)
        scale = 0.02
        return {'hidden_states': jax.random.normal(ks[0], (B, S, H), dtype=jnp.float32), 'router_weight': jax.random.normal(ks[1], (E, H), dtype=jnp.float32) * scale, 'gate_up_proj': jax.random.normal(ks[2], (E, 2 * I_MOE, H), dtype=jnp.float32) * scale, 'down_proj': jax.random.normal(ks[3], (E, H, I_MOE), dtype=jnp.float32) * scale, 'sh_gate_w': jax.random.normal(ks[4], (I_SH, H), dtype=jnp.float32) * scale, 'sh_up_w': jax.random.normal(ks[5], (I_SH, H), dtype=jnp.float32) * scale, 'sh_down_w': jax.random.normal(ks[6], (H, I_SH), dtype=jnp.float32) * scale, 'shared_gate_w': jax.random.normal(ks[7], (1, H), dtype=jnp.float32) * scale}
    _L1_ffn_all = _L1_ffn_setup()
    _L1_ffn_in = {k: v for k, v in _L1_ffn_all.items() if k in ('router_weight', 'gate_up_proj', 'down_proj', 'sh_gate_w', 'sh_up_w', 'sh_down_w', 'shared_gate_w')}
    del _L1_ffn_all
    return {'x': x, 'itok_BxS_13_99985': itok_BxS_13_99985, 'ctx_2048': ctx_2048, 'pos_BxS2': pos_BxS2, 'itok_BxS_4096_4607': itok_BxS_4096_4607, 'L0_attn_W_in': _L0_attn_in['W_in'], 'L0_attn_conv_w': _L0_attn_in['conv_w'], 'L0_attn_conv_b': _L0_attn_in['conv_b'], 'L0_attn_W_x': _L0_attn_in['W_x'], 'L0_attn_W_dt': _L0_attn_in['W_dt'], 'L0_attn_b_dt': _L0_attn_in['b_dt'], 'L0_attn_A_log': _L0_attn_in['A_log'], 'L0_attn_D': _L0_attn_in['D'], 'L0_attn_W_out': _L0_attn_in['W_out'], 'L0_ffn_in_gamma': _L0_ffn_in['in_gamma'], 'L0_ffn_in_beta': _L0_ffn_in['in_beta'], 'L0_ffn_agg_w': _L0_ffn_in['agg_w'], 'L0_ffn_agg_b': _L0_ffn_in['agg_b'], 'L0_ffn_pn_gamma': _L0_ffn_in['pn_gamma'], 'L0_ffn_pn_beta': _L0_ffn_in['pn_beta'], 'L0_ffn_d1_w': _L0_ffn_in['d1_w'], 'L0_ffn_d1_b': _L0_ffn_in['d1_b'], 'L0_ffn_d2_w': _L0_ffn_in['d2_w'], 'L0_ffn_d2_b': _L0_ffn_in['d2_b'], 'L0_ffn_bc_w': _L0_ffn_in['bc_w'], 'L0_ffn_bc_b': _L0_ffn_in['bc_b'], 'L0_ffn_gate_w': _L0_ffn_in['gate_w'], 'L0_ffn_gate_b': _L0_ffn_in['gate_b'], 'L0_ffn_out_gamma': _L0_ffn_in['out_gamma'], 'L0_ffn_out_beta': _L0_ffn_in['out_beta'], 'L1_attn_in_proj_w': _L1_attn_in['in_proj_w'], 'L1_attn_conv_w': _L1_attn_in['conv_w'], 'L1_attn_conv_b': _L1_attn_in['conv_b'], 'L1_attn_dt_bias': _L1_attn_in['dt_bias'], 'L1_attn_A_log': _L1_attn_in['A_log'], 'L1_attn_D': _L1_attn_in['D'], 'L1_attn_norm_w': _L1_attn_in['norm_w'], 'L1_attn_out_proj_w': _L1_attn_in['out_proj_w'], 'L1_xattn_Wq': _L1_xattn_in['Wq'], 'L1_xattn_Wk': _L1_xattn_in['Wk'], 'L1_xattn_Wv': _L1_xattn_in['Wv'], 'L1_xattn_Wo': _L1_xattn_in['Wo'], 'L1_xattn_q_norm_w': _L1_xattn_in['q_norm_w'], 'L1_xattn_k_norm_w': _L1_xattn_in['k_norm_w'], 'L1_ffn_router_weight': _L1_ffn_in['router_weight'], 'L1_ffn_gate_up_proj': _L1_ffn_in['gate_up_proj'], 'L1_ffn_down_proj': _L1_ffn_in['down_proj'], 'L1_ffn_sh_gate_w': _L1_ffn_in['sh_gate_w'], 'L1_ffn_sh_up_w': _L1_ffn_in['sh_up_w'], 'L1_ffn_sh_down_w': _L1_ffn_in['sh_down_w'], 'L1_ffn_shared_gate_w': _L1_ffn_in['shared_gate_w']}

def reference(x, itok_BxS_13_99985, ctx_2048, pos_BxS2, itok_BxS_4096_4607, L0_attn_W_in, L0_attn_conv_w, L0_attn_conv_b, L0_attn_W_x, L0_attn_W_dt, L0_attn_b_dt, L0_attn_A_log, L0_attn_D, L0_attn_W_out, L0_ffn_in_gamma, L0_ffn_in_beta, L0_ffn_agg_w, L0_ffn_agg_b, L0_ffn_pn_gamma, L0_ffn_pn_beta, L0_ffn_d1_w, L0_ffn_d1_b, L0_ffn_d2_w, L0_ffn_d2_b, L0_ffn_bc_w, L0_ffn_bc_b, L0_ffn_gate_w, L0_ffn_gate_b, L0_ffn_out_gamma, L0_ffn_out_beta, L1_attn_in_proj_w, L1_attn_conv_w, L1_attn_conv_b, L1_attn_dt_bias, L1_attn_A_log, L1_attn_D, L1_attn_norm_w, L1_attn_out_proj_w, L1_xattn_Wq, L1_xattn_Wk, L1_xattn_Wv, L1_xattn_Wo, L1_xattn_q_norm_w, L1_xattn_k_norm_w, L1_ffn_router_weight, L1_ffn_gate_up_proj, L1_ffn_down_proj, L1_ffn_sh_gate_w, L1_ffn_sh_up_w, L1_ffn_sh_down_w, L1_ffn_shared_gate_w):
    import jax
    import jax.numpy as jnp

    def _L0_attn_ref(x, W_in, conv_w, conv_b, W_x, W_dt, b_dt, A_log, D, W_out):
        import jax, jax.numpy as jnp
        import numpy as np
        from jax import lax
        d = conv_b.shape[0]
        S = A_log.shape[1]
        R = W_dt.shape[0]
        xz = x @ W_in
        xp, z = jnp.split(xz, 2, axis=-1)
        xc = lax.conv_general_dilated(jnp.transpose(xp, (0, 2, 1)), conv_w, (1,), [(1, 1)], feature_group_count=d, dimension_numbers=('NCH', 'OIH', 'NCH'))
        xc = jnp.transpose(xc + conv_b[None, :, None], (0, 2, 1))
        xc = jax.nn.silu(xc)
        x_dbl = xc @ W_x
        dt_in = x_dbl[..., :R]
        Bm = x_dbl[..., R:R + S]
        Cm = x_dbl[..., R + S:]
        dt = jax.nn.softplus(dt_in @ W_dt + b_dt)
        A = -jnp.exp(A_log)

        def step(h, ins):
            u_t, dt_t, B_t, C_t = ins
            dA = jnp.exp(dt_t[:, :, None] * A)
            h = dA * h + dt_t[:, :, None] * B_t[:, None, :] * u_t[:, :, None]
            y_t = jnp.einsum('bds,bs->bd', h, C_t)
            return (h, y_t)
        h0 = jnp.zeros((x.shape[0], d, S), xc.dtype)
        xsT = (jnp.swapaxes(xc, 0, 1), jnp.swapaxes(dt, 0, 1), jnp.swapaxes(Bm, 0, 1), jnp.swapaxes(Cm, 0, 1))
        _, yT = lax.scan(step, h0, xsT)
        y = jnp.swapaxes(yT, 0, 1) + xc * D
        y = y * jax.nn.silu(z)
        return y @ W_out

    def _L0_xattn_ref(hidden_states, token_ids, Wg, Wu, Wd):
        import jax, jax.numpy as jnp
        import numpy as np
        B, S, D = (4, 512, 256)
        E = 4
        F = 1024 // E
        VOCAB = 12500
        tokens_per_expert = VOCAB // E
        tid = jnp.clip(token_ids, 0, VOCAB - 1)
        expert_ids = jnp.minimum(tid // tokens_per_expert, E - 1)
        out = jnp.zeros_like(hidden_states)
        for e in range(E):
            g = jax.nn.silu(jnp.einsum('bsd,fd->bsf', hidden_states, Wg[e]))
            u = jnp.einsum('bsd,fd->bsf', hidden_states, Wu[e])
            y = jnp.einsum('bsf,df->bsd', g * u, Wd[e])
            out = jnp.where((expert_ids == e)[..., None], y, out)
        return out

    def _L0_ffn_ref(x, in_gamma, in_beta, agg_w, agg_b, pn_gamma, pn_beta, d1_w, d1_b, d2_w, d2_b, bc_w, bc_b, gate_w, gate_b, out_gamma, out_beta):
        import jax, jax.numpy as jnp
        import numpy as np
        EPS = 1e-06
        K_STEPS = 4
        USE_GATING = True

        def layer_norm(x, gamma, beta):
            mu = jnp.mean(x, axis=-1, keepdims=True)
            var = jnp.mean(jnp.square(x - mu), axis=-1, keepdims=True)
            return (x - mu) * jax.lax.rsqrt(var + EPS) * gamma + beta
        x_norm = layer_norm(x, in_gamma, in_beta)
        thought = x_norm[:, -1, :] @ agg_w + agg_b
        for _ in range(K_STEPS):
            t = layer_norm(thought, pn_gamma, pn_beta)
            t = jax.nn.gelu(t @ d1_w + d1_b, approximate=False)
            thought = thought + (t @ d2_w + d2_b)
        broadcast = (thought @ bc_w + bc_b)[:, None, :]
        if USE_GATING:
            gate = jax.nn.sigmoid(x @ gate_w + gate_b)
            out = x + gate * broadcast
        else:
            out = x + broadcast
        return layer_norm(out, out_gamma, out_beta)

    def _L1_attn_ref(input_states, in_proj_w, conv_w, conv_b, dt_bias, A_log, D, norm_w, out_proj_w):
        import jax, jax.numpy as jnp
        import numpy as np
        H, P, N, G, K, CS = (64, 64, 128, 8, 4, 32)
        EMB = 256
        INTER = H * P
        CONV_DIM = INTER + 2 * G * N
        PROJ = INTER + CONV_DIM + H
        EPS = 1e-06

        def _segsum(x):
            L = x.shape[-1]
            lo = jnp.tril(jnp.ones((L, L), bool), -1)
            cum = jnp.cumsum(jnp.where(lo, x[..., None], 0.0), axis=-2)
            return jnp.where(jnp.tril(jnp.ones((L, L), bool)), cum, -jnp.inf)

        def _ssd(input_states, in_proj_w, conv_w, conv_b, dt_bias, A_log, D, norm_w, out_proj_w):
            b, s, _ = input_states.shape
            proj = input_states @ in_proj_w.T
            gate = proj[..., :INTER]
            h_BC = proj[..., INTER:INTER + CONV_DIM]
            dt = proj[..., INTER + CONV_DIM:]
            xc = jnp.transpose(h_BC, (0, 2, 1))
            yc = jax.lax.conv_general_dilated(xc, conv_w, (1,), [(K - 1, 0)], feature_group_count=CONV_DIM, dimension_numbers=('NCH', 'OIH', 'NCH'))
            h_BC = jax.nn.silu(jnp.transpose(yc + conv_b[None, :, None], (0, 2, 1)))
            hidden = h_BC[..., :INTER]
            Bx = h_BC[..., INTER:INTER + G * N]
            Cx = h_BC[..., INTER + G * N:]
            A = -jnp.exp(A_log)
            dt2 = jax.nn.softplus(dt + dt_bias)
            hid = hidden.reshape(b, s, H, P)
            pad = (CS - s % CS) % CS
            total = s + pad
            n_c = total // CS

            def padseq(t):
                return jnp.pad(t, [(0, 0), (0, pad)] + [(0, 0)] * (t.ndim - 2))
            D_res = padseq(hid) * D[None, None, :, None]
            hid_c = padseq(hid * dt2[..., None]).reshape(b, n_c, CS, H, P)
            rep = H // G
            B_c = padseq(jnp.tile(Bx.reshape(b, s, G, N), (1, 1, rep, 1))).reshape(b, n_c, CS, H, N)
            C_c = padseq(jnp.tile(Cx.reshape(b, s, G, N), (1, 1, rep, 1))).reshape(b, n_c, CS, H, N)
            A_c = jnp.transpose(padseq(A * dt2).reshape(b, n_c, CS, H), (0, 3, 1, 2))
            A_cum = jnp.cumsum(A_c, axis=-1)
            L = jnp.exp(_segsum(A_c))
            Gm = jnp.einsum('bcihn,bcjhn->bcijh', C_c, B_c)
            M = Gm * jnp.transpose(L, (0, 2, 3, 4, 1))
            Yd = jnp.einsum('bcijh,bcjhp->bcihp', M, hid_c)
            decay = jnp.exp(A_cum[..., -1:] - A_cum)
            B_dec = B_c * jnp.transpose(decay, (0, 2, 3, 1))[..., None]
            state = jnp.einsum('bclhn,bclhp->bchpn', B_dec, hid_c)
            Sd_out = jnp.exp(A_cum)
            Yoff = jnp.einsum('bclhn,bchpn->bclhp', C_c, state) * jnp.transpose(Sd_out, (0, 2, 3, 1))[..., None]
            y = (Yd + Yoff + D_res.reshape(b, n_c, CS, H, P)).reshape(b, total, H, P)[:, :s]
            y = y.reshape(b, s, INTER)
            yg = y * jax.nn.silu(gate)
            var = jnp.mean(yg * yg, axis=-1, keepdims=True)
            normed = norm_w * (yg * jax.lax.rsqrt(var + EPS))
            return normed @ out_proj_w.T
        return _ssd(input_states, in_proj_w, conv_w, conv_b, dt_bias, A_log, D, norm_w, out_proj_w)

    def _L1_xattn_ref(draft_hidden, context_hidden, Wq, Wk, Wv, Wo, q_norm_w, k_norm_w, context_position_ids, draft_position_ids):
        import jax, jax.numpy as jnp
        import numpy as np
        B, CTX, DRAFT, D = (2, 512, 64, 256)
        H, KVH, HD = (16, 4, 128)
        N_REP = H // KVH
        EPS = 1e-06
        THETA = 10000.0
        SCALE = 1.0 / np.sqrt(HD).astype(np.float32)

        def _rms_norm(x, w):
            v = jnp.mean(jnp.square(x.astype(jnp.float32)), axis=-1, keepdims=True)
            return (w * (x.astype(jnp.float32) * jax.lax.rsqrt(v + EPS))).astype(x.dtype)

        def _rotate_half(x):
            x1, x2 = jnp.split(x, 2, axis=-1)
            return jnp.concatenate((-x2, x1), axis=-1)

        def _rope(x, pos):
            inv_freq = 1.0 / THETA ** (jnp.arange(0, HD, 2, dtype=jnp.float32) / HD)
            freqs = pos.astype(jnp.float32)[:, None, :, None] * inv_freq
            emb = jnp.concatenate((freqs, freqs), axis=-1)
            return x * jnp.cos(emb) + _rotate_half(x) * jnp.sin(emb)
        bsz, draft_len, _ = draft_hidden.shape
        ctx_len = context_hidden.shape[1]
        total_len = ctx_len + draft_len
        q = (draft_hidden @ Wq.T).reshape(bsz, draft_len, H, HD)
        q = _rms_norm(q, q_norm_w).transpose(0, 2, 1, 3)
        kv_in = jnp.concatenate([context_hidden, draft_hidden], axis=1)
        k = (kv_in @ Wk.T).reshape(bsz, total_len, KVH, HD)
        v = (kv_in @ Wv.T).reshape(bsz, total_len, KVH, HD).transpose(0, 2, 1, 3)
        k = _rms_norm(k, k_norm_w).transpose(0, 2, 1, 3)
        full_position_ids = jnp.concatenate([context_position_ids, draft_position_ids], axis=1)
        q = _rope(q, draft_position_ids)
        k = _rope(k, full_position_ids)
        k = jnp.repeat(k, N_REP, axis=1)
        v = jnp.repeat(v, N_REP, axis=1)
        scores = jnp.einsum('bhqd,bhkd->bhqk', q, k) * SCALE
        probs = jax.nn.softmax(scores, axis=-1)
        attn = jnp.einsum('bhqk,bhkd->bhqd', probs, v)
        attn = attn.transpose(0, 2, 1, 3).reshape(bsz, draft_len, H * HD)
        return attn @ Wo.T

    def _L1_ffn_ref(hidden_states, router_weight, gate_up_proj, down_proj, sh_gate_w, sh_up_w, sh_down_w, shared_gate_w):
        import jax, jax.numpy as jnp
        import numpy as np
        E = 8
        TOP_K = 2
        H = 256
        I_MOE = 176
        I_SH = 704
        B, S = (2, 256)

        def _moe_forward(hidden_states, router_weight, gate_up_proj, down_proj, sh_gate_w, sh_up_w, sh_down_w, shared_gate_w):
            b, s, h = hidden_states.shape
            x = hidden_states.reshape(-1, h)
            shared = jnp.einsum('ti,hi->th', jax.nn.silu(x @ sh_gate_w.T) * (x @ sh_up_w.T), sh_down_w)
            logits = x @ router_weight.T
            probs = jax.nn.softmax(logits.astype(jnp.float32), axis=-1)
            top_v, top_i = jax.lax.top_k(probs, TOP_K)
            top_v = top_v / top_v.sum(axis=-1, keepdims=True)
            combine = (jax.nn.one_hot(top_i, E, dtype=top_v.dtype) * top_v[..., None]).sum(axis=1)
            out = jnp.zeros_like(x)
            for e in range(E):
                gu = x @ gate_up_proj[e].T
                gate, up = (gu[:, :I_MOE], gu[:, I_MOE:])
                cur = jax.nn.silu(gate) * up @ down_proj[e].T
                out = out + cur * combine[:, e:e + 1]
            out = out + jax.nn.sigmoid(x @ shared_gate_w.T) * shared
            return out.reshape(b, s, h)
        return _moe_forward(hidden_states, router_weight, gate_up_proj, down_proj, sh_gate_w, sh_up_w, sh_down_w, shared_gate_w)
    x = _layernorm(x + _L0_attn_ref(x, L0_attn_W_in, L0_attn_conv_w, L0_attn_conv_b, L0_attn_W_x, L0_attn_W_dt, L0_attn_b_dt, L0_attn_A_log, L0_attn_D, L0_attn_W_out), axis=-1)
    x = _layernorm(x + _L0_xattn_ref(x, itok_BxS_13_99985, ctx_2048, ctx_2048, ctx_2048), axis=-1)
    x = _layernorm(x + _L0_ffn_ref(x, L0_ffn_in_gamma, L0_ffn_in_beta, L0_ffn_agg_w, L0_ffn_agg_b, L0_ffn_pn_gamma, L0_ffn_pn_beta, L0_ffn_d1_w, L0_ffn_d1_b, L0_ffn_d2_w, L0_ffn_d2_b, L0_ffn_bc_w, L0_ffn_bc_b, L0_ffn_gate_w, L0_ffn_gate_b, L0_ffn_out_gamma, L0_ffn_out_beta), axis=-1)
    x = _layernorm(x + _L1_attn_ref(x, L1_attn_in_proj_w, L1_attn_conv_w, L1_attn_conv_b, L1_attn_dt_bias, L1_attn_A_log, L1_attn_D, L1_attn_norm_w, L1_attn_out_proj_w), axis=-1)
    x = _layernorm(x + _L1_xattn_ref(x, ctx_2048, L1_xattn_Wq, L1_xattn_Wk, L1_xattn_Wv, L1_xattn_Wo, L1_xattn_q_norm_w, L1_xattn_k_norm_w, pos_BxS2, itok_BxS_4096_4607), axis=-1)
    x = _layernorm(x + _L1_ffn_ref(x, L1_ffn_router_weight, L1_ffn_gate_up_proj, L1_ffn_down_proj, L1_ffn_sh_gate_w, L1_ffn_sh_up_w, L1_ffn_sh_down_w, L1_ffn_shared_gate_w), axis=-1)
    return x

_drawn_inputs = setup_inputs


def setup_inputs(seed=0):
    import zlib

    import numpy as np

    out = dict(_drawn_inputs(seed))
    spreads = {'L0_attn_conv_b': (0.0, 0.1),
     'L0_attn_b_dt': (0.0, 0.337),
     'L0_attn_D': (1.0, 0.2),
     'L0_ffn_in_gamma': (1.0, 0.6),
     'L0_ffn_in_beta': (0.0, 0.8),
     'L0_ffn_agg_b': (0.0, 0.551),
     'L0_ffn_pn_gamma': (1.0, 0.6),
     'L0_ffn_pn_beta': (0.0, 0.8),
     'L0_ffn_d1_b': (0.0, 0.65),
     'L0_ffn_d2_b': (0.0, 0.1),
     'L0_ffn_bc_b': (0.0, 0.299),
     'L0_ffn_gate_b': (0.0, 0.8),
     'L0_ffn_out_gamma': (1.0, 0.2),
     'L0_ffn_out_beta': (0.0, 0.1),
     'L1_attn_conv_b': (0.0, 0.1),
     'L1_attn_dt_bias': (1.0, 0.6),
     'L1_attn_D': (1.0, 0.2),
     'L1_attn_norm_w': (1.0, 0.2),
     'L1_xattn_q_norm_w': (1.0, 0.6),
     'L1_xattn_k_norm_w': (1.0, 0.6)}
    factors = {'L0_ffn_gate_w': 5.893,
     'L1_attn_A_log': 8.0,
     'L1_xattn_Wq': 3.055,
     'L1_xattn_Wk': 3.076,
     'L1_ffn_router_weight': 6.553,
     'L1_ffn_gate_up_proj': 5.676,
     'L1_ffn_down_proj': 5.655,
     'L1_ffn_sh_gate_w': 3.876,
     'L1_ffn_sh_up_w': 3.834,
     'L1_ffn_sh_down_w': 3.831,
     'L1_ffn_shared_gate_w': 8.0}
    for name, (base, spread) in spreads.items():
        noise = np.random.default_rng([zlib.crc32(name.encode()), seed]).standard_normal(out[name].shape)
        drawn = base * np.exp(spread * noise) if base else spread * noise
        out[name] = jnp.asarray(drawn.astype(out[name].dtype))
    for name, factor in factors.items():
        out[name] = (out[name] * factor).astype(out[name].dtype)
    return out
```

```python
from contextlib import ExitStack

import numpy as np
import concourse.bass as bass
from concourse import mybir

F32 = mybir.dt.float32
F32R = mybir.dt.float32r
I32 = mybir.dt.int32
U32 = mybir.dt.uint32
ALU = mybir.AluOpType
ACT = mybir.ActivationFunctionType
AX = mybir.AxisListType

P = 128
BATCH, SEQ, DM = 4, 256, 256
TOK = BATCH * SEQ
NT = TOK // P
KC = DM // P
HALF = TOK // 2
LN_EPS = 1e-5

MI, MS, MR = 512, 16, 128
MC = MI // P
SH, SP, SN, SG, SK, CS = 64, 64, 128, 8, 4, 32
SI = SH * SP
QH, KVH, HD = 16, 4, 128
REP = QH // KVH
NE, IM, ISH = 8, 176, 704
FH = 1024
K_STEPS = 4
VOCAB, NEX = 12500, 4


class Link:

    def __init__(self, eng, sem):
        self.eng, self.sem, self.base, self.n = eng, sem, 0, 0

    def mark(self, ins):
        self.n = self.n + 1
        return ins.then_inc(self.sem, 1)

    def wait(self):
        self.eng.wait_ge(self.sem, self.base + self.n)

    def __call__(self, ins):
        self.mark(ins)
        self.wait()


def wait_beyond_start(eng, sem, n):
    if not (isinstance(n, int) and n == 0):
        eng.wait_ge(sem, n)


NEWTON = 3
RSQRT_LINKS = 3 + 3 * NEWTON


def pipeline(eng, count, turn, body, behind):
    for i in range(turn):
        body(i, i, lambda n, i=i: n <= i)
    with eng.Fori(1, count // turn) as r:
        for q in range(turn):
            body(turn * r + q, q, lambda n: True)
    for i in range(count, count + behind):
        body(i, i % turn, lambda n, i=i: i - n < count)


def rsqrt_seed(v, link, out, ve, bits):
    link(v.tensor_scalar(bits.bitcast(I32), ve.bitcast(I32), 1, None, ALU.logical_shift_right))
    link(v.tensor_scalar(out.bitcast(I32), bits.bitcast(I32), -1, 0x5F3759DF, ALU.mult, ALU.add))


def rsqrt_on_vector(v, link, out, var, tmp, eps):
    ve, bits, sq = tmp
    link(v.tensor_scalar(ve, var, eps, None, ALU.add))
    rsqrt_seed(v, link, out, ve, bits)
    for _ in range(NEWTON):
        link(v.tensor_tensor(sq, out, out, ALU.mult))
        link(v.scalar_tensor_tensor(out=bits, in0=sq, scalar=-0.5, in1=ve, op0=ALU.mult, op1=ALU.mult))
        link(v.scalar_tensor_tensor(out=out, in0=bits, scalar=1.5, in1=out, op0=ALU.add, op1=ALU.mult))


def split(v, link, hi, lo, x):
    link(v.tensor_copy(hi, x))
    link.mark(v.tensor_tensor(lo, x, hi, ALU.subtract))


def split_products(pe, out, w, x, start, stop):
    (w_hi, w_lo), (x_hi, x_lo) = w, x
    pe.matmul(out, w_hi, x_hi, start=start, stop=False)
    pe.matmul(out, w_hi, x_lo, start=False, stop=False)
    return pe.matmul(out, w_lo, x_hi, start=False, stop=stop)


class Shared:

    def __init__(self, nc, ctx, out):
        sb = lambda name, shape, dt=F32: ctx.enter_context(nc.sbuf_tensor(name, shape, dt))
        self.nc, self.ctx, self.out = nc, ctx, out
        self.x_tok = sb("x_tok", [P, NT, DM])
        self.x_feat = sb("x_feat", [P, KC, TOK])
        self.x_hi, self.x_lo = sb("x_hi", [P, KC, TOK], F32R), sb("x_lo", [P, KC, TOK], F32R)
        self.ctx_feat = sb("ctx_feat", [P, KC, BATCH, SEQ])
        self.ident = sb("ident", [P, P])
        self.ones = sb("ones", [P, P])
        self.stats = sb("stats", [P, NT, 6])
        self.mean_var = sb("mean_var", [P, NT, 2])
        self.rstd = sb("rstd", [P, NT])
        self.rs_tmp = sb("rs_tmp", [P, 3, 64])
        self.psum = ctx.enter_context(nc.psum_tensor("psum", [P, 8, 512], F32))

    def sem(self, name):
        return self.nc.alloc_semaphore(name=name)

    def tmp(self, n, parts=P):
        return [self.rs_tmp[0:parts, k, 0:n] for k in range(3)]


IN_PLACE = "the sum is already in x_tok"


class PostNorm:

    def __init__(self, sh, tag, last=False):
        self.sh, self.last = sh, last
        self.y_ready = sh.sem(f"{tag}_y_ready")
        self.link = sh.sem(f"{tag}_norm_link")
        self.normed = sh.sem(f"{tag}_normed")
        self.turned = sh.sem(f"{tag}_turned")
        self.x_feat_ready = sh.sem(f"{tag}_x_feat")

    def vector(self, v, add=None):
        sh = self.sh
        link = Link(v, self.link)
        for t in range(NT):
            v.wait_ge(self.y_ready, t + 1)
            x = sh.x_tok[:, t, :]
            if add is not IN_PLACE:
                link.mark(add(t) if add else v.tensor_tensor(x, x, sh.psum[:, t, 0:DM], ALU.add))
            if t:
                if add is not IN_PLACE:
                    v.wait_ge(self.link, link.n - 1)
                link.mark(v.bn_stats(sh.stats[:, t - 1, :], sh.x_tok[:, t - 1, :]))
        if add is not IN_PLACE:
            link.wait()
        link(v.bn_stats(sh.stats[:, NT - 1, :], sh.x_tok[:, NT - 1, :]))
        for t in range(NT):
            link.mark(v.bn_aggr(sh.mean_var[:, t, :], sh.stats[:, t, :]))
        link.wait()
        rsqrt_on_vector(v, link, sh.rstd[:, :], sh.mean_var[:, :, 1], sh.tmp(NT), LN_EPS)
        for t in range(NT):
            x = sh.x_tok[:, t, :]
            v.tensor_scalar(x, x, sh.mean_var[:, t, 0:1], sh.rstd[:, t:t + 1], ALU.subtract,
                            ALU.mult).then_inc(self.normed, 1)
        for t in range(0 if self.last else NT):
            part = (slice(None), slice(None), slice(t * P, (t + 1) * P))
            v.wait_ge(self.x_feat_ready, t + 1)
            split(v, link, sh.x_hi[part], sh.x_lo[part], sh.x_feat[part])

    def tensor(self, pe):
        sh = self.sh
        for t in range(NT):
            pe.wait_ge(self.normed, t + 1)
            for c in range(KC):
                mm = pe.transpose(sh.psum[:, t, DM + c * P:DM + (c + 1) * P],
                                  sh.x_tok[:, t, c * P:(c + 1) * P], sh.ident[:, :])
            mm.then_inc(self.turned, 1)

    def scalar(self, act):
        sh = self.sh
        for t in range(NT):
            act.wait_ge(self.turned, t + 1)
            act.activation(sh.x_feat[:, :, t * P:(t + 1) * P],
                           sh.psum[:, t, DM:2 * DM].rearrange("p (c n) -> p c n", c=KC),
                           ACT.Copy).then_inc(self.x_feat_ready, 1)


SM_COLS = dict(conv_w=MC * 3, conv_b=MC, b_dt=MC, a_log=MC * MS, d=MC)


def columns(table):
    at, out = 0, {}
    for name, n in table.items():
        out[name] = slice(at, at + n)
        at += n
    return out, at


def stage_mamba(nc, sh, io):
    with ExitStack() as ctx:
        def sb(name, shape, dt=F32):
            return ctx.enter_context(nc.sbuf_tensor(name, shape, dt))

        col, n_small = columns(SM_COLS)
        w_in = sb("m_w_in", [P, KC, 2 * MI])
        w_x = sb("m_w_x", [P, MC, MR + 2 * MS])
        w_dt = sb("m_w_dt", [P, MI])
        w_out = sb("m_w_out", [P, MC, DM])
        small = sb("m_small", [P, n_small])
        neg_a = sb("m_a", [P, MC, MS])
        diag_d = sb("m_diag_d", [P, MC, P])
        u = sb("m_u", [P, MC, TOK])
        gate = sb("m_gate", [P, MC, TOK])
        dt = sb("m_dt", [P, MC, TOK])
        dtu = sb("m_dtu", [P, MC, TOK])
        acc = sb("m_acc", [P, 2, 512])
        dt_in = dtu[:, 0, :]
        bc = sb("m_bc", [2 * MS, TOK])
        decay = sb("m_decay", [P, 2, MC, 2, SEQ])
        drive = sb("m_drive", [P, 2, MC, HALF])
        state = sb("m_state", [P, MC, HALF])
        read = sb("m_read", [P, 2, MC, HALF])
        b_all = sb("m_b_all", [P, 2, HALF])
        c_all = sb("m_c_all", [P, 2, HALF])
        bc_dram = nc.dram_tensor("m_bc_dram", [2 * MS, TOK], F32, kind="Internal").ap()

        s = sh.sem
        w_loaded, wx_loaded = s("m_w_loaded"), s("m_wx_loaded")
        const_made = s("m_const_made")
        proj_done, acc_made, conv_done, u_done, gate_done = (s("m_" + n) for n in (
            "proj_done", "acc_made", "conv_done", "u_done", "gate_done"))
        xdbl_done, dt_in_ready, bc_ready, bc_stored = (s("m_" + n) for n in (
            "xdbl_done", "dt_in_ready", "bc_ready", "bc_stored"))
        dtmm_done, sp_act, sp_abs, sp_log, dt_ready, dtu_ready = (s("m_" + n) for n in (
            "dtmm_done", "sp_act", "sp_abs", "sp_log", "dt_ready", "dtu_ready"))
        b_loaded = [s(f"m_b_loaded{slot}") for slot in range(2)]
        c_loaded = [s(f"m_c_loaded{slot}") for slot in range(2)]
        decay_ready, drive_ready, scan_done, read_ready, summed = (s("m_" + n) for n in (
            "decay_ready", "drive_ready", "scan_done", "read_ready", "summed"))
        y_gated, v_link, a_link = s("m_y_gated"), s("m_v_link"), s("m_a_link")
        norm = PostNorm(sh, "m")
        psum = sh.psum

        halves = [(m, h) for m in range(MC) for h in range(2)]
        block = ctx.enter_context(nc.Block())

        @block.sync
        def _(sp):
            sp.dma_start(sh.x_feat[:, :, :], io["x_feat"]).then_inc(w_loaded, 16)
            sp.dma_start(w_in[:, :, :], io["m_w_in"]).then_inc(w_loaded, 16)
            sp.dma_start(small[:, :], io["m_small"]).then_inc(w_loaded, 16)
            sp.dma_start(w_x[:, :, :], io["m_w_x"]).then_inc(wx_loaded, 16)
            sp.dma_start(w_dt[:, :], io["m_w_dt"]).then_inc(wx_loaded, 16)
            sp.dma_start(w_out[:, :, :], io["m_w_out"]).then_inc(wx_loaded, 16)
            sp.dma_start(sh.x_tok[:, :, :], io["x_tok"]).then_inc(wx_loaded, 16)
            sp.dma_start(sh.ctx_feat[:, :, :, :], io["ctx_feat"]).then_inc(wx_loaded, 16)
            sp.wait_ge(bc_ready, 2)
            sp.dma_start(bc_dram, bc[:, :]).then_inc(bc_stored, 16)
            sp.wait_ge(bc_stored, 16)
            for h in range(2):
                with sp.Fori(0, MS // 2) as r:
                    for slot in range(2):
                        n = h * MS + 2 * r + slot
                        sp.wait_ge(drive_ready, n + 1)
                        sp.dma_start(b_all[:, slot, :], bc_dram[bass.ds(2 * r + slot, 1), h * HALF:(h + 1) * HALF]
                                     .partition_broadcast(P).rearrange("p a n -> p (a n)")).then_inc(b_loaded[slot], 16)
                        sp.wait_ge(read_ready, n + 1)
                        sp.dma_start(c_all[:, slot, :], bc_dram[bass.ds(2 * r + (MS + slot), 1), h * HALF:(h + 1) * HALF]
                                     .partition_broadcast(P).rearrange("p a n -> p (a n)")).then_inc(c_loaded[slot], 16)

        @block.gpsimd
        def _(pool):
            pool.memset(sh.ones[:, :], 1.0).then_inc(const_made, 1)
            pool.memset(sh.ident[:, :], 0.0).then_inc(const_made, 1)
            pool.memset(decay[:, :, :, :, 0:1], 0.0).then_inc(const_made, 1)
            pool.wait_ge(const_made, 3)
            pool.affine_select(out=sh.ident[:, :], in_=sh.ident[:, :], compare_op=ALU.not_equal, fill=1.0,
                               base=0, pattern=[[-1, P]], channel_multiplier=1).then_inc(const_made, 1)
            pool.sem_inc(drive_ready, 2)
            for h in range(2):
                pool.wait_ge(dtu_ready, MC * (h + 1))
                with pool.Fori(0, MS // 2) as r:
                    for slot in range(2):
                        n = h * MS + 2 * r + slot
                        pool.wait_ge(b_loaded[slot], 16 * (h * (MS // 2) + r) + 16)
                        pool.wait_ge(scan_done, n + 1)
                        pool.tensor_tensor(drive[:, slot, :, :], dtu[:, :, h * HALF:(h + 1) * HALF],
                                           b_all[:, slot, :].unsqueeze(1).broadcast_to([P, MC, HALF]),
                                           ALU.mult).then_inc(drive_ready, 1)

        @block.tensor
        def _(pe):
            pe.wait_ge(w_loaded, 48)
            for j in range(4 * MC):
                m, h = j // 2, j % 2
                if j >= 4:
                    if j - 4 < 2 * MC:
                        pe.wait_ge(conv_done, j - 3)
                    else:
                        pe.wait_ge(gate_done, j - 3 - 2 * MC)
                for k in range(KC):
                    mm = pe.matmul(psum[:, j % 4, :], w_in[:, k, m * P:(m + 1) * P],
                                   sh.x_feat[:, k, h * HALF:(h + 1) * HALF], start=k == 0, stop=k == KC - 1)
                mm.then_inc(proj_done, 1)
            pe.wait_ge(wx_loaded, 80)
            pe.wait_ge(u_done, 2 * MC)
            for h in range(2):
                for rows, bank in ((slice(0, MR), 4 + h), (slice(MR, MR + 2 * MS), 6 + h)):
                    for k in range(MC):
                        mm = pe.matmul(psum[0:rows.stop - rows.start, bank, :], w_x[:, k, rows],
                                       u[:, k, h * HALF:(h + 1) * HALF], start=k == 0, stop=k == MC - 1)
                    mm.then_inc(xdbl_done, 1)
            pe.wait_ge(gate_done, 2 * MC)
            for h in range(2):
                for m in range(MC):
                    j = h * MC + m
                    pe.wait_ge(dt_in_ready, h + 1)
                    if j >= 4:
                        pe.wait_ge(sp_act, j - 3)
                    pe.matmul(psum[:, j % 4, :], w_dt[:, m * P:(m + 1) * P],
                              dt_in[:, h * HALF:(h + 1) * HALF], start=True, stop=True).then_inc(dtmm_done, 1)
            pe.wait_ge(const_made, 4 + MC)
            pe.wait_ge(sp_act, 2 * MC)
            for h in range(2):
                for m in range(MC):
                    pe.matmul(psum[:, 4 * h + m, :], diag_d[:, m, :], u[:, m, h * HALF:(h + 1) * HALF],
                              start=True, stop=False, skip_group_check=True)
                with pe.Fori(0, MS // 2) as r:
                    for slot in range(2):
                        n = h * MS + 2 * r + slot
                        pe.wait_ge(read_ready, n + 3)
                        for m in range(MC):
                            mm = pe.matmul(psum[:, 4 * h + m, :], sh.ident[:, :], read[:, slot, m, :],
                                           start=False, stop=False, skip_group_check=True)
                        mm.then_inc(summed, 1)
            for t in range(NT):
                pe.wait_ge(y_gated, 4 * (t // 4 + 1))
                if t == 0:
                    pe.wait_ge(y_gated, 4)
                for k in range(MC):
                    mm = pe.matmul(psum[:, t, 0:DM], gate[:, k, t * P:(t + 1) * P], w_out[:, k, :],
                                   start=k == 0, stop=k == MC - 1)
                mm.then_inc(norm.y_ready, 1)
            norm.tensor(pe)

        @block.scalar
        def _(act):
            act.wait_ge(w_loaded, 48)
            link = Link(act, a_link)

            def silu_u(j):
                m, h = j // 2, j % 2
                act.wait_ge(conv_done, j + 1)
                act.activation(u[:, m, h * HALF:(h + 1) * HALF], acc[:, j % 2, :], ACT.Silu).then_inc(u_done, 1)

            for j, (m, h) in enumerate(halves):
                act.wait_ge(proj_done, j + 1)
                if j >= 2:
                    act.wait_ge(u_done, j - 1)
                act.activation(acc[:, j % 2, :], psum[:, j % 4, :], ACT.Identity, bias=small[:, col["conv_b"]][:, m:m + 1],
                               scale=small[:, col["conv_w"]][:, 3 * m + 1:3 * m + 2]).then_inc(acc_made, 1)
                if j:
                    silu_u(j - 1)
            silu_u(2 * MC - 1)
            for j, (m, h) in enumerate(halves):
                act.wait_ge(proj_done, 2 * MC + j + 1)
                act.activation(gate[:, m, h * HALF:(h + 1) * HALF], psum[:, j % 4, :], ACT.Silu).then_inc(gate_done, 1)
            link(act.activation(neg_a[:, :, :].rearrange("p a b -> p (a b)"), small[:, col["a_log"]], ACT.Exp))
            link(act.mul(neg_a[:, :, :].rearrange("p a b -> p (a b)"), neg_a[:, :, :].rearrange("p a b -> p (a b)"), -1.0))
            for h in range(2):
                for m in range(MC):
                    j = h * MC + m
                    act.wait_ge(dtmm_done, j + 1)
                    act.activation(dt[:, m, h * HALF:(h + 1) * HALF], psum[:, j % 4, :], ACT.Identity,
                                   bias=small[:, col["b_dt"]][:, m:m + 1]).then_inc(sp_act, 1)
            for j, (h, m) in enumerate((h, m) for h in range(2) for m in range(MC)):
                act.wait_ge(sp_act, j + 1)
                if j >= 2:
                    act.wait_ge(dt_ready, j - 1)
                link(act.activation(acc[:, j % 2, :], dt[:, m, h * HALF:(h + 1) * HALF], ACT.Abs))
                link(act.activation(acc[:, j % 2, :], acc[:, j % 2, :], ACT.Exp, scale=-1.0))
                act.activation(acc[:, j % 2, :], acc[:, j % 2, :], ACT.Ln, bias=1.0).then_inc(sp_log, 1)
            for h in range(2):
                act.wait_ge(dt_ready, MC * (h + 1))
                with act.Fori(0, MS // 2) as r:
                    for slot in range(2):
                        n = h * MS + 2 * r + slot
                        act.wait_ge(scan_done, n + 1)
                        for m in range(MC):
                            a = act.activation(decay[:, slot, m, :, 1:SEQ],
                                               dt[:, m, h * HALF:(h + 1) * HALF].rearrange("p (b s) -> p b s", b=2)[:, :, 1:SEQ],
                                               ACT.Exp, scale=neg_a[:, m, bass.ds(2 * r + slot, 1)])
                        a.then_inc(decay_ready, 1)
            norm.scalar(act)

        @block.vector
        def _(v):
            link = Link(v, v_link)
            v.sem_inc(summed, 2)
            v.sem_inc(scan_done, 2)
            v.sem_inc(read_ready, 2)
            v.wait_ge(w_loaded, 48)
            for j, (m, h) in enumerate(halves):
                v.wait_ge(acc_made, j + 1)
                a = acc[:, j % 2, :].rearrange("p (b s) -> p b s", b=2)
                x = psum[:, j % 4, :].rearrange("p (b s) -> p b s", b=2)
                w = small[:, col["conv_w"]]
                link(v.scalar_tensor_tensor(out=a[:, :, 1:SEQ], in0=x[:, :, 0:SEQ - 1], scalar=w[:, 3 * m:3 * m + 1],
                                            in1=a[:, :, 1:SEQ], op0=ALU.mult, op1=ALU.add))
                v.scalar_tensor_tensor(out=a[:, :, 0:SEQ - 1], in0=x[:, :, 1:SEQ], scalar=w[:, 3 * m + 2:3 * m + 3],
                                       in1=a[:, :, 0:SEQ - 1], op0=ALU.mult, op1=ALU.add).then_inc(conv_done, 1)
            v.wait_ge(const_made, 4)
            for m in range(MC):
                v.tensor_scalar(diag_d[:, m, :], sh.ident[:, :], small[:, col["d"]][:, m:m + 1], None,
                                ALU.mult).then_inc(const_made, 1)
            for h in range(2):
                v.wait_ge(xdbl_done, 2 * h + 2)
                v.tensor_copy(dt_in[:, h * HALF:(h + 1) * HALF], psum[:, 4 + h, :]).then_inc(dt_in_ready, 1)
                v.tensor_copy(bc[:, h * HALF:(h + 1) * HALF], psum[0:2 * MS, 6 + h, :]).then_inc(bc_ready, 1)
            for j, (h, m) in enumerate((h, m) for h in range(2) for m in range(MC)):
                v.wait_ge(sp_log, j + 1)
                d = dt[:, m, h * HALF:(h + 1) * HALF]
                v.scalar_tensor_tensor(out=d, in0=d, scalar=0.0, in1=acc[:, j % 2, :], op0=ALU.max,
                                       op1=ALU.add).then_inc(dt_ready, 1)
                v.wait_ge(dt_ready, j + 1)
                v.wait_ge(dtmm_done, 2 * MC)
                v.tensor_tensor(dtu[:, m, h * HALF:(h + 1) * HALF], d, u[:, m, h * HALF:(h + 1) * HALF],
                                ALU.mult).then_inc(dtu_ready, 1)
            flat = lambda ap: ap.rearrange("p m n -> p (m n)")
            for h in range(2):
                with v.Fori(0, MS // 2) as r:
                    for slot in range(2):
                        n = h * MS + 2 * r + slot
                        v.wait_ge(decay_ready, n + 1)
                        v.wait_ge(drive_ready, n + 3)
                        v.wait_ge(read_ready, n + 2)
                        v.tensor_tensor_scan(flat(state[:, :, :]), decay[:, slot, :, :, :].rearrange("p m b s -> p (m b s)"),
                                             flat(drive[:, slot, :, :]), 0.0, ALU.mult, ALU.add).then_inc(scan_done, 1)
                        v.wait_ge(scan_done, n + 3)
                        v.wait_ge(c_loaded[slot], 16 * (h * (MS // 2) + r) + 16)
                        v.wait_ge(summed, n + 1)
                        v.tensor_tensor(read[:, slot, :, :], state[:, :, :],
                                        c_all[:, slot, :].unsqueeze(1).broadcast_to([P, MC, HALF]),
                                        ALU.mult).then_inc(read_ready, 1)
                v.wait_ge(summed, 2 + MS * (h + 1))
                for m in range(MC):
                    g = gate[:, m, h * HALF:(h + 1) * HALF]
                    v.tensor_tensor(g, g, psum[:, 4 * h + m, :], ALU.mult).then_inc(y_gated, 1)
            norm.vector(v)


def stage_token_experts(nc, sh, io):
    PER_EXPERT = VOCAB // NEX
    FC = SEQ // P
    with ExitStack() as ctx:
        def sb(name, shape, dt=F32):
            return ctx.enter_context(nc.sbuf_tensor(name, shape, dt))

        ids = sb("e_ids", [P, TOK], I32)
        at_least = sb("e_at_least", [P, NEX - 1, TOK])
        mask = sb("e_mask", [P, NEX, TOK])
        x_own = sb("e_x_own", [P, 2, KC, TOK])
        silu = sb("e_silu", [P, 2, HALF])
        hid = sb("e_hid", [P, NEX * FC, TOK])
        s = sh.sem
        ids_loaded, mask_ready, own_ready, v_link = s("e_ids_loaded"), s("e_mask_ready"), s("e_own_ready"), s("e_v_link")
        pre_done, silu_done, hid_done = s("e_pre_done"), s("e_silu_done"), s("e_hid_done")
        norm = PostNorm(sh, "e")
        psum, ctxw = sh.psum, sh.ctx_feat
        steps = [(e, f, h) for e in range(NEX) for f in range(FC) for h in range(2)]
        block = ctx.enter_context(nc.Block())

        @block.sync
        def _(sp):
            sp.dma_start(ids[:, :], io["token_ids"].partition_broadcast(P).rearrange("p a n -> p (a n)")).then_inc(ids_loaded, 16)

        @block.gpsimd
        def _(pool):
            for e in range(NEX):
                pool.wait_ge(mask_ready, e + 1)
                if e >= 2:
                    pool.wait_ge(pre_done, 2 * FC * (e - 1))
                pool.tensor_tensor(x_own[:, e % 2, :, :], sh.x_feat[:, :, :],
                                   mask[:, e, :].unsqueeze(1).broadcast_to([P, KC, TOK]), ALU.mult).then_inc(own_ready, 1)

        @block.tensor
        def _(pe):
            for j, (e, f, h) in enumerate(steps):
                pe.wait_ge(own_ready, e + 1)
                if j >= 4:
                    pe.wait_ge(hid_done, j - 3)
                for k in range(KC):
                    mm = pe.matmul(psum[:, j % 4, :], ctxw[:, k, e, f * P:(f + 1) * P],
                                   x_own[:, e % 2, k, h * HALF:(h + 1) * HALF], start=k == 0, stop=k == KC - 1)
                mm.then_inc(pre_done, 1)
            pe.wait_ge(hid_done, len(steps))
            for t in range(NT):
                for j in range(NEX * FC):
                    mm = pe.matmul(psum[:, t, 0:DM], hid[:, j, t * P:(t + 1) * P], ctxw[:, j % FC, j // FC, :],
                                   start=j == 0, stop=j == NEX * FC - 1)
                mm.then_inc(norm.y_ready, 1)
            norm.tensor(pe)

        @block.scalar
        def _(act):
            for j in range(len(steps)):
                act.wait_ge(pre_done, j + 1)
                if j >= 2:
                    act.wait_ge(hid_done, j - 1)
                act.activation(silu[:, j % 2, :], psum[:, j % 4, :], ACT.Silu).then_inc(silu_done, 1)
            norm.scalar(act)

        @block.vector
        def _(v):
            link = Link(v, v_link)
            v.wait_ge(ids_loaded, 16)
            v.tensor_scalar(mask[:, 0, :], ids[:, :], float(PER_EXPERT), None, ALU.is_lt).then_inc(mask_ready, 1)
            for e in range(1, NEX):
                link.mark(v.tensor_scalar(at_least[:, e - 1, :], ids[:, :], float(PER_EXPERT * e), None, ALU.is_ge))
            link.wait()
            for e in range(1, NEX - 1):
                v.tensor_tensor(mask[:, e, :], at_least[:, e - 1, :], at_least[:, e, :], ALU.subtract).then_inc(mask_ready, 1)
            v.tensor_copy(mask[:, NEX - 1, :], at_least[:, NEX - 2, :]).then_inc(mask_ready, 1)
            for j, (e, f, h) in enumerate(steps):
                v.wait_ge(silu_done, j + 1)
                v.tensor_tensor(hid[:, e * FC + f, h * HALF:(h + 1) * HALF], silu[:, j % 2, :], psum[:, j % 4, :],
                                ALU.mult).then_inc(hid_done, 1)
            norm.vector(v)


FF_COLS = dict(in_g=KC, in_b=KC, pn_g=KC, pn_b=KC, agg_b=KC, d1_b=FH // P, d2_b=KC, bc_b=KC, gate_b=KC)


def stage_thought(nc, sh, io):
    HC = FH // P
    with ExitStack() as ctx:
        def sb(name, shape, dt=F32):
            return ctx.enter_context(nc.sbuf_tensor(name, shape, dt))

        col, n_small = columns(FF_COLS)
        small = sb("f_small", [P, n_small])
        agg_w, bc_w, gate_w = (sb("f_" + n, [P, KC, DM]) for n in ("agg_w", "bc_w", "gate_w"))
        d1_w, d2_w = sb("f_d1_w", [P, KC, FH]), sb("f_d2_w", [P, HC, DM])
        out_g, out_b = sb("f_out_g", [P, DM]), sb("f_out_b", [P, DM])
        gate = sb("f_gate", [P, KC, TOK])
        mixed = sb("f_mixed", [P, KC, TOK])
        on_tok = sb("f_on_tok", [P, NT, DM])
        thought = sb("f_thought", [P, KC, BATCH])
        cen, sq, nrm = (sb("f_" + n, [P, KC, BATCH]) for n in ("cen", "sq", "nrm"))
        rs = sb("f_rs", [P, BATCH])
        var = sb("f_var", [P, BATCH])
        pre, hid = sb("f_pre", [P, HC, BATCH]), sb("f_hid", [P, HC, BATCH])
        bcast = sb("f_bcast", [P, KC, BATCH])
        s = sh.sem
        loaded, v_link, v_done, pe_done, act_done = (s("f_" + n) for n in ("loaded", "v_link", "v_done", "pe_done", "act_done"))
        gate_mm, gate_ready, mixed_ready, tok_ready, beta_added = (s("f_" + n) for n in (
            "gate_mm", "gate_ready", "mixed_ready", "tok_ready", "beta_added"))
        norm = PostNorm(sh, "f")
        psum = sh.psum
        names = ["f_small", "f_agg_w", "f_d1_w", "f_d2_w", "f_bc_w", "f_gate_w"]
        tiles = [small[:, :], agg_w[:, :, :], d1_w[:, :, :], d2_w[:, :, :], bc_w[:, :, :], gate_w[:, :, :]]
        last = sh.x_feat[:, :, SEQ - 1:TOK:SEQ]
        block = ctx.enter_context(nc.Block())

        @block.sync
        def _(sp):
            for n, tile in zip(names, tiles):
                sp.dma_start(tile, io[n]).then_inc(loaded, 16)
            for n, tile in (("f_out_g", out_g), ("f_out_b", out_b)):
                sp.dma_start(tile[:, :], io[n].partition_broadcast(P).rearrange("p a n -> p (a n)")).then_inc(loaded, 16)

        ALL = 16 * (len(names) + 2)

        @block.gpsimd
        def _(pool):
            pool.wait_ge(loaded, ALL)
            for t in range(NT):
                pool.tensor_tensor(sh.x_tok[:, t, :], sh.x_tok[:, t, :], out_b[:, :], ALU.add).then_inc(beta_added, 1)

        @block.tensor
        def _(pe):
            pe.wait_ge(loaded, ALL)
            count = [0]

            def after_vector():
                count[0] += 1
                pe.wait_ge(v_done, count[0])

            def sums(src):
                for c in range(KC):
                    mm = pe.matmul(psum[:, 0, 0:BATCH], sh.ones[:, :], src[:, c, :], start=c == 0, stop=c == KC - 1)
                mm.then_inc(pe_done, 1)

            def product(bank, w, src, n_out, n_in):
                for m in range(n_out):
                    for k in range(n_in):
                        mm = pe.matmul(psum[:, bank, m * BATCH:(m + 1) * BATCH], w[:, k, m * P:(m + 1) * P], src[:, k, :],
                                       start=k == 0, stop=k == n_in - 1)
                mm.then_inc(pe_done, 1)

            sums(last)
            after_vector()
            sums(sq)
            after_vector()
            product(1, agg_w, nrm, KC, KC)
            for m in range(KC):
                for h in range(2):
                    for k in range(KC):
                        mm = pe.matmul(psum[:, 4 + 2 * m + h, :], gate_w[:, k, m * P:(m + 1) * P],
                                       sh.x_feat[:, k, h * HALF:(h + 1) * HALF], start=k == 0, stop=k == KC - 1)
                    mm.then_inc(gate_mm, 1)
            for i in range(K_STEPS):
                after_vector()
                sums(thought)
                after_vector()
                sums(sq)
                after_vector()
                product(1, d1_w, nrm, HC, KC)
                count[0] += 1
                pe.wait_ge(act_done, i + 1)
                product(2, d2_w, hid, KC, HC)
            after_vector()
            product(1, bc_w, thought, KC, KC)
            pe.wait_ge(gate_ready, 4)
            for t in range(NT):
                pe.wait_ge(mixed_ready, 2 * (t // 2) + 2)
                for c in range(KC):
                    mm = pe.transpose(psum[:, t, c * P:(c + 1) * P], mixed[:, c, t * P:(t + 1) * P], sh.ident[:, :])
                mm.then_inc(tok_ready, 1)
            norm.tensor(pe)

        @block.scalar
        def _(act):
            act.wait_ge(loaded, ALL)
            for m in range(KC):
                for h in range(2):
                    act.wait_ge(gate_mm, 2 * m + h + 1)
                    act.activation(gate[:, m, h * HALF:(h + 1) * HALF], psum[:, 4 + 2 * m + h, :], ACT.Sigmoid,
                                   bias=small[:, col["gate_b"]][:, m:m + 1]).then_inc(gate_ready, 1)
            for i in range(K_STEPS):
                act.wait_ge(v_done, 2 + 4 * (i + 1))
                act.activation(hid[:, :, :], pre[:, :, :], ACT.Gelu).then_inc(act_done, 1)
            norm.scalar(act)

        @block.vector
        def _(v):
            link = Link(v, v_link)
            count = [0]
            bc4 = lambda name, n: small[:, col[name]].unsqueeze(2).broadcast_to([P, n, BATCH])
            bank = lambda b, n: psum[:, b, 0:n * BATCH].rearrange("p (c b) -> p c b", c=n)

            def after_tensor():
                count[0] += 1
                v.wait_ge(pe_done, count[0])

            def norm_columns(src, gamma, beta, eps):
                after_tensor()
                link(v.scalar_tensor_tensor(out=cen[:, :, :], in0=psum[:, 0, 0:BATCH].unsqueeze(1).broadcast_to([P, KC, BATCH]),
                                            scalar=-1.0 / DM, in1=src, op0=ALU.mult, op1=ALU.add))
                v.tensor_tensor(sq[:, :, :], cen[:, :, :], cen[:, :, :], ALU.mult).then_inc(v_done, 1)
                after_tensor()
                link(v.tensor_scalar(var[:, :], psum[:, 0, 0:BATCH], 1.0 / DM, None, ALU.mult))
                rsqrt_on_vector(v, link, rs[:, :], var[:, :], sh.tmp(BATCH), eps)
                link(v.tensor_tensor(nrm[:, :, :], cen[:, :, :], rs[:, :].unsqueeze(1).broadcast_to([P, KC, BATCH]), ALU.mult))
                link(v.tensor_tensor(nrm[:, :, :], nrm[:, :, :], bc4(gamma, KC), ALU.mult))
                v.tensor_tensor(nrm[:, :, :], nrm[:, :, :], bc4(beta, KC), ALU.add).then_inc(v_done, 1)

            v.wait_ge(loaded, ALL)
            norm_columns(last, "in_g", "in_b", 1e-6)
            after_tensor()
            v.tensor_tensor(thought[:, :, :], bank(1, KC), bc4("agg_b", KC), ALU.add).then_inc(v_done, 1)
            for i in range(K_STEPS):
                v.wait_ge(v_done, 4 * i + 3)
                norm_columns(thought[:, :, :], "pn_g", "pn_b", 1e-6)
                after_tensor()
                v.tensor_tensor(pre[:, :, :], bank(1, HC), bc4("d1_b", HC), ALU.add).then_inc(v_done, 1)
                after_tensor()
                link(v.tensor_tensor(thought[:, :, :], thought[:, :, :], bc4("d2_b", KC), ALU.add))
                v.tensor_tensor(thought[:, :, :], thought[:, :, :], bank(2, KC), ALU.add).then_inc(v_done, 1)
            after_tensor()
            link(v.tensor_tensor(bcast[:, :, :], bank(1, KC), bc4("bc_b", KC), ALU.add))
            v.wait_ge(gate_ready, 4)
            for b in range(BATCH):
                for c in range(KC):
                    sl = slice(b * SEQ, (b + 1) * SEQ)
                    v.scalar_tensor_tensor(out=mixed[:, c, sl], in0=gate[:, c, sl], scalar=bcast[:, c, b:b + 1],
                                           in1=sh.x_feat[:, c, sl], op0=ALU.mult, op1=ALU.add).then_inc(mixed_ready, 1)
            for t in range(NT):
                v.wait_ge(tok_ready, t + 1)
                link.mark(v.bn_stats(sh.stats[:, t, :], psum[:, t, 0:DM]))
            link.wait()
            for t in range(NT):
                link.mark(v.bn_aggr(sh.mean_var[:, t, :], sh.stats[:, t, :]))
            link.wait()
            rsqrt_on_vector(v, link, sh.rstd[:, :], sh.mean_var[:, :, 1], sh.tmp(NT), 1e-6)
            for t in range(NT):
                link.mark(v.tensor_scalar(on_tok[:, t, :], psum[:, t, 0:DM], sh.mean_var[:, t, 0:1], sh.rstd[:, t:t + 1],
                                          ALU.subtract, ALU.mult))
            link.wait()
            for t in range(NT):
                v.tensor_tensor(on_tok[:, t, :], on_tok[:, t, :], out_g[:, :], ALU.mult).then_inc(norm.y_ready, 1)
            v.wait_ge(beta_added, NT)
            norm.vector(v, add=lambda t: v.tensor_tensor(sh.x_tok[:, t, :], sh.x_tok[:, t, :], on_tok[:, t, :], ALU.add))


NB = 2 * SG
NF = SI // P
HPT = P // SP
UN = 4
QUAD = P // CS
NEVER = -1e30


def conv_taps(v, link, acc, x, w, last):
    a = acc.rearrange("p (b s) -> p b s", b=BATCH)
    x = x.rearrange("p (b s) -> p b s", b=BATCH)
    for back in range(1, SK):
        ins = v.scalar_tensor_tensor(out=a[:, :, back:SEQ], in0=x[:, :, 0:SEQ - back], scalar=w[:, SK - 1 - back:SK - back],
                                     in1=a[:, :, back:SEQ], op0=ALU.mult, op1=ALU.add)
        if back < SK - 1:
            link(ins)
        else:
            ins.then_inc(last, 1)


def stage_ssd(nc, sh, io):
    with ExitStack() as ctx:
        def sb(name, shape, dt=F32):
            return ctx.enter_context(nc.sbuf_tensor(name, shape, dt))

        k = type("Kept", (), {})()
        k.conv = sb("s_conv", [P, NF + NB, SK + 1])
        k.norm_w = sb("s_norm_w", [P, NF])
        k.acum, k.to_last, k.dt = (sb("s_" + n, [P, NT, SH]) for n in ("acum", "to_last", "dt"))
        k.score = sb("s_score", [P, SG, NT, CS])
        k.eye_c = sb("s_eye_c", [P, CS])
        k.never_c = sb("s_never_c", [P, CS])
        k.same_chunk = sb("s_same_chunk", [P, P])
        k.d_eye = sb("s_d_eye", [P, SH, CS])
        ssd_prepare(nc, sh, io, k)
        ssd_heads(nc, sh, io, k)


def ssd_prepare(nc, sh, io, k):
    with ExitStack() as ctx:
        def sb(name, shape, dt=F32):
            return ctx.enter_context(nc.sbuf_tensor(name, shape, dt))

        w_dt = sb("s_w_dt", [P, KC, SH])
        head = sb("s_head", [SH, 2])
        d_all = sb("s_d_all", [P, SH])
        neg_a = sb("s_neg_a", [SH, 1])
        w_bc = sb("s_w_bc", [P, UN, KC, P])
        bc = sb("s_bc", [P, NB, TOK])
        acc = sb("s_acc", [P, 2, TOK])
        dt_f, a_f, cum_f, last_f, keep = (sb("s_" + n, [SH, TOK]) for n in ("dt_f", "a_f", "cum_f", "last_f", "keep"))
        eye, tri = sb("s_eye", [P, P]), sb("s_tri", [P, P])
        s = sh.sem
        loaded, const, v_link, a_link = s("s_loaded"), s("s_const"), s("s_v_link"), s("s_a_link")
        w_loaded = [s(f"s_wbc_loaded{q}") for q in range(UN)]
        dt_mm, dt_act, dt_f_ready, turned_in, turned, copied = (s("s_" + n) for n in (
            "dt_mm", "dt_act", "dt_f_ready", "turned_in", "turned", "copied"))
        proj, tap0, conv, act_done = (s("s_" + n) for n in ("proj", "tap0", "conv", "act_done"))
        score_mm, score_read = s("s_score_mm"), s("s_score_read")
        psum = sh.psum
        pair = lambda n: psum[:, 2 * n:2 * n + 2, :].rearrange("p a b -> p (a b)")
        block = ctx.enter_context(nc.Block())

        @block.sync
        def _(sp):
            sp.dma_start(w_dt[:, :, :], io["s_w_dt"]).then_inc(loaded, 16)
            sp.dma_start(head[:, :], io["s_head"]).then_inc(loaded, 16)
            sp.dma_start(k.conv[:, :, :], io["s_conv"]).then_inc(loaded, 16)
            sp.dma_start(k.norm_w[:, :], io["s_norm_w"]).then_inc(loaded, 16)
            sp.dma_start(d_all[:, :], io["s_d"].partition_broadcast(P).rearrange("p a n -> p (a n)")).then_inc(loaded, 16)
            with sp.Fori(0, NB // UN) as r:
                for q in range(UN):
                    sp.wait_ge(proj, UN * r + q + 1)
                    sp.dma_start(w_bc[:, q, :, :], io["s_w_bc"][bass.ds(UN * r + q, 1), :, :, :]
                                 .rearrange("a p c n -> p (a c) n")).then_inc(w_loaded[q], 16)

        @block.gpsimd
        def _(pool):
            pool.memset(k.same_chunk[:, :], 1.0).then_inc(const, 1)
            pool.memset(tri[:, :], 0.0).then_inc(const, 1)
            pool.memset(keep[:, :], 1.0).then_inc(const, 1)
            pool.wait_ge(const, 3)
            pool.memset(keep[:, 0:TOK:CS], 0.0).then_inc(const, 1)
            pool.affine_select(out=tri[:, :], in_=tri[:, :], compare_op=ALU.is_ge, fill=NEVER, base=0,
                               pattern=[[1, P]], channel_multiplier=-1).then_inc(const, 1)
            same = k.same_chunk[:, :].rearrange("p (c n) -> p c n", c=QUAD)
            pool.affine_select(out=same, in_=same, compare_op=ALU.is_ge, fill=0.0, base=0,
                               pattern=[[-CS, QUAD], [0, CS]], channel_multiplier=1).then_inc(const, 1)
            pool.wait_ge(const, 6)
            pool.affine_select(out=same, in_=same, compare_op=ALU.is_ge, fill=0.0, base=CS - 1,
                               pattern=[[CS, QUAD], [0, CS]], channel_multiplier=-1).then_inc(const, 1)

        @block.tensor
        def _(pe):
            pe.sem_inc(proj, UN)
            pe.wait_ge(loaded, 80)
            for h in range(2):
                for c in range(KC):
                    mm = pe.matmul(psum[0:SH, h, :], w_dt[:, c, :], sh.x_feat[:, c, h * HALF:(h + 1) * HALF],
                                   start=c == 0, stop=c == KC - 1)
                mm.then_inc(dt_mm, 1)
            with pe.Fori(0, NB // UN) as r:
                for q in range(UN):
                    i = UN * r + q
                    pe.wait_ge(w_loaded[q], 16 * r + 16)
                    pe.wait_ge(conv, i + 1)
                    for h in range(2):
                        for c in range(KC):
                            mm = pe.matmul(psum[:, 4 + 2 * (q % 2) + h, :], w_bc[:, q, c, :],
                                           sh.x_feat[:, c, h * HALF:(h + 1) * HALF], start=c == 0, stop=c == KC - 1)
                    mm.then_inc(proj, 1)
            for n, src in enumerate((cum_f, last_f, dt_f)):
                pe.wait_ge(turned_in, n + 1)
                pe.wait_ge(dt_act, 2)
                for t in range(NT):
                    mm = pe.transpose(psum[:, n, t * SH:(t + 1) * SH], src[:, t * P:(t + 1) * P], sh.ident[0:SH, 0:SH])
                mm.then_inc(turned, 1)
            pe.wait_ge(act_done, NB + 2)
            for g in range(SG):
                pe.wait_ge(copied, 3)
                if g >= 4:
                    pe.wait_ge(score_read, g - 3)
                for t in range(NT):
                    tok = slice(t * P, (t + 1) * P)
                    mm = pe.matmul(pair(g % 4)[:, tok], bc[:, g, tok], bc[:, SG + g, tok], start=True, stop=True)
                mm.then_inc(score_mm, 1)

        @block.scalar
        def _(act):
            link = Link(act, a_link)
            act.sem_inc(act_done, 2)
            act.wait_ge(loaded, 80)
            for h in range(2):
                act.wait_ge(dt_mm, h + 1)
                act.activation(dt_f[:, h * HALF:(h + 1) * HALF], psum[0:SH, h, :], ACT.Identity,
                               bias=head[:, 0:1]).then_inc(dt_act, 1)
            act.wait_ge(dt_act, 2)
            link(act.activation(neg_a[:, :], head[:, 1:2], ACT.Exp))
            link(act.activation(a_f[:, :], dt_f[:, :], ACT.Abs))
            link(act.activation(a_f[:, :], a_f[:, :], ACT.Exp, scale=-1.0))
            link(act.activation(a_f[:, :], a_f[:, :], ACT.Ln, bias=1.0))

            def step(i, q, exists):
                if exists(0):
                    act.wait_ge(proj, i + 1 + UN)
                    act.wait_ge(act_done, i + 1)
                    w = k.conv[:, bass.ds(i + NF, 1), :].rearrange("p a n -> p (a n)")
                    act.activation(acc[:, q % 2, :], pair(2 + q % 2), ACT.Identity, bias=w[:, SK:SK + 1],
                                   scale=w[:, SK - 1:SK]).then_inc(tap0, 1)
                if exists(1):
                    act.wait_ge(conv, i + 2)
                    act.activation(bc[:, bass.ds(i - 1, 1), :].rearrange("p a n -> p (a n)"), acc[:, (q - 1) % 2, :],
                                   ACT.Silu).then_inc(act_done, 1)
            pipeline(act, NB, UN, step, 1)

        @block.vector
        def _(v):
            link = Link(v, v_link)
            v.sem_inc(conv, 2)
            v.wait_ge(const, 7)
            for c in range(QUAD):
                own = slice(c * CS, (c + 1) * CS)
                link.mark(v.tensor_copy(k.eye_c[own, :], sh.ident[own, own]))
                link.mark(v.tensor_copy(k.never_c[own, :], tri[own, own]))
            link.wait()
            v.wait_ge(loaded, 80)
            link(v.tensor_tensor(k.d_eye[:, :, :], d_all[:, :].unsqueeze(2).broadcast_to([P, SH, CS]),
                                 k.eye_c[:, :].unsqueeze(1).broadcast_to([P, SH, CS]), ALU.mult))
            v.wait_ge(a_link, 4)
            link(v.scalar_tensor_tensor(out=dt_f[:, :], in0=dt_f[:, :], scalar=0.0, in1=a_f[:, :], op0=ALU.max, op1=ALU.add))
            link(v.tensor_scalar(a_f[:, :], dt_f[:, :], neg_a[:, 0:1], -1.0, ALU.mult, ALU.mult))
            link(v.tensor_tensor_scan(cum_f[:, :], keep[:, :], a_f[:, :], 0.0, ALU.mult, ALU.add))
            v.sem_inc(turned_in, 1)
            chunks = lambda ap: ap.rearrange("p (c n) -> p c n", n=CS)
            v.tensor_tensor(chunks(last_f[:, :]), cum_f[:, CS - 1:TOK:CS].unsqueeze(2).broadcast_to([SH, TOK // CS, CS]),
                            chunks(cum_f[:, :]), ALU.subtract).then_inc(turned_in, 2)
            before = link.n
            with v.Fori(0, NB // UN) as r:
                for q in range(UN):
                    i = UN * r + q
                    v.wait_ge(tap0, i + 1)
                    w = k.conv[:, bass.ds(i + NF, 1), :].rearrange("p a n -> p (a n)")
                    link.n = before + 2 * i
                    conv_taps(v, link, acc[:, q % 2, :], pair(2 + q % 2), w, conv)
            link.n = before + 2 * NB
            for n, dst in enumerate((k.acum, k.to_last, k.dt)):
                v.wait_ge(turned, n + 1)
                v.tensor_copy(dst[:, :, :].rearrange("p t h -> p (t h)"), psum[:, n, :]).then_inc(copied, 1)
            for g in range(SG):
                v.wait_ge(score_mm, g + 1)
                for c in range(QUAD):
                    own = slice(c * CS, (c + 1) * CS)
                    ins = v.tensor_copy(k.score[own, g, :, :], pair(g % 4)[own, :].rearrange("p (t n) -> p t n", t=NT)[:, :, own])
                ins.then_inc(score_read, 1)


def ssd_heads(nc, sh, io, k):
    with ExitStack() as ctx:
        def sb(name, shape, dt=F32):
            return ctx.enter_context(nc.sbuf_tensor(name, shape, dt))

        w_in = sb("h_w_in", [P, UN, 2 * KC * P])
        w_hi, w_lo = (sb("h_w_" + n, [P, 2, 2, KC, P], F32R) for n in ("hi", "lo"))
        w_out = sb("h_w_out", [P, UN, DM])
        raw, acc = sb("h_raw", [P, 2, TOK]), sb("h_acc", [P, 2, TOK])
        hid = sb("h_hid", [P, 2, NT, P])
        gate = sb("h_gate", [P, UN, TOK])
        yg = sb("h_yg", [P, 2, TOK])
        sq = sb("h_sq", [P, 2, TOK])
        sq_sum = sb("h_sq_sum", [P, TOK])
        mat = sb("h_mat", [P, 2, NT * HPT, P])
        CW = [P, 2, NT, HPT, CS]
        spread, seg, seg_l, seg_m, score_dt = (sb("h_" + n, CW) for n in ("spread", "seg", "seg_l", "seg_m", "score_dt"))
        ssum, rs = sb("h_ssum", [P, NT]), sb("h_rs", [P, NT])
        s = sh.sem
        w_loaded = [s(f"h_w_loaded{q}") for q in range(UN)]
        wo_loaded = [s(f"h_wo_loaded{q}") for q in range(UN)]
        w_hi_ready, w_lo_ready, wo_ready, ssum_mm = s("h_w_hi"), s("h_w_lo"), s("h_wo"), s("h_ssum_mm")
        (hid_mm, out_mm, ai_mm, gate_mm, ht_mm, y_mm) = (s("h_" + n) for n in (
            "hid_mm", "out_mm", "ai_mm", "gate_mm", "ht_mm", "y_mm"))
        (raw_done, u_done, gate_read, ht_read, exp_done, sq_done) = (s("h_" + n) for n in (
            "raw_done", "u_done", "gate_read", "ht_read", "exp_done", "sq_done"))
        (conv, mul_done, seg_done, mat_done, yg_done, v_link, zeroed) = (s("h_" + n) for n in (
            "conv", "mul_done", "seg_done", "mat_done", "yg_done", "v_link", "zeroed"))
        (spread_done, score_dt_done, masked, summed, sq_added, exp_l) = (s("h_" + n) for n in (
            "spread_done", "score_dt_done", "masked", "summed", "sq_added", "exp_l"))
        norm = PostNorm(sh, "h")
        psum = sh.psum
        pair = lambda n: psum[:, 2 * n:2 * n + 2, :].rearrange("p a b -> p (a b)")
        X, Z = pair(0), pair(1)
        tiles = lambda ap: ap.rearrange("p (t n) -> p t n", t=NT)
        comp = lambda ap: ap.rearrange("p (t h n) -> p t h n", t=NT, h=HPT)
        flat = lambda ap: ap.rearrange("p t h n -> p (t h n)")

        def heads(tile, i):
            return tile[:, :, bass.ds(HPT * i, HPT)].unsqueeze(3).broadcast_to([P, NT, HPT, CS])

        block = ctx.enter_context(nc.Block())

        @block.sync
        def _(sp):
            def load(i, q, exists):
                if not isinstance(i, int) or i >= UN:
                    sp.wait_ge(w_lo_ready, i - UN + 1)
                sp.dma_start(w_in[:, q, :], io["s_w_in"][bass.ds(i, 1), :, :].rearrange("a p n -> p (a n)")).then_inc(w_loaded[q], 16)
                if not isinstance(i, int) or i >= UN:
                    sp.wait_ge(out_mm, i - UN + 1)
                sp.dma_start(w_out[:, q, :], io["s_w_out"][bass.ds(i, 1), :, :].rearrange("a p n -> p (a n)")).then_inc(wo_loaded[q], 16)
            pipeline(sp, NF, UN, load, 0)

        @block.tensor
        def _(pe):
            pe.wait_ge(zeroed, 2)
            for bank in range(4, 8):
                pe.matmul(psum[:, bank, :], sh.ident[:, :], mat[:, 0, 0:4, :].rearrange("p a n -> p (a n)"),
                          start=True, stop=False, skip_group_check=True)

            def out_part(i, q, tt):
                for t in tt:
                    mm = pe.matmul(psum[:, 4 + t // 2, (t % 2) * DM:(t % 2 + 1) * DM], yg[:, q % 2, t * P:(t + 1) * P],
                                   w_out[:, (q - 2) % UN, :], start=False, stop=False, skip_group_check=True)
                return mm

            def project(out, q, which):
                for h in range(2):
                    own = slice(h * HALF, (h + 1) * HALF)
                    for c in range(KC):
                        mm = split_products(pe, out[:, own], (w_hi[:, q % 2, which, c, :], w_lo[:, q % 2, which, c, :]),
                                            (sh.x_hi[:, c, own], sh.x_lo[:, c, own]), c == 0, c == KC - 1)
                return mm

            def step(i, q, exists):
                if exists(0):
                    pe.wait_ge(w_lo_ready, i + 1)
                    if exists(1):
                        pe.wait_ge(seg_done, 2 * i)
                    project(X, q, 0).then_inc(hid_mm, 1)
                if exists(2):
                    pe.wait_ge(wo_ready, i - 1)
                    pe.wait_ge(yg_done, i - 1)
                    out_part(i, q, range(NT // 2))
                if exists(1):
                    if exists(0):
                        pe.wait_ge(raw_done, i + 1)
                    else:
                        pe.wait_ge(seg_done, 2 * i)
                    pe.wait_ge(u_done, i)
                    for t in range(NT):
                        mm = pe.transpose(X[:, t * P:(t + 1) * P], acc[:, (q - 1) % 2, t * P:(t + 1) * P], sh.ident[:, :])
                    mm.then_inc(ht_mm, 1)
                if exists(0):
                    if exists(1) and not exists(2):
                        pe.wait_ge(gate_read, i)
                    project(Z, q, 1).then_inc(gate_mm, 1)
                    pe.wait_ge(spread_done, i + 1)
                    pe.wait_ge(raw_done, i + 1)
                    if exists(1):
                        pe.wait_ge(ht_read, i)
                    pe.matmul(X[:, 0:512], k.same_chunk[:, :], flat(spread[:, q % 2]), start=True, stop=True).then_inc(ai_mm, 1)
                if exists(2):
                    out_part(i, q, range(NT // 2, NT)).then_inc(out_mm, 1)
                if exists(1):
                    if exists(0):
                        pe.wait_ge(gate_read, i + 1)
                    pe.wait_ge(mat_done, i)
                    pe.wait_ge(ht_read, i)
                    for t in range(NT):
                        for hh in range(HPT):
                            own = slice(hh * SP, (hh + 1) * SP)
                            mm = pe.matmul(Z[own, t * P:(t + 1) * P], hid[:, (q - 1) % 2, t, own],
                                           mat[:, (q - 1) % 2, t * HPT + hh, :], start=True, stop=True)
                    mm.then_inc(y_mm, 1)
            pipeline(pe, NF, UN, step, 2)
            pe.wait_ge(sq_added, NF + 1)
            for t in range(NT):
                mm = pe.matmul(X[:, t:t + 1], sq_sum[:, t * P:(t + 1) * P], sh.ones[:, 0:1], start=True, stop=True)
            mm.then_inc(ssum_mm, 1)
            pe.wait_ge(out_mm, NF)
            norm.tensor(pe)

        @block.scalar
        def _(act):
            def split_weights(i, q, exists):
                act.wait_ge(w_loaded[q], 16 // UN * (i - q) + 16)
                if exists(2):
                    act.wait_ge(gate_mm, i - 1)
                act.activation(w_hi[:, q % 2].rearrange("p a c n -> p (a c n)"), w_in[:, q, :], ACT.Copy).then_inc(w_hi_ready, 1)

            def step(i, q, exists):
                if exists(1):
                    last = acc[:, (q - 1) % 2, :]
                    act.wait_ge(conv, i)
                    act.activation(last, last, ACT.Silu).then_inc(u_done, 1)
                if exists(0):
                    act.wait_ge(hid_mm, i + 1)
                    if exists(2):
                        act.wait_ge(conv, i - 1)
                    act.activation(raw[:, q % 2, :], X, ACT.Copy).then_inc(raw_done, 1)
                if exists(1):
                    act.wait_ge(ht_mm, i)
                    if exists(3):
                        act.wait_ge(y_mm, i - 2)
                    act.activation(hid[:, (q - 1) % 2].rearrange("p t n -> p (t n)"), X, ACT.Copy).then_inc(ht_read, 1)
                if exists(2):
                    if exists(4):
                        act.wait_ge(sq_added, i - 2)
                    act.wait_ge(yg_done, i - 1)
                    act.activation(sq[:, q % 2, :], yg[:, q % 2, :], ACT.Square).then_inc(sq_done, 1)
                if exists(0):
                    act.wait_ge(gate_mm, i + 1)
                    if exists(4):
                        act.wait_ge(yg_done, i - 3)
                    act.activation(gate[:, q, :], Z, ACT.Silu).then_inc(gate_read, 1)
                    act.wait_ge(seg_done, 2 * i + 2)
                    act.activation(flat(seg_m[:, q % 2]), flat(seg_m[:, q % 2]), ACT.Exp).then_inc(exp_done, 1)
                    act.wait_ge(masked, i + 1)
                    act.activation(flat(seg_l[:, q % 2]), flat(seg_l[:, q % 2]), ACT.Exp).then_inc(exp_l, 1)

            def turn(i, q, exists):
                if exists(0):
                    split_weights(i, q, exists)
                step(i - 1, (q - 1) % UN, lambda n: exists(n + 1))
            pipeline(act, NF, UN, turn, 3)
            norm.scalar(act)

        @block.gpsimd
        def _(pool):
            pool.memset(sq_sum[:, :], 0.0).then_inc(sq_added, 1)
            bc = lambda tile: tile[:, :].unsqueeze(1).unsqueeze(1).broadcast_to([P, NT, HPT, CS])

            def split_weights(i, q, exists):
                pool.wait_ge(w_hi_ready, i + 1)
                pool.tensor_tensor(w_lo[:, q % 2].rearrange("p a c n -> p (a c n)"), w_in[:, q, :],
                                   w_hi[:, q % 2].rearrange("p a c n -> p (a c n)"), ALU.subtract).then_inc(w_lo_ready, 1)

            def step(i, q, exists):
                if exists(0):
                    if exists(2):
                        pool.wait_ge(ai_mm, i - 1)
                    pool.tensor_tensor(spread[:, q % 2], heads(k.acum, i), bc(k.eye_c), ALU.mult).then_inc(spread_done, 1)
                    if exists(2):
                        pool.wait_ge(mat_done, i - 1)
                    pool.tensor_tensor(score_dt[:, q % 2], k.score[:, HPT * q:HPT * (q + 1), :, :].rearrange("p g t n -> p t g n"),
                                       heads(k.dt, i), ALU.mult).then_inc(score_dt_done, 1)
                    pool.wait_ge(seg_done, 2 * i + 2)
                    pool.tensor_tensor(seg_l[:, q % 2], seg[:, q % 2], bc(k.never_c), ALU.add).then_inc(masked, 1)
                if exists(0):
                    pool.wait_ge(exp_done, i + 1)
                    pool.wait_ge(exp_l, i + 1)
                    pool.tensor_tensor(seg_l[:, q % 2], seg_l[:, q % 2], seg_m[:, q % 2], ALU.add).then_inc(summed, 1)
                if exists(2):
                    pool.wait_ge(sq_done, i - 1)
                    pool.wait_ge(sq_added, i - 1)
                    pool.tensor_tensor(sq_sum[:, :], sq_sum[:, :], sq[:, q % 2, :], ALU.add).then_inc(sq_added, 1)

            def turn(i, q, exists):
                if exists(0):
                    split_weights(i, q, exists)
                step(i - 1, (q - 1) % UN, lambda n: exists(n + 1))
            pipeline(pool, NF, UN, turn, 3)

        @block.vector
        def _(v):
            link = Link(v, v_link)
            v.memset(mat[:, 0], 0.0).then_inc(zeroed, 1)
            v.memset(mat[:, 1], 0.0).then_inc(zeroed, 1)
            v.wait_ge(zeroed, 2)

            def step(i, q, exists):
                if exists(2):
                    v.wait_ge(y_mm, i - 1)
                    v.wait_ge(gate_read, i - 1)
                    if exists(4):
                        v.wait_ge(out_mm, i - 3)
                        v.wait_ge(sq_done, i - 3)
                    v.tensor_tensor(yg[:, q % 2, :], Z, gate[:, (q - 2) % UN, :], ALU.mult).then_inc(yg_done, 1)
                if exists(0):
                    v.wait_ge(wo_loaded[q], 16 // UN * (i - q) + 16)
                    v.tensor_scalar(w_out[:, q, :], w_out[:, q, :], k.norm_w[:, bass.ds(i, 1)], None, ALU.mult).then_inc(wo_ready, 1)
                if exists(1):
                    m = (q - 1) % 2
                    v.wait_ge(summed, i)
                    v.wait_ge(score_dt_done, i)
                    v.tensor_tensor(seg_l[:, m], seg_l[:, m], score_dt[:, m], ALU.mult).then_inc(mul_done, 1)
                    v.wait_ge(mul_done, i)
                    if exists(3):
                        v.wait_ge(y_mm, i - 2)
                    for c in range(QUAD):
                        own = slice(c * CS, (c + 1) * CS)
                        ins = v.tensor_tensor(mat[own, m, :, own].rearrange("p (t h) n -> p t h n", t=NT), seg_l[own, m],
                                              k.d_eye[own, bass.ds(HPT * (i - 1), HPT), :].unsqueeze(1).broadcast_to([CS, NT, HPT, CS]),
                                              ALU.add)
                    ins.then_inc(mat_done, 1)
                if exists(0):
                    v.wait_ge(raw_done, i + 1)
                    if exists(2):
                        v.wait_ge(ht_mm, i - 1)
                    w = k.conv[:, bass.ds(i, 1), :].rearrange("p a n -> p (a n)")
                    link.n = 3 * i
                    link(v.tensor_scalar(acc[:, q % 2, :], raw[:, q % 2, :], w[:, SK - 1:SK], w[:, SK:SK + 1], ALU.mult, ALU.add))
                    conv_taps(v, link, acc[:, q % 2, :], raw[:, q % 2, :], w, conv)
                    v.wait_ge(ai_mm, i + 1)
                    if exists(2):
                        v.wait_ge(summed, i - 1)
                    z = comp(X[:, 0:512])
                    v.tensor_tensor(seg[:, q % 2], z, heads(k.acum, i), ALU.subtract).then_inc(seg_done, 1)
                    v.tensor_tensor(seg_m[:, q % 2], z, heads(k.to_last, i), ALU.add).then_inc(seg_done, 1)
            pipeline(v, NF, UN, step, 2)
            v.wait_ge(ssum_mm, 1)
            link.n = 3 * NF
            link(v.tensor_scalar(ssum[:, :], X[:, 0:NT], 1.0 / SI, None, ALU.mult))
            rsqrt_on_vector(v, link, rs[:, :], ssum[:, :], sh.tmp(NT), 1e-6)
            v.wait_ge(out_mm, NF)
            v.sem_inc(norm.y_ready, NT)
            norm.vector(v, add=lambda t: v.scalar_tensor_tensor(
                out=sh.x_tok[:, t, :], in0=psum[:, 4 + t // 2, (t % 2) * DM:(t % 2 + 1) * DM], scalar=rs[:, t:t + 1],
                in1=sh.x_tok[:, t, :], op0=ALU.mult, op1=ALU.add))


ROPE = HD // 2
KT = 2 * SEQ // P
QT = SEQ // P
TWO_PI = 6.283185307179586
PI_1 = 6.28125
PI_2 = 0.0019350051879882812
PI_3 = TWO_PI - PI_1 - PI_2
ROUND = 12582912.0
PI_F = 3.1415925


def rope_tables(nc, sh, io, tabs, w_kv, w_query, w_o, loaded_w):
    NTAB = BATCH * KT
    with ExitStack() as ctx:
        def sb(name, shape, dt=F32):
            return ctx.enter_context(nc.sbuf_tensor(name, shape, dt))

        pos, pos_f = sb("r_pos", [P, NTAB], I32), sb("r_pos_f", [P, NTAB])
        rows = sb("r_rows", [P, 5, ROPE])
        freq, w_q, w_k = rows[:, 0, :], rows[:, 1:3, :], rows[:, 3:5, :]
        arg, cyc, rem = (sb("r_" + n, [P, NTAB, ROPE]) for n in ("arg", "cyc", "rem"))
        sin, cos = sb("r_sin", [P, NTAB, ROPE]), sb("r_cos", [P, NTAB, ROPE])
        kv_raw = sb("r_kv_raw", [P, KC * KVH * 2 * HD])
        s = sh.sem
        loaded, v_link, reduced, looked_up = s("r_loaded"), s("r_v_link"), s("r_reduced"), s("r_looked_up")
        kv_loaded, kv_split = s("r_kv_loaded"), s("r_kv_split")
        block = ctx.enter_context(nc.Block())

        @block.sync
        def _(sp):
            sp.dma_start(pos[:, :], io["r_pos"]).then_inc(loaded, 16)
            sp.dma_start(rows[:, :, :].rearrange("p a n -> p (a n)"), io["r_rows"].partition_broadcast(P).rearrange("p a n -> p (a n)")).then_inc(loaded, 16)
            sp.dma_start(kv_raw[:, :], io["a_w_kv"].rearrange("p c g n -> p (c g n)")).then_inc(kv_loaded, 16)
            sp.dma_start(w_query[:, :, :, :], io["a_w_q"]).then_inc(loaded_w, 16)
            sp.dma_start(w_o[:, :, :], io["a_w_o"]).then_inc(loaded_w, 16)

        @block.gpsimd
        def _(pool):
            hi, lo = (w[:, :, :, :].rearrange("p c g n -> p (c g n)") for w in w_kv)
            pool.wait_ge(kv_loaded, 16)
            pool.tensor_copy(hi, kv_raw[:, :]).then_inc(kv_split, 1)
            pool.wait_ge(kv_split, 1)
            pool.tensor_tensor(lo, kv_raw[:, :], hi, ALU.subtract).then_inc(kv_split, 1)
            pool.wait_ge(kv_split, 2)

        @block.scalar
        def _(act):
            for n, out in enumerate((sin, cos)):
                act.wait_ge(reduced, n + 1)
                act.activation(out[:, :, :], (rem if n == 0 else arg)[:, :, :], ACT.Sin).then_inc(looked_up, 1)

        @block.vector
        def _(v):
            link = Link(v, v_link)
            v.wait_ge(loaded, 32)
            link(v.tensor_copy(pos_f[:, :], pos[:, :]))
            link(v.tensor_tensor(arg[:, :, :], pos_f[:, :].unsqueeze(2).broadcast_to([P, NTAB, ROPE]),
                                 freq.unsqueeze(1).broadcast_to([P, NTAB, ROPE]), ALU.mult))
            for shift, out in ((0.0, rem), (0.25, arg)):
                link(v.tensor_scalar(cyc[:, :, :], arg[:, :, :], 1.0 / TWO_PI, shift, ALU.mult, ALU.add))
                link(v.tensor_scalar(cyc[:, :, :], cyc[:, :, :], ROUND, ROUND, ALU.add, ALU.subtract))
                link(v.scalar_tensor_tensor(out=out[:, :, :], in0=cyc[:, :, :], scalar=-PI_1, in1=arg[:, :, :], op0=ALU.mult, op1=ALU.add))
                link(v.scalar_tensor_tensor(out=out[:, :, :], in0=cyc[:, :, :], scalar=-PI_2, in1=out[:, :, :], op0=ALU.mult, op1=ALU.add))
                link(v.scalar_tensor_tensor(out=out[:, :, :], in0=cyc[:, :, :], scalar=-PI_3, in1=out[:, :, :], op0=ALU.mult, op1=ALU.add))
                if shift:
                    link(v.tensor_scalar(out[:, :, :], out[:, :, :], TWO_PI / 4, None, ALU.add))
                v.tensor_scalar(out[:, :, :], out[:, :, :], PI_F, -PI_F, ALU.min, ALU.max).then_inc(reduced, 1)
            v.wait_ge(looked_up, 2)
            for name, w in (("k", w_k), ("q", w_q)):
                c_tab, s_tab = tabs[name]
                pick = (lambda t: t[:, :, :]) if name == "k" else (
                    lambda t: t[:, :, :].rearrange("p (b t) n -> p b t n", b=BATCH)[:, :, KT - QT:KT, :])
                shape = [P, NTAB, ROPE] if name == "k" else [P, BATCH, QT, ROPE]

                def wide(ap):
                    ap = ap.unsqueeze(1)
                    return ap.broadcast_to(shape) if name == "k" else ap.unsqueeze(1).broadcast_to(shape)

                part = lambda t, half: (t[:, :, half, :] if name == "k" else
                                        t[:, :, half, :].rearrange("p (b t) n -> p b t n", b=BATCH))
                for half in range(2):
                    link.mark(v.tensor_tensor(part(c_tab, half), pick(cos), wide(w[:, half, :]), ALU.mult))
                    link.mark(v.tensor_tensor(part(s_tab, half), pick(sin), wide(w[:, 1 - half, :]), ALU.mult))
                link.wait()
                link(v.tensor_scalar(s_tab[:, :, 0, :], s_tab[:, :, 0, :], -1.0, None, ALU.mult))


def stage_attention(nc, sh, io):
    with ExitStack() as ctx:
        def sb(name, shape, dt=F32):
            return ctx.enter_context(nc.sbuf_tensor(name, shape, dt))

        k_cos, k_sin = (sb("a_k_" + n, [P, BATCH * KT, 2, ROPE]) for n in ("cos", "sin"))
        q_cos, q_sin = (sb("a_q_" + n, [P, BATCH * QT, 2, ROPE]) for n in ("cos", "sin"))
        w_kv = [sb("a_w_kv_" + n, [P, KC, KVH, 2 * HD], F32R) for n in ("hi", "lo")]
        w_q, w_o = sb("a_w_q", [P, KC, KVH, REP * HD]), sb("a_w_o", [P, QH, DM])
        loaded = sh.sem("a_loaded")
        rope_tables(nc, sh, io, {"k": (k_cos, k_sin), "q": (q_cos, q_sin)}, w_kv, w_q, w_o, loaded)
        src = [sb("a_src_" + n, [P, KC, 2 * SEQ], F32R) for n in ("hi", "lo")]
        src_own = sb("a_src_own", [P, KC, SEQ])
        k_rot, k_t2 = (sb("a_" + n, [P, KT, 2, ROPE]) for n in ("k_rot", "k_t2"))
        q_rot, q_t2 = (sb("a_" + n, [P, QT, REP, 2, ROPE]) for n in ("q_rot", "q_t2"))
        sq = sb("a_sq", [P, KT + QT * REP, HD])
        three_halves, soft_scale = sb("a_three_halves", [P, KT + QT * REP]), sb("a_soft_scale", [P, QT * REP])
        ms, rs = sb("a_ms", [P, KT + QT * REP]), sb("a_rs", [P, KT + QT * REP])
        q_scale = sb("a_q_scale", [P, 2, QT * REP])
        k_t, q_t = sb("a_k_t", [P, KT, HD]), sb("a_q_t", [P, QT, REP, HD])
        k_f = [sb("a_k_f_" + n, [P, 2, 2 * SEQ], F32R) for n in ("hi", "lo")]
        q_f = [sb("a_q_f_" + n, [P, 2, REP, SEQ], F32R) for n in ("hi", "lo")]
        val = [sb("a_val_" + n, [P, 2, KT, HD], F32R) for n in ("hi", "lo")]
        neg_max, bias, total, inv = (sb("a_" + n, [P, QT]) for n in ("neg_max", "bias", "total", "inv"))
        prob = sb("a_prob", [P, 2, QT, 2 * SEQ])
        prob_t = [sb("a_prob_t_" + n, [P, 2, QT, KT, P], F32R) for n in ("hi", "lo")]
        attn_f = sb("a_attn_f", [P, 2, SEQ])
        s = sh.sem
        (src_ready, kv_mm, q_mm, kt_mm, qt_mm, s_mm, p_mm, pv_mm, wo_mm) = (s("a_" + n) for n in (
            "src_ready", "kv_mm", "q_mm", "kt_mm", "qt_mm", "s_mm", "p_mm", "pv_mm", "wo_mm"))
        (k_sq, kv_read, q_sq, k_turned, q_turned, exp_done, p_turned, attn_read) = (s("a_" + n) for n in (
            "k_sq", "kv_read", "q_sq", "k_turned", "q_turned", "exp_done", "p_turned", "attn_read"))
        (k_parts, q_parts, seeded, q_rs_done, bias_done, scaled, y_read, v_link, p_link) = (s("a_" + n) for n in (
            "k_parts", "q_parts", "seeded", "q_rs_done", "bias_done", "scaled", "y_read", "v_link", "p_link"))
        k_rot_done, q_rot_done, g_link, q_read = s("a_k_rot_done"), s("a_q_rot_done"), s("a_g_link"), s("a_q_read")
        const = s("a_const")
        (val_hi, val_split, k_hi, q_hi, p_hi) = (s("a_" + n) for n in ("val_hi", "val_split", "k_hi", "q_hi", "p_hi"))
        norm = PostNorm(sh, "a")
        psum = sh.psum
        SCORE, TURN, PV, OUT, PROJ = 0, 2, 4, 5, 6
        proj = psum[:, PROJ:PROJ + 2, :]
        kv_psum = proj.rearrange("p b (t n) -> p (b t) n", t=2)
        proj_flat = proj.rearrange("p b n -> p (b n)")
        NG = BATCH * KVH

        def over_batches(eng, body):
            body(0, True, False)
            with eng.Fori(1, BATCH - 1) as b:
                body(b, False, False)
            body(BATCH - 1, False, True)

        def plan(last):
            for kvh in range(KVH):
                for j in range(REP):
                    yield kvh, j, not (last and kvh == KVH - 1)

        block = ctx.enter_context(nc.Block())

        @block.gpsimd
        def _(pool):
            def take_source(b):
                context = sh.ctx_feat[:, :, bass.ds(b, 1), :].rearrange("p c a n -> p c (a n)")
                own = bass.ds(SEQ * b, SEQ)
                pool.tensor_copy(src[0][:, :, 0:SEQ], context).then_inc(src_ready, 1)
                for part, x in zip(src, (sh.x_hi, sh.x_lo)):
                    pool.tensor_copy(part[:, :, SEQ:2 * SEQ], x[:, :, own]).then_inc(src_ready, 1)
                pool.wait_ge(src_ready, 5 * b + 1)
                pool.tensor_copy(src_own[:, :, :], sh.x_feat[:, :, own]).then_inc(src_ready, 1)
                pool.tensor_tensor(src[1][:, :, 0:SEQ], context, src[0][:, :, 0:SEQ], ALU.subtract).then_inc(src_ready, 1)

            def keys(g):
                pool.wait_ge(k_parts, g + 1)
                pool.tensor_tensor(k_rot[:, :, :, :], k_rot[:, :, :, :], k_t2[:, :, :, :], ALU.add).then_inc(g_link, 1)

            def factors(g, slot):
                link = Link(pool, p_link)
                link.n = (2 + 4 * NEWTON) * g
                tmp = sh.tmp(KT + QT * REP)[0]
                pool.wait_ge(seeded, g + 1)
                for _ in range(NEWTON):
                    link(pool.tensor_tensor(tmp, rs[:, :], rs[:, :], ALU.mult))
                    link(pool.tensor_tensor(tmp, tmp, ms[:, :], ALU.mult))
                    link(pool.tensor_tensor(tmp, tmp, three_halves[:, :], ALU.add))
                    link(pool.tensor_tensor(rs[:, :], rs[:, :], tmp, ALU.mult))
                link(pool.tensor_tensor(q_scale[:, slot, :], rs[:, KT:KT + QT * REP], soft_scale[:, :], ALU.mult))
                pool.sem_inc(q_rs_done, 1)
                k_rs = rs[:, 0:KT]
                pool.wait_ge(g_link, g + 1)
                flat = k_rot[:, :, :, :].rearrange("p t a n -> p t (a n)")
                link.mark(pool.tensor_tensor(flat, flat, k_rs.unsqueeze(2).broadcast_to([P, KT, HD]), ALU.mult))
                link.wait()
                pool.sem_inc(k_rot_done, 1)

            def queries(g):
                pool.wait_ge(q_parts, g + 1)
                pool.tensor_tensor(q_rot[:, :, :, :, :].rearrange("p t h a n -> p (t h a n)"),
                                   q_rot[:, :, :, :, :].rearrange("p t h a n -> p (t h a n)"),
                                   q_t2[:, :, :, :, :].rearrange("p t h a n -> p (t h a n)"), ALU.add).then_inc(q_rot_done, 1)

            pool.memset(three_halves[:, :], 1.5).then_inc(const, 1)
            pool.memset(soft_scale[:, :], HD ** -0.5).then_inc(const, 1)
            pool.wait_ge(const, 2)
            take_source(0)
            queries(0)
            keys(0)
            factors(0, 0)

            def body(b, first, last):
                for kvh, j, more in plan(last):
                    if not more:
                        continue
                    g = KVH * b + kvh + 1
                    if kvh == KVH - 1 and j == 0:
                        pool.wait_ge(kv_mm, g)
                        take_source(b + 1)
                    if j == 0:
                        queries(g)
                    if j == 1:
                        keys(g)
                        factors(g, (kvh + 1) % 2)
            over_batches(pool, body)

        @block.tensor
        def _(pe):
            pe.sem_inc(p_mm, 2 * QT)
            pe.sem_inc(pv_mm, 1)
            pe.wait_ge(loaded, 32)

            def project_kv(g, kvh):
                pe.wait_ge(q_read, g + 1)
                for t in range(KT):
                    for c in range(KC):
                        mm = split_products(pe, kv_psum[:, t, :], [x[:, c, t * P:(t + 1) * P] for x in src],
                                            [w[:, c, kvh, :] for w in w_kv], c == 0, c == KC - 1)
                mm.then_inc(kv_mm, 1)

            def project_q(g, kvh, b):
                pe.wait_ge(src_ready, 5 * b + 5)
                wait_beyond_start(pe, k_turned, g)
                for t in range(QT):
                    for c in range(KC):
                        mm = pe.matmul(psum[:, PROJ + t, :], src_own[:, c, t * P:(t + 1) * P], w_q[:, c, kvh, :], start=c == 0, stop=c == KC - 1)
                mm.then_inc(q_mm, 1)

            def turn_k(g):
                pe.wait_ge(k_rot_done, g + 1)
                pe.wait_ge(q_turned, g + 1)
                for t in range(KT):
                    mm = pe.transpose(proj_flat[:, t * P:(t + 1) * P], k_rot[:, t, :, :].rearrange("p a n -> p (a n)"), sh.ident[:, :])
                mm.then_inc(kt_mm, 1)

            def turn_q(g):
                pe.wait_ge(q_rot_done, g + 1)
                pe.wait_ge(val_split, g + 1)
                for h in range(REP):
                    for t in range(QT):
                        at = (h * QT + t) * P
                        mm = pe.transpose(proj_flat[:, at:at + P], q_rot[:, t, h, :, :].rearrange("p a n -> p (a n)"), sh.ident[:, :])
                mm.then_inc(qt_mm, 1)

            def scores(n, g, slot, h):
                if h == 0:
                    pe.wait_ge(k_turned, g + 1)
                    pe.wait_ge(q_turned, g + 1)
                for t in range(QT):
                    pe.wait_ge(exp_done, QT * n + t + 1)
                    split_products(pe, psum[:, SCORE + t, :], [q[:, slot, h, t * P:(t + 1) * P] for q in q_f],
                                   [x[:, slot, :] for x in k_f], True, True).then_inc(s_mm, 1)

            def turn_probs(n, p):
                for t in range(QT):
                    pe.wait_ge(scaled, QT * n + t + 1)
                    pe.wait_ge(p_turned, QT * n + t + 1)
                    for c in range(KT):
                        mm = pe.transpose(psum[:, TURN + t, c * P:(c + 1) * P], prob[:, p, t, c * P:(c + 1) * P], sh.ident[:, :])
                    mm.then_inc(p_mm, 1)

            def values(n, slot, p):
                pe.wait_ge(p_turned, QT * n + 2 * QT)
                pe.wait_ge(attn_read, n + 1)
                for c in range(KT):
                    mm = split_products(pe, psum[:, PV, 0:SEQ], [x[:, slot, c, :] for x in val],
                                        [x[:, p, :, c, :] for x in prob_t], c == 0, c == KT - 1)
                mm.then_inc(pv_mm, 1)

            def output(n, m, b):
                pe.wait_ge(attn_read, n + 2)
                if m == 0 and not (isinstance(b, int) and b == 0):
                    pe.wait_ge(y_read, b)
                for t in range(QT):
                    mm = pe.matmul(psum[:, OUT, t * DM:(t + 1) * DM], attn_f[:, m % 2, t * P:(t + 1) * P], w_o[:, m, :],
                                   start=m == 0 and t == 0, stop=m == QH - 1, skip_group_check=True)
                mm.then_inc(wo_mm, 1)

            project_q(0, 0, 0)
            project_kv(0, 0)
            turn_q(0)
            turn_k(0)

            def body(b, first, last):
                for kvh, j, more in plan(last):
                    m = REP * kvh + j
                    n, g = QH * b + m, KVH * b + kvh
                    nb, nk = (b, kvh + 1) if kvh < KVH - 1 else (b + 1, 0)
                    scores(n, g, kvh % 2, j)
                    if more and j == 3:
                        turn_k(g + 1)
                    if m >= 2 or not first:
                        values(n - 2, (m - 2) // REP % 2, m % 2)
                    if m >= 1 or not first:
                        turn_probs(n - 1, (m - 1) % 2)
                    if more and j == 0:
                        project_q(g + 1, nk, nb)
                    if more and j == 1:
                        project_kv(g + 1, nk)
                    if m >= 3 or not first:
                        output(n - 3, (m - 3) % QH, b)
                    if more and j == 2:
                        turn_q(g + 1)
            over_batches(pe, body)
            n, m = QH * BATCH, QH
            values(n - 2, (m - 2) // REP % 2, m % 2)
            turn_probs(n - 1, (m - 1) % 2)
            output(n - 3, m - 3, BATCH)
            values(n - 1, (m - 1) // REP % 2, (m - 1) % 2)
            output(n - 2, m - 2, BATCH)
            output(n - 1, m - 1, BATCH)
            norm.tensor(pe)

        @block.scalar
        def _(act):
            act.sem_inc(exp_done, QT)
            act.sem_inc(attn_read, 1)

            def squares(x, n):
                return act.activation(sq[:, n, :], x, ACT.Square, accum_out=ms[:, n:n + 1])

            def keys(g):
                act.wait_ge(kv_mm, g + 1)
                if not (isinstance(g, int) and g == 0):
                    act.wait_ge(k_parts, g)
                    act.wait_ge(k_sq, g)
                act.activation(k_t[:, :, :], kv_psum[:, :, 0:HD], ACT.Copy).then_inc(kv_read, 1)
                act.wait_ge(kv_read, g + 1)
                wait_beyond_start(act, q_rs_done, g)
                for t in range(KT):
                    ins = squares(k_t[:, t, :], t)
                ins.then_inc(k_sq, 1)

            def values(g, slot):
                if not (isinstance(g, int) and g == 0):
                    act.wait_ge(pv_mm, REP * (g - 1) + 1)
                act.wait_ge(kv_mm, g + 1)
                act.activation(val[0][:, slot, :, :], kv_psum[:, :, HD:2 * HD], ACT.Copy).then_inc(val_hi, 1)

            def queries(g):
                act.wait_ge(q_mm, g + 1)
                wait_beyond_start(act, q_parts, g)
                act.activation(q_t[:, :, :, :].rearrange("p t h n -> p (t h n)"), proj_flat, ACT.Copy).then_inc(q_read, 1)
                act.wait_ge(q_read, g + 1)
                for n in range(QT * REP):
                    ins = squares(q_t[:, n // REP, n % REP, :], KT + n)
                ins.then_inc(q_sq, 1)

            def keys_turned(g, slot):
                act.wait_ge(kt_mm, g + 1)
                act.activation(k_f[0][:, slot, :], proj_flat[:, 0:2 * SEQ], ACT.Copy).then_inc(k_hi, 1)

            def queries_turned(g, slot):
                act.wait_ge(qt_mm, g + 1)
                act.activation(q_f[0][:, slot, :, :].rearrange("p h n -> p (h n)"), proj_flat, ACT.Copy).then_inc(q_hi, 1)

            def probs_turned(n, t, p):
                act.wait_ge(p_mm, QT * n + t + 1 + 2 * QT)
                wait_beyond_start(act, pv_mm, n)
                act.activation(prob_t[0][:, p, t, :, :].rearrange("p c n -> p (c n)"), psum[:, TURN + t, :], ACT.Copy).then_inc(p_hi, 1)

            def exps(n, t, slot, h, p):
                act.wait_ge(bias_done, QT * n + t + 1)
                act.wait_ge(p_mm, QT * n + QT)
                act.activation(prob[:, p, t, :], psum[:, SCORE + t, :], ACT.Exp, bias=bias[:, t:t + 1],
                               scale=q_scale[:, slot, t * REP + h:t * REP + h + 1], accum_out=total[:, t:t + 1]).then_inc(exp_done, 1)

            def attended(n, m):
                act.wait_ge(pv_mm, n + 2)
                if not isinstance(n, int) or n >= 2:
                    act.wait_ge(wo_mm, n - 1)
                act.activation(attn_f[:, m % 2, :], psum[:, PV, 0:SEQ], ACT.Copy).then_inc(attn_read, 1)

            queries(0)
            keys(0)
            values(0, 0)
            queries_turned(0, 0)
            keys_turned(0, 0)

            def body(b, first, last):
                for kvh, j, more in plan(last):
                    m = REP * kvh + j
                    n, g, nxt = QH * b + m, KVH * b + kvh, (kvh + 1) % 2
                    for t in range(QT):
                        exps(n, t, kvh % 2, j, m % 2)
                    if m >= 2 or not first:
                        attended(n - 2, (m - 2) % QH)
                    if more and j == 3:
                        keys_turned(g + 1, nxt)
                    if m >= 1 or not first:
                        for t in range(QT):
                            probs_turned(n - 1, t, (m - 1) % 2)
                    if more and j == 0:
                        queries(g + 1)
                    if more and j == 1:
                        keys(g + 1)
                        values(g + 1, nxt)
                    if more and j == 2:
                        queries_turned(g + 1, nxt)
            over_batches(act, body)
            n = QH * BATCH - 1
            attended(n - 1, 0)
            for t in range(QT):
                probs_turned(n, t, 1)
            attended(n, 1)
            norm.scalar(act)

        @block.vector
        def _(v):
            link = Link(v, v_link)
            v.sem_inc(p_turned, QT)

            def keys(g, b, slot):
                v.wait_ge(kv_read, g + 1)
                wait_beyond_start(v, kt_mm, g)
                x = k_t[:, :, :].rearrange("p t (a n) -> p t a n", a=2)
                cos, sin = (tab[:, bass.ds(KT * b, KT), :, :] for tab in (k_cos, k_sin))
                link.mark(v.tensor_tensor(k_rot[:, :, :, :], x, cos, ALU.mult))
                for half in range(2):
                    link.mark(v.tensor_tensor(k_t2[:, :, half, :], x[:, :, 1 - half, :], sin[:, :, half, :], ALU.mult))
                link.wait()
                v.sem_inc(k_parts, 1)

            def values(g, slot):
                v.wait_ge(val_hi, g + 1)
                v.tensor_tensor(val[1][:, slot, :, :], kv_psum[:, :, HD:2 * HD], val[0][:, slot, :, :], ALU.subtract).then_inc(val_split, 1)

            def queries(g, b, slot):
                v.wait_ge(q_read, g + 1)
                wait_beyond_start(v, qt_mm, g)
                for t in range(QT):
                    x = q_t[:, t, :, :].rearrange("p h (a n) -> p h a n", a=2)
                    cos, sin = (tab[:, bass.ds(QT * b + t, 1), :, :] for tab in (q_cos, q_sin))
                    link.mark(v.tensor_tensor(q_rot[:, t, :, :, :], x, cos.broadcast_to([P, REP, 2, ROPE]), ALU.mult))
                    for half in range(2):
                        link.mark(v.tensor_tensor(q_t2[:, t, :, half, :], x[:, :, 1 - half, :],
                                                  sin[:, :, half, :].broadcast_to([P, REP, ROPE]), ALU.mult))
                link.wait()
                v.sem_inc(q_parts, 1)

            def seeds(g):
                v.wait_ge(k_sq, g + 1)
                v.wait_ge(q_sq, g + 1)
                wait_beyond_start(v, k_rot_done, g)
                link(v.tensor_scalar(ms[:, :], ms[:, :], 1.0 / HD, 1e-6, ALU.mult, ALU.add))
                rsqrt_seed(v, link, rs[:, :], ms[:, :], sh.tmp(KT + QT * REP)[1])
                link(v.tensor_scalar(ms[:, :], ms[:, :], -0.5, None, ALU.mult))
                v.sem_inc(seeded, 1)

            def maxima(n, g, slot, h):
                if h == 0:
                    v.wait_ge(q_rs_done, g + 1)
                for t in range(QT):
                    v.wait_ge(s_mm, QT * n + t + 1)
                    link(v.tensor_reduce(neg_max[:, t:t + 1], psum[:, SCORE + t, :], AX.X, ALU.max, negate=True))
                    v.tensor_tensor(bias[:, t:t + 1], neg_max[:, t:t + 1], q_scale[:, slot, t * REP + h:t * REP + h + 1],
                                    ALU.mult).then_inc(bias_done, 1)

            def scale_probs(n, p):
                for t in range(QT):
                    v.wait_ge(exp_done, QT * n + t + 1 + QT)
                    link(v.reciprocal(inv[:, t:t + 1], total[:, t:t + 1]))
                    v.tensor_scalar(prob[:, p, t, :], prob[:, p, t, :], inv[:, t:t + 1], None, ALU.mult).then_inc(scaled, 1)

            def keys_turned(g, slot):
                v.wait_ge(k_hi, g + 1)
                v.tensor_tensor(k_f[1][:, slot, :], proj_flat[:, 0:2 * SEQ], k_f[0][:, slot, :], ALU.subtract).then_inc(k_turned, 1)

            def queries_turned(g, slot):
                v.wait_ge(q_hi, g + 1)
                v.tensor_tensor(q_f[1][:, slot, :, :].rearrange("p h n -> p (h n)"), proj_flat,
                                q_f[0][:, slot, :, :].rearrange("p h n -> p (h n)"), ALU.subtract).then_inc(q_turned, 1)

            def probs_turned(n, t, p):
                v.wait_ge(p_hi, QT * n + t + 1)
                v.tensor_tensor(prob_t[1][:, p, t, :, :].rearrange("p c n -> p (c n)"), psum[:, TURN + t, :],
                                prob_t[0][:, p, t, :, :].rearrange("p c n -> p (c n)"), ALU.subtract).then_inc(p_turned, 1)

            def residual(b):
                v.wait_ge(wo_mm, QH * (b + 1))
                for t in range(QT):
                    x = sh.x_tok[:, bass.ds(QT * b + t, 1), :].rearrange("p a n -> p (a n)")
                    link(v.tensor_tensor(x, x, psum[:, OUT, t * DM:(t + 1) * DM], ALU.add))
                v.sem_inc(y_read, 1)

            queries(0, 0, 0)
            keys(0, 0, 0)
            values(0, 0)
            seeds(0)
            queries_turned(0, 0)
            keys_turned(0, 0)

            def body(b, first, last):
                for kvh, j, more in plan(last):
                    m = REP * kvh + j
                    n, g, nxt = QH * b + m, KVH * b + kvh, (kvh + 1) % 2
                    nb = b if kvh < KVH - 1 else b + 1
                    if m == 3 and not first:
                        residual(b - 1)
                    maxima(n, g, kvh % 2, j)
                    scale_probs(n, m % 2)
                    if more and j == 3:
                        keys_turned(g + 1, nxt)
                    if m >= 1 or not first:
                        for t in range(QT):
                            probs_turned(n - 1, t, (m - 1) % 2)
                    if more and j == 0:
                        queries(g + 1, nb, nxt)
                    if more and j == 1:
                        keys(g + 1, nb, nxt)
                        values(g + 1, nxt)
                        seeds(g + 1)
                    if more and j == 2:
                        queries_turned(g + 1, nxt)

            body(0, True, False)
            first = link.n
            per_seq = 2 * QT * QH + KVH * (3 + 3 * QT + 4) + QT
            with v.Fori(1, BATCH - 1) as b:
                link.base, link.n = first + per_seq * (b - 1), 0
                body(b, False, False)
                assert link.n == per_seq
            link.base, link.n = 0, first + per_seq * (BATCH - 2)
            body(BATCH - 1, False, True)
            for t in range(QT):
                probs_turned(QH * BATCH - 1, t, 1)
            residual(BATCH - 1)
            v.wait_ge(y_read, BATCH)
            v.sem_inc(norm.y_ready, NT)
            norm.vector(v, add=IN_PLACE)
NSH = ISH // IM
NV = NE + NSH
IC = 2
IP = IM // IC


def stage_moe(nc, sh, io):
    with ExitStack() as ctx:
        def sb(name, shape, dt=F32):
            return ctx.enter_context(nc.sbuf_tensor(name, shape, dt))

        w_r = sb("x_w_r", [P, KC, NE + 1])
        w_gu, w_dn = sb("x_w_gu", [P, 2, KC, 2 * IM]), sb("x_w_dn", [IP, 2, IC, DM])
        logit, shifted = sb("x_logit", [P, NT, NE + 1]), sb("x_shifted", [P, NT, NE])
        neg_max, total = sb("x_neg_max", [P, NT]), sb("x_total", [P, NT])
        prob, top, hit = sb("x_prob", [P, NT, NE]), sb("x_top", [P, NT, 8]), sb("x_hit", [P, NT, NE])
        top_at, top_at_f = sb("x_top_at", [P, NT, 8], U32), sb("x_top_at_f", [P, NT, 2])
        expert, expert_f = sb("x_expert", [P, NE], I32), sb("x_expert_f", [P, NE])
        share = sb("x_share", [P, NT, NV])
        zeros = sb("x_zeros", [P, 512])
        silu, hid = sb("x_silu", [P, 2, IM]), sb("x_hid", [P, 2, IM])
        hid_f = sb("x_hid_f", [IP, 2, IC, P])
        s = sh.sem
        r_loaded, const, r_mm, r_act, v_link = (s("x_" + n) for n in ("r_loaded", "const", "r_mm", "r_act", "v_link"))
        shifted_done, share_ready, logit_ready = s("x_shifted_done"), s("x_share_ready"), s("x_logit_ready")
        gu_loaded = [s(f"x_gu_loaded{i}") for i in range(2)]
        dn_loaded = [s(f"x_dn_loaded{i}") for i in range(2)]
        gu_mm, ht_mm, dn_mm, silu_done, ht_read, hid_done, stored = (s("x_" + n) for n in (
            "gu_mm", "ht_mm", "dn_mm", "silu_done", "ht_read", "hid_done", "stored"))
        norm = PostNorm(sh, "x", last=True)
        psum = sh.psum
        TURN = 2 * NT
        block = ctx.enter_context(nc.Block())

        @block.sync
        def _(sp):
            sp.dma_start(w_r[:, :, :], io["x_w_r"]).then_inc(r_loaded, 16)

            def load(v, slot, first):
                if not first:
                    sp.wait_ge(gu_mm, NT * (v - 1))
                sp.dma_start(w_gu[:, slot, :, :], io["x_w_gu"][bass.ds(v, 1), :, :, :].rearrange("a p c n -> p (a c) n")).then_inc(gu_loaded[slot], 16)
                if not first:
                    sp.wait_ge(dn_mm, NT * (v - 1))
                sp.dma_start(w_dn[:, slot, :, :], io["x_w_dn"][bass.ds(v, 1), :, :, :].rearrange("a p c n -> p (a c) n")).then_inc(dn_loaded[slot], 16)

            load(0, 0, True)
            load(1, 1, True)
            with sp.Fori(1, NV // 2) as r:
                for slot in range(2):
                    load(2 * r + slot, slot, False)
            if sh.out is not None:
                for t in range(NT):
                    sp.wait_ge(norm.normed, t + 1)
                    sp.dma_start(sh.out[t * P:(t + 1) * P, :], sh.x_tok[:, t, :]).then_inc(stored, 16)
                sp.wait_ge(stored, 16 * NT)

        @block.gpsimd
        def _(pool):
            pool.memset(zeros[:, :], 0.0).then_inc(const, 1)
            pool.iota(expert[:, :], pattern=[[1, NE]], base=0, channel_multiplier=0).then_inc(const, 1)
            pool.wait_ge(const, 2)
            pool.tensor_copy(expert_f[:, :], expert[:, :]).then_inc(const, 1)

        @block.tensor
        def _(pe):
            pe.wait_ge(r_loaded, 16)
            for t in range(NT):
                for c in range(KC):
                    mm = pe.matmul(psum[:, 0, t * 16:t * 16 + NE + 1], sh.x_feat[:, c, t * P:(t + 1) * P], w_r[:, c, :],
                                   start=c == 0, stop=c == KC - 1)
            mm.then_inc(r_mm, 1)
            pe.wait_ge(const, 1)
            for bank in range(4, 8):
                pe.matmul(psum[:, bank, :], sh.ident[:, :], zeros[:, :], start=True, stop=False, skip_group_check=True)
            pe.wait_ge(logit_ready, 1)

            def step(u, j, exists):
                if exists(0):
                    if j % NT == 0:
                        slot = j // NT
                        pe.wait_ge(gu_loaded[slot], 16 // TURN * (u - j) + 16)
                    if exists(2):
                        pe.wait_ge(hid_done, u - 1)
                    t = j % NT
                    for c in range(KC):
                        mm = pe.matmul(psum[:, j % 2, 0:2 * IM], sh.x_feat[:, c, t * P:(t + 1) * P], w_gu[:, j // NT, c, :],
                                       start=c == 0, stop=c == KC - 1)
                    mm.then_inc(gu_mm, 1)
                if exists(1):
                    pe.wait_ge(hid_done, u)
                    if exists(3):
                        pe.wait_ge(ht_read, u - 2)
                    for c in range(IC):
                        mm = pe.transpose(psum[0:IP, 2 + (j - 1) % 2, c * P:(c + 1) * P], hid[:, (j - 1) % 2, c * IP:(c + 1) * IP], sh.ident[:, :])
                    mm.then_inc(ht_mm, 1)
                if exists(2):
                    jj = (j - 2) % TURN
                    t, slot = jj % NT, jj // NT
                    if t == 0:
                        pe.wait_ge(dn_loaded[slot], 16 // TURN * (u - 2 - jj) + 16)
                    pe.wait_ge(ht_read, u - 1)
                    for c in range(IC):
                        mm = pe.matmul(psum[:, 4 + t // 2, (t % 2) * DM:(t % 2 + 1) * DM], hid_f[:, j % 2, c, :], w_dn[:, slot, c, :],
                                       start=False, stop=False, skip_group_check=True)
                    mm.then_inc(dn_mm, 1)
            pipeline(pe, NV * NT, TURN, step, 2)

        @block.scalar
        def _(act):
            act.wait_ge(shifted_done, 1)
            act.activation(shifted[:, :, :], shifted[:, :, :], ACT.Exp).then_inc(r_act, 1)
            act.activation(share[:, :, NE:NV], logit[:, :, NE:NE + 1].broadcast_to([P, NT, NSH]), ACT.Sigmoid).then_inc(r_act, 1)

            def step(u, j, exists):
                if exists(0):
                    act.wait_ge(gu_mm, u + 1)
                    if exists(2):
                        act.wait_ge(hid_done, u - 1)
                    act.activation(silu[:, j % 2, :], psum[:, j % 2, 0:IM], ACT.Silu).then_inc(silu_done, 1)
                if exists(1):
                    act.wait_ge(ht_mm, u)
                    if exists(3):
                        act.wait_ge(dn_mm, u - 2)
                    act.activation(hid_f[:, (j - 1) % 2, :, :].rearrange("p c n -> p (c n)"), psum[0:IP, 2 + (j - 1) % 2, 0:IC * P],
                                   ACT.Copy).then_inc(ht_read, 1)
            pipeline(act, NV * NT, TURN, step, 1)

        @block.vector
        def _(v):
            link = Link(v, v_link)
            wide = lambda ap, n=NE: ap.unsqueeze(2).broadcast_to([P, NT, n])
            v.wait_ge(r_mm, 1)
            v.tensor_copy(logit[:, :, :], psum[:, 0, 0:16 * NT].rearrange("p (t n) -> p t n", t=NT)[:, :, 0:NE + 1]).then_inc(logit_ready, 1)
            v.wait_ge(logit_ready, 1)
            link(v.tensor_reduce(neg_max[:, :], logit[:, :, 0:NE], AX.X, ALU.max, negate=True))
            v.tensor_tensor(shifted[:, :, :], logit[:, :, 0:NE], wide(neg_max[:, :]), ALU.add).then_inc(shifted_done, 1)
            v.wait_ge(r_act, 1)
            link(v.tensor_reduce(total[:, :], shifted[:, :, :], AX.X, ALU.add))
            link(v.reciprocal(total[:, :], total[:, :]))
            link(v.tensor_tensor(prob[:, :, :], shifted[:, :, :], wide(total[:, :]), ALU.mult))
            for t in range(NT):
                link.mark(v.max(top[:, t, :], prob[:, t, :]))
            link.wait()
            for t in range(NT):
                link.mark(v.max_index(top_at[:, t, :], top[:, t, :], prob[:, t, :]))
            link.wait()
            link(v.tensor_copy(top_at_f[:, :, :], top_at[:, :, 0:2]))
            link(v.tensor_tensor(total[:, :], top[:, :, 0], top[:, :, 1], ALU.add))
            link(v.reciprocal(total[:, :], total[:, :]))
            v.wait_ge(const, 3)
            for n, out in enumerate((share[:, :, 0:NE], hit[:, :, :])):
                link(v.tensor_tensor(out, expert_f[:, :].unsqueeze(1).broadcast_to([P, NT, NE]), wide(top_at_f[:, :, n]), ALU.is_equal))
                link(v.tensor_tensor(out, out, wide(top[:, :, n]), ALU.mult))
            link(v.tensor_tensor(share[:, :, 0:NE], share[:, :, 0:NE], hit[:, :, :], ALU.add))
            link(v.tensor_tensor(share[:, :, 0:NE], share[:, :, 0:NE], wide(total[:, :]), ALU.mult))
            v.wait_ge(r_act, 2)

            def step(u, j, exists):
                e = u // NT if isinstance(u, int) else (u - j) // NT + j // NT
                v.wait_ge(silu_done, u + 1)
                if exists(2):
                    v.wait_ge(ht_mm, u - 1)
                v.scalar_tensor_tensor(out=hid[:, j % 2, :], in0=silu[:, j % 2, :], scalar=share[:, j % NT, bass.ds(e, 1)],
                                       in1=psum[:, j % 2, IM:2 * IM], op0=ALU.mult, op1=ALU.mult).then_inc(hid_done, 1)
            pipeline(v, NV * NT, TURN, step, 0)
            v.wait_ge(dn_mm, NV * NT)
            v.sem_inc(norm.y_ready, NT)
            norm.vector(v, add=lambda t: v.tensor_tensor(
                sh.x_tok[:, t, :], sh.x_tok[:, t, :], psum[:, 4 + t // 2, (t % 2) * DM:(t % 2 + 1) * DM], ALU.add))




STAGES = [stage_mamba, stage_token_experts, stage_thought, stage_ssd, stage_attention, stage_moe]


def build(nc, io, out):
    with ExitStack() as ctx:
        sh = Shared(nc, ctx, out.rearrange("b s d -> (b s) d"))
        for stage in STAGES:
            with nc.cleanup_on_exit():
                stage(nc, sh, io)


def chunked(a):
    return np.ascontiguousarray(a.reshape(-1, P, a.shape[-1]).transpose(1, 0, 2))


def lay_out(i):
    g = {}
    x = i["x"].reshape(TOK, DM)
    g["x_tok"] = chunked(x)
    g["x_feat"] = chunked(x.T)
    g["m_w_in"] = chunked(i["L0_attn_W_in"])
    g["m_w_x"] = chunked(i["L0_attn_W_x"])
    g["m_w_dt"] = i["L0_attn_W_dt"]
    g["m_w_out"] = chunked(i["L0_attn_W_out"])
    per = lambda a: chunked(a.reshape(a.shape[0], -1)).reshape(P, -1)
    g["m_small"] = np.concatenate([per(i["L0_attn_" + n]) for n in ("conv_w", "conv_b", "b_dt", "A_log", "D")], axis=1)
    g["ctx_feat"] = i["ctx_2048"].transpose(2, 0, 1).reshape(KC, P, BATCH, SEQ).transpose(1, 0, 2, 3)
    g["token_ids"] = i["itok_BxS_13_99985"].reshape(1, TOK)
    ff = lambda n: i["L0_ffn_" + n]
    g["f_small"] = np.concatenate([per(ff(n)) for n in (
        "in_gamma", "in_beta", "pn_gamma", "pn_beta", "agg_b", "d1_b", "d2_b", "bc_b", "gate_b")], axis=1)
    for n in ("agg_w", "d1_w", "d2_w", "bc_w", "gate_w"):
        g["f_" + n] = chunked(ff(n))
    g["f_out_g"], g["f_out_b"] = ff("out_gamma").reshape(1, DM), ff("out_beta").reshape(1, DM)
    w = i["L1_attn_in_proj_w"].T
    feature_tiles = lambda a: a.reshape(KC, P, -1, P).transpose(2, 1, 0, 3)
    hid_gate = np.stack([feature_tiles(w[:, SI:2 * SI]), feature_tiles(w[:, :SI])], axis=2)
    g["s_w_in"] = hid_gate.reshape(NF, P, 2 * KC * P)
    g["s_w_bc"] = feature_tiles(w[:, 2 * SI:2 * SI + NB * P])
    g["s_w_dt"] = chunked(w[:, 2 * SI + NB * P:])
    g["s_head"] = np.stack([i["L1_attn_dt_bias"], i["L1_attn_A_log"]], axis=1)
    g["s_conv"] = chunked(np.concatenate([i["L1_attn_conv_w"][:, 0, :], i["L1_attn_conv_b"][:, None]], axis=1))
    g["s_norm_w"] = per(i["L1_attn_norm_w"])
    g["s_d"] = i["L1_attn_D"].reshape(1, SH)
    g["s_w_out"] = i["L1_attn_out_proj_w"].T.reshape(NF, P, DM)
    g["r_pos"] = np.concatenate([i["pos_BxS2"], i["itok_BxS_4096_4607"]], axis=1).reshape(BATCH * KT, P).T
    freq = (1.0 / np.float32(10000.0) ** (np.arange(0, HD, 2, dtype=np.float32) / HD)).astype(np.float32)
    g["r_rows"] = np.concatenate([freq, i["L1_xattn_q_norm_w"], i["L1_xattn_k_norm_w"]]).reshape(1, 5 * ROPE)[:, None, :][0]
    xa = lambda n: chunked(i["L1_xattn_" + n].T)
    g["a_w_kv"] = np.concatenate([xa("Wk").reshape(P, KC, KVH, HD), xa("Wv").reshape(P, KC, KVH, HD)], axis=3)
    g["a_w_q"] = xa("Wq").reshape(P, KC, KVH, REP * HD)
    g["a_w_o"] = xa("Wo")
    rows = np.concatenate([i["L1_ffn_router_weight"], i["L1_ffn_shared_gate_w"]], axis=0)
    g["x_w_r"] = chunked(rows.T)
    shared = lambda n: i["L1_ffn_" + n].reshape(NSH, IM, DM)
    gu = np.concatenate([i["L1_ffn_gate_up_proj"],
                         np.concatenate([shared("sh_gate_w"), shared("sh_up_w")], axis=1)], axis=0)
    g["x_w_gu"] = gu.transpose(0, 2, 1).reshape(NV, KC, P, 2 * IM).transpose(0, 2, 1, 3)
    dn = np.concatenate([i["L1_ffn_down_proj"], i["L1_ffn_sh_down_w"].reshape(DM, NSH, IM).transpose(1, 0, 2)], axis=0)
    g["x_w_dn"] = dn.transpose(0, 2, 1).reshape(NV, IC, IP, DM).transpose(0, 2, 1, 3)
    return {name: np.ascontiguousarray(a) for name, a in g.items()}


def kernel(**inputs):
    import concourse.bacc as bacc
    from concourse.bass_utils import run_bass_kernel_spmd

    nc = bacc.Bacc("TRN2", target_bir_lowering=False, num_devices=1)
    arrays = {f"in_{n}": a for n, a in lay_out({n: np.asarray(a) for n, a in inputs.items()}).items()}
    io = {n[3:]: nc.dram_tensor(n, a.shape, mybir.dt.from_np(a.dtype), kind="ExternalInput").ap() for n, a in arrays.items()}
    out = nc.dram_tensor("out", (BATCH, SEQ, DM), F32, kind="ExternalOutput").ap()
    build(nc, io, out)
    return run_bass_kernel_spmd(nc, [arrays], core_ids=[0]).results[0]["out"]
```

```python
from contextlib import ExitStack

import numpy as np
import concourse.bass as bass
from concourse import mybir

F32 = mybir.dt.float32
F32R = mybir.dt.float32r
I32 = mybir.dt.int32
U32 = mybir.dt.uint32
ALU = mybir.AluOpType
ACT = mybir.ActivationFunctionType
AX = mybir.AxisListType

P = 128
BATCH, SEQ, DM = 4, 256, 256
TOK = BATCH * SEQ
NT = TOK // P
KC = DM // P
HALF = TOK // 2
LN_EPS = 1e-5

MI, MS, MR = 512, 16, 128
MC = MI // P
SH, SP, SG, SK, CS = 64, 64, 8, 4, 32
SI = SH * SP
QH, KVH, HD = 16, 4, 128
REP = QH // KVH
NE, IM, ISH = 8, 176, 704
FH = 1024
K_STEPS = 4
VOCAB, NEX = 12500, 4


class Link:

    def __init__(self, eng, sem):
        self.eng, self.sem, self.base, self.n = eng, sem, 0, 0

    def mark(self, ins):
        self.n = self.n + 1
        return ins.then_inc(self.sem, 1)

    def wait(self):
        self.eng.wait_ge(self.sem, self.base + self.n)

    def __call__(self, ins):
        self.mark(ins)
        self.wait()


def wait_beyond_start(eng, sem, n):
    if not (isinstance(n, int) and n == 0):
        eng.wait_ge(sem, n)


NEWTON = 3


def pipeline(eng, count, turn, body, behind):
    for i in range(turn):
        body(i, i, lambda n, i=i: n <= i)
    with eng.Fori(1, count // turn) as r:
        for q in range(turn):
            body(turn * r + q, q, lambda n: True)
    for i in range(count, count + behind):
        body(i, i % turn, lambda n, i=i: i - n < count)


def rsqrt_seed(v, link, out, ve, bits):
    link(v.tensor_scalar(bits.bitcast(I32), ve.bitcast(I32), 1, None, ALU.logical_shift_right))
    link(v.tensor_scalar(out.bitcast(I32), bits.bitcast(I32), -1, 0x5F3759DF, ALU.mult, ALU.add))


def rsqrt_on_vector(v, link, out, var, tmp, eps):
    ve, bits, sq = tmp
    link(v.tensor_scalar(ve, var, eps, None, ALU.add))
    rsqrt_seed(v, link, out, ve, bits)
    for _ in range(NEWTON):
        link(v.tensor_tensor(sq, out, out, ALU.mult))
        link(v.scalar_tensor_tensor(out=bits, in0=sq, scalar=-0.5, in1=ve, op0=ALU.mult, op1=ALU.mult))
        link(v.scalar_tensor_tensor(out=out, in0=bits, scalar=1.5, in1=out, op0=ALU.add, op1=ALU.mult))


def split_products(pe, out, w, x, start, stop, **options):
    (w_hi, w_lo), (x_hi, x_lo) = w, x
    pe.matmul(out, w_hi, x_hi, start=start, stop=False, **options)
    pe.matmul(out, w_hi, x_lo, start=False, stop=False, **options)
    return pe.matmul(out, w_lo, x_hi, start=False, stop=stop, **options)


class Shared:

    def __init__(self, nc, ctx, out):
        sb = lambda name, shape, dt=F32: ctx.enter_context(nc.sbuf_tensor(name, shape, dt))
        self.nc, self.ctx, self.out = nc, ctx, out
        self.x_tok = sb("x_tok", [P, NT, DM])
        self.x_feat = sb("x_feat", [P, KC, TOK])
        self.x_hi, self.x_lo = sb("x_hi", [P, KC, TOK], F32R), sb("x_lo", [P, KC, TOK], F32R)
        self.ctx_feat = sb("ctx_feat", [P, KC, BATCH, SEQ])
        self.ident = sb("ident", [P, P])
        self.ones = sb("ones", [P, P])
        self.stats = sb("stats", [P, NT, 6])
        self.mean_var = sb("mean_var", [P, NT, 2])
        self.rstd = sb("rstd", [P, NT])
        self.rs_tmp = sb("rs_tmp", [P, 3, 64])
        self.psum = ctx.enter_context(nc.psum_tensor("psum", [P, 8, 512], F32))

    def sem(self, name):
        return self.nc.alloc_semaphore(name=name)

    def tmp(self, n, parts=P):
        return [self.rs_tmp[0:parts, k, 0:n] for k in range(3)]


IN_PLACE = "the sum is already in x_tok"


class PostNorm:

    def __init__(self, sh, tag, parts=False, groups=1):
        self.sh, self.parts, self.groups = sh, parts, groups
        self.y_ready = sh.sem(f"{tag}_y_ready")
        self.link = sh.sem(f"{tag}_norm_link")
        self.normed = sh.sem(f"{tag}_normed")
        self.turned = sh.sem(f"{tag}_turned")
        self.x_feat_ready = sh.sem(f"{tag}_x_feat")
        self.hi_ready, self.lo_ready = sh.sem(f"{tag}_x_hi"), sh.sem(f"{tag}_x_lo")

    def vector(self, v, add=None):
        sh = self.sh
        link = Link(v, self.link)
        n = NT // self.groups
        for first in range(0, NT, n):
            for t in range(first, first + n):
                v.wait_ge(self.y_ready, t + 1)
                x = sh.x_tok[:, t, :]
                if add is not IN_PLACE:
                    link.mark(add(t) if add else v.tensor_tensor(x, x, sh.psum[:, t, 0:DM], ALU.add))
                if t > first:
                    if add is not IN_PLACE:
                        v.wait_ge(self.link, link.n - 1)
                    link.mark(v.bn_stats(sh.stats[:, t - 1, :], sh.x_tok[:, t - 1, :]))
            if add is not IN_PLACE:
                link.wait()
            link(v.bn_stats(sh.stats[:, t, :], sh.x_tok[:, t, :]))
            for t in range(first, first + n):
                link.mark(v.bn_aggr(sh.mean_var[:, t, :], sh.stats[:, t, :]))
            link.wait()
            rsqrt_on_vector(v, link, sh.rstd[:, first:first + n], sh.mean_var[:, first:first + n, 1], sh.tmp(n), LN_EPS)
            for t in range(first, first + n):
                x = sh.x_tok[:, t, :]
                v.tensor_scalar(x, x, sh.mean_var[:, t, 0:1], sh.rstd[:, t:t + 1], ALU.subtract,
                                ALU.mult).then_inc(self.normed, 1)
        for t in range(NT if self.parts else 0):
            part = (slice(None), slice(None), slice(t * P, (t + 1) * P))
            v.wait_ge(self.x_feat_ready, t + 1)
            v.tensor_copy(sh.x_hi[part], sh.x_feat[part]).then_inc(self.hi_ready, 1)

    def gpsimd(self, pool):
        sh = self.sh
        for t in range(NT):
            part = (slice(None), slice(None), slice(t * P, (t + 1) * P))
            pool.wait_ge(self.hi_ready, t + 1)
            pool.tensor_tensor(sh.x_lo[part], sh.x_feat[part], sh.x_hi[part], ALU.subtract).then_inc(self.lo_ready, 1)

    def tensor(self, pe):
        sh = self.sh
        for t in range(NT):
            pe.wait_ge(self.normed, t + 1)
            for c in range(KC):
                mm = pe.transpose(sh.psum[:, t, DM + c * P:DM + (c + 1) * P],
                                  sh.x_tok[:, t, c * P:(c + 1) * P], sh.ident[:, :])
            mm.then_inc(self.turned, 1)

    def scalar(self, act):
        sh = self.sh
        for t in range(NT):
            act.wait_ge(self.turned, t + 1)
            act.activation(sh.x_feat[:, :, t * P:(t + 1) * P],
                           sh.psum[:, t, DM:2 * DM].rearrange("p (c n) -> p c n", c=KC),
                           ACT.Copy).then_inc(self.x_feat_ready, 1)


SM_COLS = dict(conv_w=MC * 3, conv_b=MC, b_dt=MC, a_log=MC * MS, d=MC)


def columns(table):
    at, out = 0, {}
    for name, n in table.items():
        out[name] = slice(at, at + n)
        at += n
    return out, at


def stage_mamba(nc, sh, io):
    with ExitStack() as ctx:
        def sb(name, shape, dt=F32):
            return ctx.enter_context(nc.sbuf_tensor(name, shape, dt))

        col, n_small = columns(SM_COLS)
        w_in = sb("m_w_in", [P, KC, 2 * MI])
        w_x = sb("m_w_x", [P, MC, MR + 2 * MS])
        w_dt = sb("m_w_dt", [P, MI])
        w_out = sb("m_w_out", [P, MC, DM])
        small = sb("m_small", [P, n_small])
        neg_a = sb("m_a", [P, MC, MS])
        diag_d = sb("m_diag_d", [P, MC, P])
        u = sb("m_u", [P, MC, TOK])
        gate = sb("m_gate", [P, MC, TOK])
        dt = sb("m_dt", [P, MC, TOK])
        dtu = sb("m_dtu", [P, MC, TOK])
        acc = sb("m_acc", [P, 2, 512])
        dt_in = dtu[:, 0, :]
        bc = sb("m_bc", [2 * MS, TOK])
        decay = sb("m_decay", [P, 2, MC, 2, SEQ])
        drive = sb("m_drive", [P, 2, MC, HALF])
        state = sb("m_state", [P, 2, MC, HALF])
        read = sb("m_read", [P, 2, MC, HALF])
        soft = read[:, :, :, :].rearrange("p a m n -> p (a m n)").rearrange("p (m n) -> p m n", m=MC)
        b_all = sb("m_b_all", [P, 2, HALF])
        c_all = sb("m_c_all", [P, 2, HALF])
        bc_dram = nc.dram_tensor("m_bc_dram", [2 * MS, TOK], F32, kind="Internal").ap()

        s = sh.sem
        w_loaded, wx_loaded = s("m_w_loaded"), s("m_wx_loaded")
        const_made = s("m_const_made")
        proj_done, acc_made, conv_done, u_done, gate_done = (s("m_" + n) for n in (
            "proj_done", "acc_made", "conv_done", "u_done", "gate_done"))
        z_done, z_taken, z_copied = s("m_z_done"), s("m_z_taken"), s("m_z_copied")
        minus_abs = s("m_minus_abs")
        xdbl_done, dt_in_ready, bc_ready, bc_stored = (s("m_" + n) for n in (
            "xdbl_done", "dt_in_ready", "bc_ready", "bc_stored"))
        dtmm_done, sp_act, sp_log, dt_ready, dtu_ready = (s("m_" + n) for n in (
            "dtmm_done", "sp_act", "sp_log", "dt_ready", "dtu_ready"))
        b_loaded = [s(f"m_b_loaded{slot}") for slot in range(2)]
        c_loaded = [s(f"m_c_loaded{slot}") for slot in range(2)]
        decay_ready, drive_ready, scan_done, read_ready, summed = (s("m_" + n) for n in (
            "decay_ready", "drive_ready", "scan_done", "read_ready", "summed"))
        y_gated, v_link, a_link = s("m_y_gated"), s("m_v_link"), s("m_a_link")
        norm = PostNorm(sh, "m", groups=2)
        psum = sh.psum

        halves = [(m, h) for m in range(MC) for h in range(2)]
        block = ctx.enter_context(nc.Block())

        @block.sync
        def _(sp):
            sp.dma_start(sh.x_feat[:, :, :], io["x_feat"]).then_inc(w_loaded, 16)
            sp.dma_start(w_in[:, :, :], io["m_w_in"]).then_inc(w_loaded, 16)
            sp.dma_start(small[:, :], io["m_small"]).then_inc(w_loaded, 16)
            sp.dma_start(w_x[:, :, :], io["m_w_x"]).then_inc(wx_loaded, 16)
            sp.dma_start(w_dt[:, :], io["m_w_dt"]).then_inc(wx_loaded, 16)
            sp.dma_start(w_out[:, :, :], io["m_w_out"]).then_inc(wx_loaded, 16)
            sp.dma_start(sh.x_tok[:, :, :], io["x_tok"]).then_inc(wx_loaded, 16)
            sp.dma_start(sh.ctx_feat[:, :, :, :], io["ctx_feat"]).then_inc(wx_loaded, 16)
            sp.wait_ge(bc_ready, 2)
            sp.dma_start(bc_dram, bc[:, :]).then_inc(bc_stored, 16)
            sp.wait_ge(bc_stored, 16)

            def load_b(h, n, slot):
                sp.wait_ge(drive_ready, h * MS + n + 1)
                sp.dma_start(b_all[:, slot, :], bc_dram[bass.ds(n, 1), h * HALF:(h + 1) * HALF]
                             .partition_broadcast(P).rearrange("p a n -> p (a n)")).then_inc(b_loaded[slot], 16)

            def load_c(h, n, slot):
                sp.wait_ge(read_ready, h * MS + n + 1)
                sp.dma_start(c_all[:, slot, :], bc_dram[bass.ds(MS + n, 1), h * HALF:(h + 1) * HALF]
                             .partition_broadcast(P).rearrange("p a n -> p (a n)")).then_inc(c_loaded[slot], 16)

            load_b(0, 0, 0)
            for h in range(2):
                with sp.Fori(0, MS // 2 - 1) as r:
                    load_b(h, 2 * r + 1, 1)
                    load_c(h, 2 * r, 0)
                    load_b(h, 2 * r + 2, 0)
                    load_c(h, 2 * r + 1, 1)
                load_b(h, MS - 1, 1)
                load_c(h, MS - 2, 0)
                if h == 0:
                    load_b(1, 0, 0)
                load_c(h, MS - 1, 1)

        @block.gpsimd
        def _(pool):
            pool.memset(sh.ones[:, :], 1.0).then_inc(const_made, 1)
            pool.memset(sh.ident[:, :], 0.0).then_inc(const_made, 1)
            pool.memset(decay[:, :, :, :, 0:1], 0.0).then_inc(const_made, 1)
            pool.wait_ge(const_made, 3)
            pool.affine_select(out=sh.ident[:, :], in_=sh.ident[:, :], compare_op=ALU.not_equal, fill=1.0,
                               base=0, pattern=[[-1, P]], channel_multiplier=1).then_inc(const_made, 1)
            pool.sem_inc(drive_ready, 2)
            for h in range(2):
                pool.wait_ge(dtu_ready, h + 1)
                with pool.Fori(0, MS // 2) as r:
                    for slot in range(2):
                        n = h * MS + 2 * r + slot
                        pool.wait_ge(b_loaded[slot], 16 * (h * (MS // 2) + r) + 16)
                        pool.wait_ge(scan_done, n + 1)
                        pool.tensor_tensor(drive[:, slot, :, :], dtu[:, :, h * HALF:(h + 1) * HALF],
                                           b_all[:, slot, :].unsqueeze(1).broadcast_to([P, MC, HALF]),
                                           ALU.mult).then_inc(drive_ready, 1)

        @block.tensor
        def _(pe):
            pe.wait_ge(w_loaded, 48)

            def project(m, h, bank):
                for k in range(KC):
                    mm = pe.matmul(psum[:, bank, :], w_in[:, k, m * P:(m + 1) * P],
                                   sh.x_feat[:, k, h * HALF:(h + 1) * HALF], start=k == 0, stop=k == KC - 1)
                return mm

            for j, (m, h) in enumerate(halves):
                if j >= 4:
                    pe.wait_ge(conv_done, j - 3)
                project(m, h, j % 4).then_inc(proj_done, 1)
            pe.wait_ge(wx_loaded, 80)
            pe.wait_ge(u_done, 2 * MC)
            for h in range(2):
                for rows, bank in ((slice(0, MR), 4 + h), (slice(MR, MR + 2 * MS), 6 + h)):
                    for k in range(MC):
                        mm = pe.matmul(psum[0:rows.stop - rows.start, bank, :], w_x[:, k, rows],
                                       u[:, k, h * HALF:(h + 1) * HALF], start=k == 0, stop=k == MC - 1)
                    mm.then_inc(xdbl_done, 1)
            for h in range(2):
                for m in range(MC):
                    j = h * MC + m
                    pe.wait_ge(dt_in_ready, h + 1)
                    if j >= 4:
                        pe.wait_ge(sp_act, j - 3)
                    pe.matmul(psum[:, j % 4, :], w_dt[:, m * P:(m + 1) * P],
                              dt_in[:, h * HALF:(h + 1) * HALF], start=True, stop=True).then_inc(dtmm_done, 1)
            pe.wait_ge(bc_ready, 2)
            for h in range(2):
                for m in range(MC):
                    if h:
                        pe.wait_ge(z_taken, m + 1)
                    project(MC + m, h, 4 + m).then_inc(z_done, 1)
            pe.wait_ge(const_made, 4 + MC)
            pe.wait_ge(sp_act, 2 * MC)
            for h in range(2):
                if h:
                    pe.wait_ge(z_copied, MC)
                for m in range(MC):
                    pe.matmul(psum[:, 4 * h + m, :], diag_d[:, m, :], u[:, m, h * HALF:(h + 1) * HALF],
                              start=True, stop=False, skip_group_check=True)
                with pe.Fori(0, MS // 2) as r:
                    for slot in range(2):
                        n = h * MS + 2 * r + slot
                        pe.wait_ge(read_ready, n + 3)
                        for m in range(MC):
                            mm = pe.matmul(psum[:, 4 * h + m, :], sh.ident[:, :], read[:, slot, m, :],
                                           start=False, stop=False, skip_group_check=True)
                        mm.then_inc(summed, 1)
            for t in range(NT):
                pe.wait_ge(y_gated, 4 * (t // 4 + 1))
                if t == 0:
                    pe.wait_ge(y_gated, 4)
                for k in range(MC):
                    mm = pe.matmul(psum[:, t, 0:DM], gate[:, k, t * P:(t + 1) * P], w_out[:, k, :],
                                   start=k == 0, stop=k == MC - 1)
                mm.then_inc(norm.y_ready, 1)
            norm.tensor(pe)

        @block.scalar
        def _(act):
            act.wait_ge(w_loaded, 48)
            link = Link(act, a_link)

            def silu_u(j):
                m, h = j // 2, j % 2
                act.wait_ge(conv_done, j + 1)
                act.activation(u[:, m, h * HALF:(h + 1) * HALF], acc[:, j % 2, :], ACT.Silu).then_inc(u_done, 1)

            for j, (m, h) in enumerate(halves):
                act.wait_ge(proj_done, j + 1)
                if j >= 2:
                    act.wait_ge(u_done, j - 1)
                act.activation(acc[:, j % 2, :], psum[:, j % 4, :], ACT.Identity, bias=small[:, col["conv_b"]][:, m:m + 1],
                               scale=small[:, col["conv_w"]][:, 3 * m + 1:3 * m + 2]).then_inc(acc_made, 1)
                if j:
                    silu_u(j - 1)
            silu_u(2 * MC - 1)
            link(act.activation(neg_a[:, :, :].rearrange("p a b -> p (a b)"), small[:, col["a_log"]], ACT.Exp))
            link(act.mul(neg_a[:, :, :].rearrange("p a b -> p (a b)"), neg_a[:, :, :].rearrange("p a b -> p (a b)"), -1.0))
            for h in range(2):
                for m in range(MC):
                    j = h * MC + m
                    act.wait_ge(dtmm_done, j + 1)
                    act.activation(dt[:, m, h * HALF:(h + 1) * HALF], psum[:, j % 4, :], ACT.Identity,
                                   bias=small[:, col["b_dt"]][:, m:m + 1]).then_inc(sp_act, 1)
            own = [slice(h * HALF, (h + 1) * HALF) for h in range(2)]
            for h in range(2):
                act.wait_ge(minus_abs, h + 1)
                link(act.activation(soft[:, :, own[h]], soft[:, :, own[h]], ACT.Exp))
            for h in range(2):
                act.activation(soft[:, :, own[h]], soft[:, :, own[h]], ACT.Ln, bias=1.0).then_inc(sp_log, 1)
            for m in range(MC):
                act.wait_ge(z_done, MC + m + 1)
                act.activation(gate[:, m, own[1]], psum[:, 4 + m, :], ACT.Identity).then_inc(z_copied, 1)
            for h in range(2):
                act.wait_ge(dt_ready, h + 1)
                with act.Fori(0, MS // 4) as r:
                    for q in range(4):
                        n, slot = h * MS + 4 * r + q, q % 2
                        act.wait_ge(scan_done, n + 1)
                        for m in range(MC):
                            a = act.activation(decay[:, slot, m, :, 1:SEQ],
                                               dt[:, m, h * HALF:(h + 1) * HALF].rearrange("p (b s) -> p b s", b=2)[:, :, 1:SEQ],
                                               ACT.Exp, scale=neg_a[:, m, bass.ds(4 * r + q, 1)])
                        a.then_inc(decay_ready, 1)
                if h:
                    act.wait_ge(z_copied, MC)
                else:
                    act.wait_ge(z_taken, MC)
                act.activation(gate[:, :, own[h]], gate[:, :, own[h]], ACT.Silu).then_inc(gate_done, 1)
            norm.scalar(act)

        @block.vector
        def _(v):
            link = Link(v, v_link)
            v.sem_inc(summed, 2)
            v.sem_inc(scan_done, 2)
            v.sem_inc(read_ready, 2)
            v.wait_ge(w_loaded, 48)
            for j, (m, h) in enumerate(halves):
                v.wait_ge(acc_made, j + 1)
                a = acc[:, j % 2, :].rearrange("p (b s) -> p b s", b=2)
                x = psum[:, j % 4, :].rearrange("p (b s) -> p b s", b=2)
                w = small[:, col["conv_w"]]
                link(v.scalar_tensor_tensor(out=a[:, :, 1:SEQ], in0=x[:, :, 0:SEQ - 1], scalar=w[:, 3 * m:3 * m + 1],
                                            in1=a[:, :, 1:SEQ], op0=ALU.mult, op1=ALU.add))
                v.scalar_tensor_tensor(out=a[:, :, 0:SEQ - 1], in0=x[:, :, 1:SEQ], scalar=w[:, 3 * m + 2:3 * m + 3],
                                       in1=a[:, :, 0:SEQ - 1], op0=ALU.mult, op1=ALU.add).then_inc(conv_done, 1)
            v.wait_ge(const_made, 4)
            for m in range(MC):
                v.tensor_scalar(diag_d[:, m, :], sh.ident[:, :], small[:, col["d"]][:, m:m + 1], None,
                                ALU.mult).then_inc(const_made, 1)
            for h in range(2):
                v.wait_ge(xdbl_done, 2 * h + 2)
                v.tensor_copy(dt_in[:, h * HALF:(h + 1) * HALF], psum[:, 4 + h, :]).then_inc(dt_in_ready, 1)
                v.tensor_copy(bc[:, h * HALF:(h + 1) * HALF], psum[0:2 * MS, 6 + h, :]).then_inc(bc_ready, 1)
            for h in range(2):
                d = dt[:, :, h * HALF:(h + 1) * HALF]
                v.wait_ge(sp_act, MC * (h + 1))
                v.scalar_tensor_tensor(out=soft[:, :, h * HALF:(h + 1) * HALF], in0=d, scalar=-1.0, in1=d,
                                       op0=ALU.mult, op1=ALU.min).then_inc(minus_abs, 1)
            for m in range(MC):
                v.wait_ge(z_done, m + 1)
                v.tensor_copy(gate[:, m, 0:HALF], psum[:, 4 + m, :]).then_inc(z_taken, 1)
            v.wait_ge(dtmm_done, 2 * MC)
            for h in range(2):
                own = slice(h * HALF, (h + 1) * HALF)
                d = dt[:, :, own]
                v.wait_ge(sp_log, h + 1)
                v.scalar_tensor_tensor(out=d, in0=d, scalar=0.0, in1=soft[:, :, own], op0=ALU.max, op1=ALU.add).then_inc(dt_ready, 1)
                v.wait_ge(dt_ready, h + 1)
                v.tensor_tensor(dtu[:, :, own], d, u[:, :, own], ALU.mult).then_inc(dtu_ready, 1)
            flat = lambda ap: ap.rearrange("p m n -> p (m n)")

            def scan(n, slot):
                v.wait_ge(decay_ready, n + 1)
                v.wait_ge(drive_ready, n + 3)
                v.wait_ge(read_ready, n + 1)
                v.tensor_tensor_scan(flat(state[:, slot, :, :]), decay[:, slot, :, :, :].rearrange("p m b s -> p (m b s)"),
                                     flat(drive[:, slot, :, :]), 0.0, ALU.mult, ALU.add).then_inc(scan_done, 1)

            def read_out(n, slot, pair):
                v.wait_ge(scan_done, n + 3)
                v.wait_ge(c_loaded[slot], 16 * pair + 16)
                v.wait_ge(summed, n + 1)
                v.tensor_tensor(read[:, slot, :, :], state[:, slot, :, :],
                                c_all[:, slot, :].unsqueeze(1).broadcast_to([P, MC, HALF]),
                                ALU.mult).then_inc(read_ready, 1)

            for h in range(2):
                scan(h * MS, 0)
                with v.Fori(0, MS // 2 - 1) as r:
                    n = h * MS + 2 * r
                    scan(n + 1, 1)
                    read_out(n, 0, h * (MS // 2) + r)
                    scan(n + 2, 0)
                    read_out(n + 1, 1, h * (MS // 2) + r)
                n = h * MS + MS - 2
                scan(n + 1, 1)
                for slot in range(2):
                    read_out(n + slot, slot, n // 2)
            for h in range(2):
                v.wait_ge(summed, 2 + MS * (h + 1))
                v.wait_ge(gate_done, h + 1)
                for m in range(MC):
                    g = gate[:, m, h * HALF:(h + 1) * HALF]
                    v.tensor_tensor(g, g, psum[:, 4 * h + m, :], ALU.mult).then_inc(y_gated, 1)
            norm.vector(v)


ROPE = HD // 2
KT = 2 * SEQ // P
QT = SEQ // P
TWO_PI = 6.283185307179586
PI_1 = 6.28125
PI_2 = 0.0019350051879882812
PI_3 = TWO_PI - PI_1 - PI_2
ROUND = 12582912.0
PI_F = 3.1415925


class Rope:

    def __init__(self, sh):
        ntab = BATCH * KT
        keep = lambda name, n: sh.ctx.enter_context(sh.nc.sbuf_tensor(name, [P, n, 2, ROPE], F32))
        self.k = keep("r_k_cos", ntab), keep("r_k_sin", ntab)
        self.q = keep("r_q_cos", BATCH * QT), keep("r_q_sin", BATCH * QT)

    def scratch(self, sh, sb):
        ntab = BATCH * KT
        self.ntab = ntab
        self.pos, self.pos_f = sb("r_pos", [P, ntab], I32), sb("r_pos_f", [P, ntab])
        self.rows = sb("r_rows", [P, 5, ROPE])
        self.minus = sb("r_minus", [P, 2, ROPE])
        self.arg, self.cyc, self.rem = (sb("r_" + n, [P, ntab, ROPE]) for n in ("arg", "cyc", "rem"))
        self.loaded, self.reduced, self.looked_up, self.minus_made, self.made = (sh.sem("r_" + n) for n in (
            "loaded", "reduced", "looked_up", "minus_made", "made"))

    def load(self, sp, io):
        sp.dma_start(self.pos[:, :], io["r_pos"]).then_inc(self.loaded, 16)
        sp.dma_start(self.rows[:, :, :].rearrange("p a n -> p (a n)"), io["r_rows"].partition_broadcast(P).rearrange("p a n -> p (a n)")).then_inc(self.loaded, 16)

    def reduce(self, v, link, cosine):
        arg, cyc, pos_f = self.arg, self.cyc, self.pos_f
        out, shift = (arg, 0.25) if cosine else (self.rem, 0.0)
        shape = [P, self.ntab, ROPE]
        if not cosine:
            v.wait_ge(self.loaded, 32)
            v.tensor_scalar(self.minus[:, :, :], self.rows[:, 2:5:2, :], -1.0, None, ALU.mult).then_inc(self.minus_made, 1)
            link(v.tensor_copy(pos_f[:, :], self.pos[:, :]))
            link(v.tensor_tensor(arg[:, :, :], pos_f[:, :].unsqueeze(2).broadcast_to(shape),
                                 self.rows[:, 0, :].unsqueeze(1).broadcast_to(shape), ALU.mult))
        link(v.tensor_scalar(cyc[:, :, :], arg[:, :, :], 1.0 / TWO_PI, shift, ALU.mult, ALU.add))
        link(v.tensor_scalar(cyc[:, :, :], cyc[:, :, :], ROUND, ROUND, ALU.add, ALU.subtract))
        link(v.scalar_tensor_tensor(out=out[:, :, :], in0=cyc[:, :, :], scalar=-PI_1, in1=arg[:, :, :], op0=ALU.mult, op1=ALU.add))
        link(v.scalar_tensor_tensor(out=out[:, :, :], in0=cyc[:, :, :], scalar=-PI_2, in1=out[:, :, :], op0=ALU.mult, op1=ALU.add))
        link(v.scalar_tensor_tensor(out=out[:, :, :], in0=cyc[:, :, :], scalar=-PI_3, in1=out[:, :, :], op0=ALU.mult, op1=ALU.add))
        if cosine:
            link(v.tensor_scalar(out[:, :, :], out[:, :, :], TWO_PI / 4, None, ALU.add))
        v.tensor_scalar(out[:, :, :], out[:, :, :], PI_F, -PI_F, ALU.min, ALU.max).then_inc(self.reduced, 1)

    def look_up(self, act, cosine):
        act.wait_ge(self.reduced, 2 if cosine else 1)
        angle = self.arg if cosine else self.rem
        act.activation(angle[:, :, :], angle[:, :, :], ACT.Sin).then_inc(self.looked_up, 1)

    def tables(self, pool):
        pool.wait_ge(self.minus_made, 1)
        for source, cosine in ((self.rem, False), (self.arg, True)):
            pool.wait_ge(self.looked_up, 1 + cosine)
            for which, (c_tab, s_tab) in enumerate((self.q, self.k)):
                w = self.rows[:, 1 + 2 * which:3 + 2 * which, :]
                for half in range(2):
                    row = w[:, half, :] if cosine else (w[:, 0, :] if half else self.minus[:, which, :])
                    tab = (c_tab if cosine else s_tab)[:, :, half, :]
                    src, row = source[:, :, :], row.unsqueeze(1)
                    if which == 0:
                        src = src.rearrange("p (b t) n -> p b t n", b=BATCH)[:, :, KT - QT:KT, :]
                        tab, row = tab.rearrange("p (b t) n -> p b t n", b=BATCH), row.unsqueeze(1)
                    pool.tensor_tensor(tab, src, row.broadcast_to(src.shape), ALU.mult).then_inc(self.made, 1)
        pool.wait_ge(self.made, 8)


FF_COLS = dict(in_g=KC, in_b=KC, pn_g=KC, pn_b=KC, agg_b=KC, d1_b=FH // P, d2_b=KC, bc_b=KC, gate_b=KC)


class Ahead:

    def __init__(self, sh):
        self.ctx = ExitStack()
        self.sb = lambda name, shape, dt=F32: self.ctx.enter_context(sh.nc.sbuf_tensor(name, shape, dt))


def thought_weights(sh):
    w, hc = Ahead(sh), FH // P
    w.col, n_small = columns(FF_COLS)
    w.small = w.sb("f_small", [P, n_small])
    w.weights = ([w.sb("f_" + n, [P, KC, DM]) for n in ("agg_w", "bc_w", "gate_w")] +
                 [w.sb("f_d1_w", [P, KC, FH]), w.sb("f_d2_w", [P, hc, DM]), w.sb("f_out_g", [P, DM]), w.sb("f_out_b", [P, DM])])
    return w


def ssd_weights(sh):
    w = Ahead(sh)
    w.conv = w.sb("s_conv", [P, NF + NB, SK + 1])
    w.norm_w = w.sb("s_norm_w", [P, NF])
    w.w_dt, w.head = w.sb("s_w_dt", [P, KC, SH]), w.sb("s_head", [SH, 2])
    w.d_all = w.sb("s_d_all", [P, SH])
    return w


def load_ahead(sp, sh, io, loaded):
    t, k = sh.thought, sh.ssd
    loads = [(t.small[:, :], io["f_small"])]
    for n, tile in zip(("agg_w", "bc_w", "gate_w", "d1_w", "d2_w"), t.weights):
        loads.append((tile[:, :, :], io["f_" + n]))
    across = lambda ap: ap.partition_broadcast(P).rearrange("p a n -> p (a n)")
    loads += [(t.weights[5][:, :], across(io["f_out_g"])), (t.weights[6][:, :], across(io["f_out_b"])),
              (k.w_dt[:, :, :], io["s_w_dt"]), (k.head[:, :], io["s_head"]), (k.conv[:, :, :], io["s_conv"]),
              (k.norm_w[:, :], io["s_norm_w"]), (k.d_all[:, :], across(io["s_d"]))]
    for tile, source in loads:
        sp.dma_start(tile, source).then_inc(loaded, 16)
    return 16 * len(loads)


def stage_token_experts(nc, sh, io):
    PER_EXPERT = VOCAB // NEX
    FC = SEQ // P
    rope = sh.rope = Rope(sh)
    sh.in_turn = sh.ctx.enter_context(nc.sbuf_tensor("in_turn", [P, 4096], F32))
    sh.ssd, sh.thought = ssd_weights(sh), thought_weights(sh)
    with ExitStack() as ctx:
        def sb(name, shape, dt=F32):
            return ctx.enter_context(nc.sbuf_tensor(name, shape, dt))

        rope.scratch(sh, sb)
        ids = sb("e_ids", [P, TOK], I32)
        at_least = sb("e_at_least", [P, NEX - 1, TOK])
        mask = sb("e_mask", [P, NEX, TOK])
        x_own = sb("e_x_own", [P, 2, KC, TOK])
        silu = sb("e_silu", [P, 2, HALF])
        hid = sb("e_hid", [P, NEX * FC, TOK])
        s = sh.sem
        mask_ready, own_ready, v_link = s("e_mask_ready"), s("e_own_ready"), s("e_v_link")
        ids_loaded, ahead_loaded = s("e_ids_loaded"), s("e_ahead_loaded")
        pre_done, silu_done, hid_done = s("e_pre_done"), s("e_silu_done"), s("e_hid_done")
        norm = PostNorm(sh, "e", groups=2)
        psum, ctxw = sh.psum, sh.ctx_feat
        steps = [(e, f, h) for e in range(NEX) for f in range(FC) for h in range(2)]
        block = ctx.enter_context(nc.Block())

        @block.sync
        def _(sp):
            sp.dma_start(ids[:, :], io["token_ids"].partition_broadcast(P).rearrange("p a n -> p (a n)")).then_inc(ids_loaded, 16)
            rope.load(sp, io)
            sp.wait_ge(ahead_loaded, load_ahead(sp, sh, io, ahead_loaded))

        @block.gpsimd
        def _(pool):
            for e in range(1, NEX):
                pool.wait_ge(mask_ready, e + 1)
                if e >= 2:
                    pool.wait_ge(pre_done, 2 * FC * (e - 1))
                pool.tensor_tensor(x_own[:, e % 2, :, :], sh.x_feat[:, :, :],
                                   mask[:, e, :].unsqueeze(1).broadcast_to([P, KC, TOK]), ALU.mult).then_inc(own_ready, 1)
            rope.tables(pool)

        @block.tensor
        def _(pe):
            for j, (e, f, h) in enumerate(steps):
                pe.wait_ge(own_ready, e + 1)
                if j >= 4:
                    pe.wait_ge(hid_done, j - 3)
                for k in range(KC):
                    mm = pe.matmul(psum[:, j % 4, :], ctxw[:, k, e, f * P:(f + 1) * P],
                                   x_own[:, e % 2, k, h * HALF:(h + 1) * HALF], start=k == 0, stop=k == KC - 1)
                mm.then_inc(pre_done, 1)
            pe.wait_ge(hid_done, len(steps))
            for t in range(NT):
                for j in range(NEX * FC):
                    mm = pe.matmul(psum[:, t, 0:DM], hid[:, j, t * P:(t + 1) * P], ctxw[:, j % FC, j // FC, :],
                                   start=j == 0, stop=j == NEX * FC - 1)
                mm.then_inc(norm.y_ready, 1)
            norm.tensor(pe)

        @block.scalar
        def _(act):
            for j in range(len(steps)):
                act.wait_ge(pre_done, j + 1)
                if j >= 2:
                    act.wait_ge(hid_done, j - 1)
                act.activation(silu[:, j % 2, :], psum[:, j % 4, :], ACT.Silu).then_inc(silu_done, 1)
            rope.look_up(act, False)
            rope.look_up(act, True)
            norm.scalar(act)

        @block.vector
        def _(v):
            link = Link(v, v_link)
            v.wait_ge(ids_loaded, 16)
            v.tensor_scalar(mask[:, 0, :], ids[:, :], float(PER_EXPERT), None, ALU.is_lt).then_inc(mask_ready, 1)
            v.wait_ge(mask_ready, 1)
            v.tensor_tensor(x_own[:, 0, :, :], sh.x_feat[:, :, :], mask[:, 0, :].unsqueeze(1).broadcast_to([P, KC, TOK]),
                            ALU.mult).then_inc(own_ready, 1)
            for e in range(1, NEX):
                link.mark(v.tensor_scalar(at_least[:, e - 1, :], ids[:, :], float(PER_EXPERT * e), None, ALU.is_ge))
            link.wait()
            for e in range(1, NEX - 1):
                v.tensor_tensor(mask[:, e, :], at_least[:, e - 1, :], at_least[:, e, :], ALU.subtract).then_inc(mask_ready, 1)
            v.tensor_copy(mask[:, NEX - 1, :], at_least[:, NEX - 2, :]).then_inc(mask_ready, 1)
            for j, (e, f, h) in enumerate(steps):
                v.wait_ge(silu_done, j + 1)
                v.tensor_tensor(hid[:, e * FC + f, h * HALF:(h + 1) * HALF], silu[:, j % 2, :], psum[:, j % 4, :],
                                ALU.mult).then_inc(hid_done, 1)
                if j in (4, 9):
                    rope.reduce(v, link, j == 9)
            norm.vector(v)




def stage_thought(nc, sh, io):
    HC = FH // P
    with sh.thought.ctx as ctx:
        def sb(name, shape, dt=F32):
            return ctx.enter_context(nc.sbuf_tensor(name, shape, dt))

        col, small = sh.thought.col, sh.thought.small
        agg_w, bc_w, gate_w, d1_w, d2_w, out_g, out_b = sh.thought.weights
        gate = sb("f_gate", [P, KC, TOK])
        mixed = sb("f_mixed", [P, KC, TOK])
        on_tok = sb("f_on_tok", [P, NT, DM])
        thought = sb("f_thought", [P, KC, BATCH])
        cen, sq, nrm = (sb("f_" + n, [P, KC, BATCH]) for n in ("cen", "sq", "nrm"))
        rs = sb("f_rs", [P, BATCH])
        var = sb("f_var", [P, BATCH])
        pre, hid = sb("f_pre", [P, HC, BATCH]), sb("f_hid", [P, HC, BATCH])
        bcast = sb("f_bcast", [P, KC, BATCH])
        s = sh.sem
        v_link, v_done, pe_done, act_done = (s("f_" + n) for n in ("v_link", "v_done", "pe_done", "act_done"))
        gate_mm, gate_ready, mixed_ready, tok_ready, beta_added = (s("f_" + n) for n in (
            "gate_mm", "gate_ready", "mixed_ready", "tok_ready", "beta_added"))
        norm = PostNorm(sh, "f", parts=True)
        psum = sh.psum
        last = sh.x_feat[:, :, SEQ - 1:TOK:SEQ]
        block = ctx.enter_context(nc.Block())

        @block.gpsimd
        def _(pool):
            for t in range(NT):
                pool.tensor_tensor(sh.x_tok[:, t, :], sh.x_tok[:, t, :], out_b[:, :], ALU.add).then_inc(beta_added, 1)
            norm.gpsimd(pool)

        @block.tensor
        def _(pe):
            count = [0]

            def after_vector():
                count[0] += 1
                pe.wait_ge(v_done, count[0])

            def sums(src):
                for c in range(KC):
                    mm = pe.matmul(psum[:, 0, 0:BATCH], sh.ones[:, :], src[:, c, :], start=c == 0, stop=c == KC - 1)
                mm.then_inc(pe_done, 1)

            def product(bank, w, src, n_out, n_in):
                for m in range(n_out):
                    for k in range(n_in):
                        mm = pe.matmul(psum[:, bank, m * BATCH:(m + 1) * BATCH], w[:, k, m * P:(m + 1) * P], src[:, k, :],
                                       start=k == 0, stop=k == n_in - 1)
                mm.then_inc(pe_done, 1)

            sums(last)
            after_vector()
            sums(sq)
            after_vector()
            product(1, agg_w, nrm, KC, KC)
            for m in range(KC):
                for h in range(2):
                    for k in range(KC):
                        mm = pe.matmul(psum[:, 4 + 2 * m + h, :], gate_w[:, k, m * P:(m + 1) * P],
                                       sh.x_feat[:, k, h * HALF:(h + 1) * HALF], start=k == 0, stop=k == KC - 1)
                    mm.then_inc(gate_mm, 1)
            for i in range(K_STEPS):
                after_vector()
                sums(thought)
                after_vector()
                sums(sq)
                after_vector()
                product(1, d1_w, nrm, HC, KC)
                count[0] += 1
                pe.wait_ge(act_done, i + 1)
                product(2, d2_w, hid, KC, HC)
            after_vector()
            product(1, bc_w, thought, KC, KC)
            pe.wait_ge(gate_ready, 4)
            for t in range(NT):
                pe.wait_ge(mixed_ready, 2 * (t // 2) + 2)
                for c in range(KC):
                    mm = pe.transpose(psum[:, t, c * P:(c + 1) * P], mixed[:, c, t * P:(t + 1) * P], sh.ident[:, :])
                mm.then_inc(tok_ready, 1)
            norm.tensor(pe)

        @block.scalar
        def _(act):
            for m in range(KC):
                for h in range(2):
                    act.wait_ge(gate_mm, 2 * m + h + 1)
                    act.activation(gate[:, m, h * HALF:(h + 1) * HALF], psum[:, 4 + 2 * m + h, :], ACT.Sigmoid,
                                   bias=small[:, col["gate_b"]][:, m:m + 1]).then_inc(gate_ready, 1)
            for i in range(K_STEPS):
                act.wait_ge(v_done, 2 + 4 * (i + 1))
                act.activation(hid[:, :, :], pre[:, :, :], ACT.Gelu).then_inc(act_done, 1)
            norm.scalar(act)

        @block.vector
        def _(v):
            link = Link(v, v_link)
            count = [0]
            bc4 = lambda name, n: small[:, col[name]].unsqueeze(2).broadcast_to([P, n, BATCH])
            bank = lambda b, n: psum[:, b, 0:n * BATCH].rearrange("p (c b) -> p c b", c=n)

            def after_tensor():
                count[0] += 1
                v.wait_ge(pe_done, count[0])

            def norm_columns(src, gamma, beta, eps):
                after_tensor()
                link(v.scalar_tensor_tensor(out=cen[:, :, :], in0=psum[:, 0, 0:BATCH].unsqueeze(1).broadcast_to([P, KC, BATCH]),
                                            scalar=-1.0 / DM, in1=src, op0=ALU.mult, op1=ALU.add))
                v.tensor_tensor(sq[:, :, :], cen[:, :, :], cen[:, :, :], ALU.mult).then_inc(v_done, 1)
                after_tensor()
                link(v.tensor_scalar(var[:, :], psum[:, 0, 0:BATCH], 1.0 / DM, None, ALU.mult))
                rsqrt_on_vector(v, link, rs[:, :], var[:, :], sh.tmp(BATCH), eps)
                link(v.tensor_tensor(nrm[:, :, :], cen[:, :, :], rs[:, :].unsqueeze(1).broadcast_to([P, KC, BATCH]), ALU.mult))
                link(v.tensor_tensor(nrm[:, :, :], nrm[:, :, :], bc4(gamma, KC), ALU.mult))
                v.tensor_tensor(nrm[:, :, :], nrm[:, :, :], bc4(beta, KC), ALU.add).then_inc(v_done, 1)

            norm_columns(last, "in_g", "in_b", 1e-6)
            after_tensor()
            v.tensor_tensor(thought[:, :, :], bank(1, KC), bc4("agg_b", KC), ALU.add).then_inc(v_done, 1)
            for i in range(K_STEPS):
                v.wait_ge(v_done, 4 * i + 3)
                norm_columns(thought[:, :, :], "pn_g", "pn_b", 1e-6)
                after_tensor()
                v.tensor_tensor(pre[:, :, :], bank(1, HC), bc4("d1_b", HC), ALU.add).then_inc(v_done, 1)
                after_tensor()
                link(v.tensor_tensor(thought[:, :, :], thought[:, :, :], bc4("d2_b", KC), ALU.add))
                v.tensor_tensor(thought[:, :, :], thought[:, :, :], bank(2, KC), ALU.add).then_inc(v_done, 1)
            after_tensor()
            link(v.tensor_tensor(bcast[:, :, :], bank(1, KC), bc4("bc_b", KC), ALU.add))
            v.wait_ge(gate_ready, 4)
            for b in range(BATCH):
                for c in range(KC):
                    sl = slice(b * SEQ, (b + 1) * SEQ)
                    v.scalar_tensor_tensor(out=mixed[:, c, sl], in0=gate[:, c, sl], scalar=bcast[:, c, b:b + 1],
                                           in1=sh.x_feat[:, c, sl], op0=ALU.mult, op1=ALU.add).then_inc(mixed_ready, 1)
            for t in range(NT):
                v.wait_ge(tok_ready, t + 1)
                link.mark(v.bn_stats(sh.stats[:, t, :], psum[:, t, 0:DM]))
            link.wait()
            for t in range(NT):
                link.mark(v.bn_aggr(sh.mean_var[:, t, :], sh.stats[:, t, :]))
            link.wait()
            rsqrt_on_vector(v, link, sh.rstd[:, :], sh.mean_var[:, :, 1], sh.tmp(NT), 1e-6)
            for t in range(NT):
                link.mark(v.tensor_scalar(on_tok[:, t, :], psum[:, t, 0:DM], sh.mean_var[:, t, 0:1], sh.rstd[:, t:t + 1],
                                          ALU.subtract, ALU.mult))
            link.wait()
            for t in range(NT):
                v.tensor_tensor(on_tok[:, t, :], on_tok[:, t, :], out_g[:, :], ALU.mult).then_inc(norm.y_ready, 1)
            v.wait_ge(beta_added, NT)
            norm.vector(v, add=lambda t: v.tensor_tensor(sh.x_tok[:, t, :], sh.x_tok[:, t, :], on_tok[:, t, :], ALU.add))


NB = 2 * SG
NF = SI // P
HPT = P // SP
UN = 4
QUAD = P // CS
NEVER = -1e30


def conv_taps(v, link, acc, x, w, last, nearest=1):
    a = acc.rearrange("p (b s) -> p b s", b=BATCH)
    x = x.rearrange("p (b s) -> p b s", b=BATCH)
    for back in range(nearest, SK):
        ins = v.scalar_tensor_tensor(out=a[:, :, back:SEQ], in0=x[:, :, 0:SEQ - back], scalar=w[:, SK - 1 - back:SK - back],
                                     in1=a[:, :, back:SEQ], op0=ALU.mult, op1=ALU.add)
        if back < SK - 1:
            link(ins)
        else:
            ins.then_inc(last, 1)


def stage_ssd(nc, sh, io):
    k = sh.ssd
    with k.ctx:
        sb = k.sb
        k.acum, k.to_last, k.dt = (sb("s_" + n, [P, NT, SH]) for n in ("acum", "to_last", "dt"))
        k.score = sb("s_score", [P, SG, NT, CS])
        k.eye_c = sb("s_eye_c", [P, CS])
        k.never_c = sb("s_never_c", [P, CS])
        k.same_chunk = sb("s_same_chunk", [P, P])
        k.d_eye = sb("s_d_eye", [P, SH, CS])
        ssd_prepare(nc, sh, io, k)
        ssd_heads(nc, sh, io, k)


def ssd_prepare(nc, sh, io, k):
    with ExitStack() as ctx:
        def sb(name, shape, dt=F32):
            return ctx.enter_context(nc.sbuf_tensor(name, shape, dt))

        w_dt, head, d_all = k.w_dt, k.head, k.d_all
        neg_a = sb("s_neg_a", [SH, 1])
        w_bc = sb("s_w_bc", [P, UN, KC, P])
        bc = sb("s_bc", [P, NB, TOK])
        acc = sh.in_turn[:, :].rearrange("p (q n) -> p q n", q=UN)
        side = sb("s_side", [P, 2, TOK])
        dt_f, a_f, cum_f, last_f, keep = (sb("s_" + n, [SH, TOK]) for n in ("dt_f", "a_f", "cum_f", "last_f", "keep"))
        tri = sb("s_tri", [P, P])
        s = sh.sem
        const, v_link, a_link = s("s_const"), s("s_v_link"), s("s_a_link")
        w_loaded = [s(f"s_wbc_loaded{q}") for q in range(UN)]
        dt_mm, dt_act, turned_in, turned, copied = (s("s_" + n) for n in (
            "dt_mm", "dt_act", "turned_in", "turned", "copied"))
        proj, tap0, side_done, conv, side_added, act_done = (s("s_" + n) for n in (
            "proj", "tap0", "side_done", "conv", "side_added", "act_done"))
        score_mm, score_read = s("s_score_mm"), s("s_score_read")
        psum = sh.psum
        pair = lambda n: psum[:, 2 * n:2 * n + 2, :].rearrange("p a b -> p (a b)")
        block = ctx.enter_context(nc.Block())

        @block.sync
        def _(sp):
            with sp.Fori(0, NB // UN) as r:
                for q in range(UN):
                    sp.wait_ge(proj, UN * r + q + 1)
                    sp.dma_start(w_bc[:, q, :, :], io["s_w_bc"][bass.ds(UN * r + q, 1), :, :, :]
                                 .rearrange("a p c n -> p (a c) n")).then_inc(w_loaded[q], 16)

        @block.gpsimd
        def _(pool):
            pool.memset(k.same_chunk[:, :], 1.0).then_inc(const, 1)
            pool.memset(tri[:, :], 0.0).then_inc(const, 1)
            pool.memset(keep[:, :], 1.0).then_inc(const, 1)
            pool.wait_ge(const, 3)
            pool.memset(keep[:, 0:TOK:CS], 0.0).then_inc(const, 1)
            pool.affine_select(out=tri[:, :], in_=tri[:, :], compare_op=ALU.is_ge, fill=NEVER, base=0,
                               pattern=[[1, P]], channel_multiplier=-1).then_inc(const, 1)
            same = k.same_chunk[:, :].rearrange("p (c n) -> p c n", c=QUAD)
            pool.affine_select(out=same, in_=same, compare_op=ALU.is_ge, fill=0.0, base=0,
                               pattern=[[-CS, QUAD], [0, CS]], channel_multiplier=1).then_inc(const, 1)
            pool.wait_ge(const, 6)
            pool.affine_select(out=same, in_=same, compare_op=ALU.is_ge, fill=0.0, base=CS - 1,
                               pattern=[[CS, QUAD], [0, CS]], channel_multiplier=-1).then_inc(const, 1)
            with pool.Fori(0, NB // UN) as r:
                for q in range(UN):
                    i = UN * r + q
                    pool.wait_ge(conv, i + 1 + UN)
                    a, x = (t.rearrange("p (b s) -> p b s", b=BATCH) for t in (acc[:, q, :], side[:, q % 2, :]))
                    pool.tensor_tensor(a[:, :, 1:SEQ], a[:, :, 1:SEQ], x[:, :, 0:SEQ - 1], ALU.add).then_inc(side_added, 1)

        @block.tensor
        def _(pe):
            pe.sem_inc(proj, UN)
            for h in range(2):
                for c in range(KC):
                    mm = pe.matmul(psum[0:SH, h, :], w_dt[:, c, :], sh.x_feat[:, c, h * HALF:(h + 1) * HALF],
                                   start=c == 0, stop=c == KC - 1)
                mm.then_inc(dt_mm, 1)
            pe.wait_ge(dt_act, 2)
            with pe.Fori(0, NB // UN) as r:
                for q in range(UN):
                    i = UN * r + q
                    pe.wait_ge(w_loaded[q], 16 * r + 16)
                    pe.wait_ge(conv, i + 1)
                    for h in range(2):
                        for c in range(KC):
                            mm = pe.matmul(psum[:, 2 * q + h, :], w_bc[:, q, c, :],
                                           sh.x_feat[:, c, h * HALF:(h + 1) * HALF], start=c == 0, stop=c == KC - 1)
                    mm.then_inc(proj, 1)
            for n, src in enumerate((cum_f, last_f, dt_f)):
                pe.wait_ge(turned_in, n + 1)
                pe.wait_ge(conv, NB + UN)
                for t in range(NT):
                    mm = pe.transpose(psum[:, n, t * SH:(t + 1) * SH], src[:, t * P:(t + 1) * P], sh.ident[0:SH, 0:SH])
                mm.then_inc(turned, 1)
            pe.wait_ge(act_done, NB)
            for g in range(SG):
                pe.wait_ge(copied, 3)
                if g >= 4:
                    pe.wait_ge(score_read, g - 3)
                for t in range(NT):
                    tok = slice(t * P, (t + 1) * P)
                    mm = pe.matmul(pair(g % 4)[:, tok], bc[:, g, tok], bc[:, SG + g, tok], start=True, stop=True)
                mm.then_inc(score_mm, 1)

        @block.scalar
        def _(act):
            link = Link(act, a_link)
            for h in range(2):
                act.wait_ge(dt_mm, h + 1)
                act.activation(dt_f[:, h * HALF:(h + 1) * HALF], psum[0:SH, h, :], ACT.Identity,
                               bias=head[:, 0:1]).then_inc(dt_act, 1)
            act.wait_ge(dt_act, 2)
            link(act.activation(neg_a[:, :], head[:, 1:2], ACT.Exp))
            link(act.activation(a_f[:, :], dt_f[:, :], ACT.Abs))
            link(act.activation(a_f[:, :], a_f[:, :], ACT.Exp, scale=-1.0))
            link(act.activation(a_f[:, :], a_f[:, :], ACT.Ln, bias=1.0))

            def step(i, q, exists):
                if exists(0):
                    act.wait_ge(proj, i + 1 + UN)
                    if exists(UN):
                        act.wait_ge(act_done, i - UN + 1)
                    w = k.conv[:, bass.ds(i + NF, 1), :].rearrange("p a n -> p (a n)")
                    act.activation(acc[:, q, :], pair(q), ACT.Identity, bias=w[:, SK:SK + 1],
                                   scale=w[:, SK - 1:SK]).then_inc(tap0, 1)
                    if exists(2):
                        act.wait_ge(side_added, i - 1)
                    act.activation(side[:, q % 2, :], pair(q), ACT.Copy, scale=w[:, SK - 2:SK - 1]).then_inc(side_done, 1)
                if exists(2):
                    act.wait_ge(side_added, i - 1)
                    act.activation(bc[:, bass.ds(i - 2, 1), :].rearrange("p a n -> p (a n)"), acc[:, (q - 2) % UN, :],
                                   ACT.Silu).then_inc(act_done, 1)
            pipeline(act, NB, UN, step, 2)

        @block.vector
        def _(v):
            link = Link(v, v_link)
            v.sem_inc(conv, UN)
            v.wait_ge(const, 7)
            for c in range(QUAD):
                own = slice(c * CS, (c + 1) * CS)
                link.mark(v.tensor_copy(k.eye_c[own, :], sh.ident[own, own]))
                link.mark(v.tensor_copy(k.never_c[own, :], tri[own, own]))
            link.wait()
            link(v.tensor_tensor(k.d_eye[:, :, :], d_all[:, :].unsqueeze(2).broadcast_to([P, SH, CS]),
                                 k.eye_c[:, :].unsqueeze(1).broadcast_to([P, SH, CS]), ALU.mult))
            v.wait_ge(a_link, 4)
            link(v.scalar_tensor_tensor(out=dt_f[:, :], in0=dt_f[:, :], scalar=0.0, in1=a_f[:, :], op0=ALU.max, op1=ALU.add))
            link(v.tensor_scalar(a_f[:, :], dt_f[:, :], neg_a[:, 0:1], -1.0, ALU.mult, ALU.mult))
            link(v.tensor_tensor_scan(cum_f[:, :], keep[:, :], a_f[:, :], 0.0, ALU.mult, ALU.add))
            v.sem_inc(turned_in, 1)
            chunks = lambda ap: ap.rearrange("p (c n) -> p c n", n=CS)
            v.tensor_tensor(chunks(last_f[:, :]), cum_f[:, CS - 1:TOK:CS].unsqueeze(2).broadcast_to([SH, TOK // CS, CS]),
                            chunks(cum_f[:, :]), ALU.subtract).then_inc(turned_in, 2)
            before = link.n
            with v.Fori(0, NB // UN) as r:
                for q in range(UN):
                    i = UN * r + q
                    v.wait_ge(side_done, i + 1)
                    w = k.conv[:, bass.ds(i + NF, 1), :].rearrange("p a n -> p (a n)")
                    link.n = before + (SK - 3) * i
                    conv_taps(v, link, acc[:, q, :], pair(q), w, conv, nearest=2)
            link.n = before + (SK - 3) * NB
            for n, dst in enumerate((k.acum, k.to_last, k.dt)):
                v.wait_ge(turned, n + 1)
                v.tensor_copy(dst[:, :, :].rearrange("p t h -> p (t h)"), psum[:, n, :]).then_inc(copied, 1)
            for g in range(SG):
                v.wait_ge(score_mm, g + 1)
                for c in range(QUAD):
                    own = slice(c * CS, (c + 1) * CS)
                    ins = v.tensor_copy(k.score[own, g, :, :], pair(g % 4)[own, :].rearrange("p (t n) -> p t n", t=NT)[:, :, own])
                ins.then_inc(score_read, 1)


def ssd_heads(nc, sh, io, k):
    with ExitStack() as ctx:
        def sb(name, shape, dt=F32):
            return ctx.enter_context(nc.sbuf_tensor(name, shape, dt))

        w_in = sb("h_w_in", [P, UN, 2 * KC * P])
        w_hi, w_lo = (sb("h_w_" + n, [P, 2, 2, KC, P], F32R) for n in ("hi", "lo"))
        w_out = sb("h_w_out", [P, 2, DM])
        wo = [sb("h_wo_" + n, [P, 2, DM], F32R) for n in ("hi", "lo")]
        raw, acc = sb("h_raw", [P, TOK]), sb("h_acc", [P, 2, TOK])
        hid = sb("h_hid", [P, 2, NT, P])
        gate = sb("h_gate", [P, 2, TOK])
        yg = sb("h_yg", [P, TOK])
        yg_parts = [sb("h_yg_" + n, [P, 2, TOK], F32R) for n in ("hi", "lo")]
        sq = sb("h_sq", [P, TOK])
        sq_sum = sb("h_sq_sum", [P, TOK])
        mat = sh.in_turn[:, :].rearrange("p (q b n) -> p q b n", q=2, n=P)
        CW = [P, 2, NT, HPT, CS]
        spread, minus, seg_l, seg_m, score_dt = (sb("h_" + n, CW) for n in ("spread", "minus", "seg_l", "seg_m", "score_dt"))
        ssum, rs = sb("h_ssum", [P, NT]), sb("h_rs", [P, NT])
        s = sh.sem
        w_loaded = [s(f"h_w_loaded{q}") for q in range(UN)]
        wo_loaded = [s(f"h_wo_loaded{q}") for q in range(UN)]
        w_hi_ready, w_lo_ready, wo_ready, ssum_mm = s("h_w_hi"), s("h_w_lo"), s("h_wo"), s("h_ssum_mm")
        ahead_loaded = s("h_ahead_loaded")
        wo_hi, yg_hi, yg_split = s("h_wo_hi"), s("h_yg_hi_done"), s("h_yg_split")
        (hid_mm, out_mm, ai_mm, gate_mm, ht_mm, y_mm) = (s("h_" + n) for n in (
            "hid_mm", "out_mm", "ai_mm", "gate_mm", "ht_mm", "y_mm"))
        (raw_done, u_done, gate_read, ht_read, exp_done, sq_done) = (s("h_" + n) for n in (
            "raw_done", "u_done", "gate_read", "ht_read", "exp_done", "sq_done"))
        (conv, mul_done, seg_done, mat_done, yg_done, v_link, zeroed) = (s("h_" + n) for n in (
            "conv", "mul_done", "seg_done", "mat_done", "yg_done", "v_link", "zeroed"))
        (spread_done, score_dt_done, masked, summed, sq_added, exp_l) = (s("h_" + n) for n in (
            "spread_done", "score_dt_done", "masked", "summed", "sq_added", "exp_l"))
        norm = PostNorm(sh, "h", parts=True)
        psum = sh.psum
        pair = lambda n: psum[:, 2 * n:2 * n + 2, :].rearrange("p a b -> p (a b)")
        X, Z = pair(0), pair(1)
        comp = lambda ap: ap.rearrange("p (t h n) -> p t h n", t=NT, h=HPT)
        flat = lambda ap: ap.rearrange("p t h n -> p (t h n)")

        def heads(tile, i):
            return tile[:, :, bass.ds(HPT * i, HPT)].unsqueeze(3).broadcast_to([P, NT, HPT, CS])

        block = ctx.enter_context(nc.Block())

        @block.sync
        def _(sp):
            def load(i, q, exists):
                if exists(0):
                    if exists(UN):
                        sp.wait_ge(w_lo_ready, i - UN + 1)
                    sp.dma_start(w_in[:, q, :], io["s_w_in"][bass.ds(i, 1), :, :].rearrange("a p n -> p (a n)")).then_inc(w_loaded[q], 16)
                if exists(2):
                    if exists(4):
                        sp.wait_ge(wo_ready, i - 3)
                    sp.dma_start(w_out[:, q % 2, :], io["s_w_out"][bass.ds(i - 2, 1), :, :]
                                 .rearrange("a p n -> p (a n)")).then_inc(wo_loaded[(q - 2) % UN], 16)
            pipeline(sp, NF, UN, load, 2)
            sp.wait_ge(y_mm, NF)
            sp.dma_start(sh.in_turn[:, :], io["a_w_q"].rearrange("p c g n -> p (c g n)")).then_inc(ahead_loaded, 16)
            sp.wait_ge(ahead_loaded, 16)

        @block.tensor
        def _(pe):
            pe.wait_ge(zeroed, 2)
            for bank in range(4, 8):
                pe.matmul(psum[:, bank, :], sh.ident[:, :], mat[:, 0, 0:4, :].rearrange("p a n -> p (a n)"),
                          start=True, stop=False, skip_group_check=True)

            def out_part(i, q, tt):
                for t in tt:
                    mm = split_products(pe, psum[:, 4 + t // 2, (t % 2) * DM:(t % 2 + 1) * DM],
                                        [y[:, (q - 3) % 2, t * P:(t + 1) * P] for y in yg_parts],
                                        [w[:, (q - 3) % 2, :] for w in wo], False, False, skip_group_check=True)
                return mm

            def project(out, q, which):
                for h in range(2):
                    own = slice(h * HALF, (h + 1) * HALF)
                    for c in range(KC):
                        mm = split_products(pe, out[:, own], (w_hi[:, q % 2, which, c, :], w_lo[:, q % 2, which, c, :]),
                                            (sh.x_hi[:, c, own], sh.x_lo[:, c, own]), c == 0, c == KC - 1)
                return mm

            def step(i, q, exists):
                if exists(0):
                    pe.wait_ge(w_lo_ready, i + 1)
                    if exists(1):
                        pe.wait_ge(seg_done, 2 * i)
                    project(X, q, 0).then_inc(hid_mm, 1)
                if exists(3):
                    pe.wait_ge(wo_ready, i - 2)
                    pe.wait_ge(yg_split, i - 2)
                    out_part(i, q, range(NT // 2))
                if exists(1):
                    if exists(0):
                        pe.wait_ge(raw_done, i + 1)
                    else:
                        pe.wait_ge(seg_done, 2 * i)
                    pe.wait_ge(u_done, i)
                    for t in range(NT):
                        mm = pe.transpose(X[:, t * P:(t + 1) * P], acc[:, (q - 1) % 2, t * P:(t + 1) * P], sh.ident[:, :])
                    mm.then_inc(ht_mm, 1)
                if exists(0):
                    if exists(2):
                        pe.wait_ge(yg_done, i - 1)
                    elif exists(1):
                        pe.wait_ge(gate_read, i)
                    project(Z, q, 1).then_inc(gate_mm, 1)
                    pe.wait_ge(spread_done, i + 1)
                    pe.wait_ge(raw_done, i + 1)
                    if exists(1):
                        pe.wait_ge(ht_read, i)
                    pe.matmul(X[:, 0:512], k.same_chunk[:, :], flat(spread[:, q % 2]), start=True, stop=True).then_inc(ai_mm, 1)
                if exists(3):
                    out_part(i, q, range(NT // 2, NT)).then_inc(out_mm, 1)
                if exists(1):
                    if exists(0):
                        pe.wait_ge(gate_read, i + 1)
                    else:
                        pe.wait_ge(yg_done, i - 1)
                    pe.wait_ge(mat_done, i)
                    pe.wait_ge(ht_read, i)
                    for t in range(NT):
                        for hh in range(HPT):
                            own = slice(hh * SP, (hh + 1) * SP)
                            mm = pe.matmul(Z[own, t * P:(t + 1) * P], hid[:, (q - 1) % 2, t, own],
                                           mat[:, (q - 1) % 2, t * HPT + hh, :], start=True, stop=True)
                    mm.then_inc(y_mm, 1)
            pipeline(pe, NF, UN, step, 3)
            pe.wait_ge(sq_added, NF + 1)
            for t in range(NT):
                mm = pe.matmul(X[:, t:t + 1], sq_sum[:, t * P:(t + 1) * P], sh.ones[:, 0:1], start=True, stop=True)
            mm.then_inc(ssum_mm, 1)
            pe.wait_ge(out_mm, NF)
            norm.tensor(pe)

        @block.scalar
        def _(act):
            def split_weights(i, q, exists):
                act.wait_ge(w_loaded[q], 16 // UN * (i - q) + 16)
                if exists(2):
                    act.wait_ge(gate_mm, i - 1)
                act.activation(w_hi[:, q % 2].rearrange("p a c n -> p (a c n)"), w_in[:, q, :], ACT.Copy).then_inc(w_hi_ready, 1)

            def step(i, q, exists):
                if exists(1):
                    last = acc[:, (q - 1) % 2, :]
                    act.wait_ge(conv, i)
                    act.activation(last, last, ACT.Silu).then_inc(u_done, 1)
                if exists(0):
                    act.wait_ge(hid_mm, i + 1)
                    if exists(1):
                        act.wait_ge(conv, i)
                    act.activation(raw[:, :], X, ACT.Copy).then_inc(raw_done, 1)
                if exists(1):
                    act.wait_ge(ht_mm, i)
                    if exists(3):
                        act.wait_ge(y_mm, i - 2)
                    act.activation(hid[:, (q - 1) % 2].rearrange("p t n -> p (t n)"), X, ACT.Copy).then_inc(ht_read, 1)
                if exists(2):
                    act.wait_ge(yg_done, i - 1)
                    if exists(4):
                        act.wait_ge(out_mm, i - 3)
                    act.activation(yg_parts[0][:, q % 2, :], yg[:, :], ACT.Copy).then_inc(yg_hi, 1)
                    if exists(3):
                        act.wait_ge(sq_added, i - 1)
                    act.activation(sq[:, :], yg[:, :], ACT.Square).then_inc(sq_done, 1)
                    qo = (q - 2) % UN
                    act.wait_ge(wo_loaded[qo], 16 // UN * (i - 2 - qo) + 16)
                    act.activation(wo[0][:, q % 2, :], w_out[:, q % 2, :], ACT.Copy,
                                   scale=k.norm_w[:, bass.ds(i - 2, 1)]).then_inc(wo_hi, 1)
                if exists(0):
                    act.wait_ge(gate_mm, i + 1)
                    if exists(2):
                        act.wait_ge(yg_done, i - 1)
                    act.activation(gate[:, q % 2, :], Z, ACT.Silu).then_inc(gate_read, 1)
                    act.wait_ge(seg_done, 2 * i + 2)
                    act.activation(flat(seg_m[:, q % 2]), flat(seg_m[:, q % 2]), ACT.Exp).then_inc(exp_done, 1)
                    act.activation(flat(seg_l[:, q % 2]), flat(seg_l[:, q % 2]), ACT.Exp).then_inc(exp_l, 1)

            def turn(i, q, exists):
                if exists(0):
                    split_weights(i, q, exists)
                step(i - 1, (q - 1) % UN, lambda n: exists(n + 1))
            pipeline(act, NF, UN, turn, 3)
            norm.scalar(act)

        @block.gpsimd
        def _(pool):
            pool.memset(sq_sum[:, :], 0.0).then_inc(sq_added, 1)
            bc = lambda tile: tile[:, :].unsqueeze(1).unsqueeze(1).broadcast_to([P, NT, HPT, CS])

            def split_weights(i, q, exists):
                pool.wait_ge(w_hi_ready, i + 1)
                pool.tensor_tensor(w_lo[:, q % 2].rearrange("p a c n -> p (a c n)"), w_in[:, q, :],
                                   w_hi[:, q % 2].rearrange("p a c n -> p (a c n)"), ALU.subtract).then_inc(w_lo_ready, 1)

            def step(i, q, exists):
                if exists(0):
                    if exists(2):
                        pool.wait_ge(ai_mm, i - 1)
                    pool.tensor_tensor(spread[:, q % 2], heads(k.acum, i), bc(k.eye_c), ALU.mult).then_inc(spread_done, 1)
                    if exists(2):
                        pool.wait_ge(mat_done, i - 1)
                    pool.tensor_tensor(score_dt[:, q % 2], k.score[:, HPT * q:HPT * (q + 1), :, :].rearrange("p g t n -> p t g n"),
                                       heads(k.dt, i), ALU.mult).then_inc(score_dt_done, 1)
                    pool.tensor_tensor(minus[:, q % 2], bc(k.never_c), heads(k.acum, i), ALU.subtract).then_inc(masked, 1)
                if exists(2):
                    pool.wait_ge(yg_hi, i - 1)
                    pool.tensor_tensor(yg_parts[1][:, q % 2, :], yg[:, :], yg_parts[0][:, q % 2, :], ALU.subtract).then_inc(yg_split, 1)
                if exists(0):
                    pool.wait_ge(exp_done, i + 1)
                    pool.wait_ge(exp_l, i + 1)
                    pool.tensor_tensor(seg_l[:, q % 2], seg_l[:, q % 2], seg_m[:, q % 2], ALU.add).then_inc(summed, 1)
                if exists(2):
                    pool.wait_ge(sq_done, i - 1)
                    pool.wait_ge(sq_added, i - 1)
                    pool.tensor_tensor(sq_sum[:, :], sq_sum[:, :], sq[:, :], ALU.add).then_inc(sq_added, 1)

            def turn(i, q, exists):
                if exists(0):
                    split_weights(i, q, exists)
                step(i - 1, (q - 1) % UN, lambda n: exists(n + 1))
            pipeline(pool, NF, UN, turn, 3)
            norm.gpsimd(pool)

        @block.vector
        def _(v):
            link = Link(v, v_link)
            v.memset(mat[:, 0], 0.0).then_inc(zeroed, 1)
            v.memset(mat[:, 1], 0.0).then_inc(zeroed, 1)
            v.wait_ge(zeroed, 2)

            def step(i, q, exists):
                if exists(2):
                    v.wait_ge(y_mm, i - 1)
                    v.wait_ge(gate_read, i - 1)
                    if exists(3):
                        v.wait_ge(yg_split, i - 2)
                        v.wait_ge(sq_done, i - 2)
                    v.tensor_tensor(yg[:, :], Z, gate[:, q % 2, :], ALU.mult).then_inc(yg_done, 1)
                if exists(1):
                    m = (q - 1) % 2
                    v.wait_ge(summed, i)
                    v.wait_ge(score_dt_done, i)
                    v.tensor_tensor(seg_l[:, m], seg_l[:, m], score_dt[:, m], ALU.mult).then_inc(mul_done, 1)
                    v.wait_ge(mul_done, i)
                    if exists(3):
                        v.wait_ge(y_mm, i - 2)
                    for c in range(QUAD):
                        own = slice(c * CS, (c + 1) * CS)
                        ins = v.tensor_tensor(mat[own, m, :, own].rearrange("p (t h) n -> p t h n", t=NT), seg_l[own, m],
                                              k.d_eye[own, bass.ds(HPT * (i - 1), HPT), :].unsqueeze(1).broadcast_to([CS, NT, HPT, CS]),
                                              ALU.add)
                    ins.then_inc(mat_done, 1)
                if exists(0):
                    v.wait_ge(raw_done, i + 1)
                    if exists(2):
                        v.wait_ge(ht_mm, i - 1)
                    w = k.conv[:, bass.ds(i, 1), :].rearrange("p a n -> p (a n)")
                    link.n = 3 * i
                    link(v.tensor_scalar(acc[:, q % 2, :], raw[:, :], w[:, SK - 1:SK], w[:, SK:SK + 1], ALU.mult, ALU.add))
                    conv_taps(v, link, acc[:, q % 2, :], raw[:, :], w, conv)
                    v.wait_ge(ai_mm, i + 1)
                    if exists(2):
                        v.wait_ge(summed, i - 1)
                    z = comp(X[:, 0:512])
                    v.wait_ge(masked, i + 1)
                    v.tensor_tensor(seg_l[:, q % 2], z, minus[:, q % 2], ALU.add).then_inc(seg_done, 1)
                    v.tensor_tensor(seg_m[:, q % 2], z, heads(k.to_last, i), ALU.add).then_inc(seg_done, 1)
                if exists(2):
                    v.wait_ge(wo_hi, i - 1)
                    v.scalar_tensor_tensor(out=wo[1][:, q % 2, :], in0=w_out[:, q % 2, :], scalar=k.norm_w[:, bass.ds(i - 2, 1)],
                                           in1=wo[0][:, q % 2, :], op0=ALU.mult, op1=ALU.subtract).then_inc(wo_ready, 1)
            pipeline(v, NF, UN, step, 2)
            v.wait_ge(ssum_mm, 1)
            link.n = 3 * NF
            link(v.tensor_scalar(ssum[:, :], X[:, 0:NT], 1.0 / SI, None, ALU.mult))
            rsqrt_on_vector(v, link, rs[:, :], ssum[:, :], sh.tmp(NT), 1e-6)
            v.wait_ge(out_mm, NF)
            v.sem_inc(norm.y_ready, NT)
            norm.vector(v, add=lambda t: v.scalar_tensor_tensor(
                out=sh.x_tok[:, t, :], in0=psum[:, 4 + t // 2, (t % 2) * DM:(t % 2 + 1) * DM], scalar=rs[:, t:t + 1],
                in1=sh.x_tok[:, t, :], op0=ALU.mult, op1=ALU.add))


def stage_attention(nc, sh, io):
    with ExitStack() as ctx:
        def sb(name, shape, dt=F32):
            return ctx.enter_context(nc.sbuf_tensor(name, shape, dt))

        (k_cos, k_sin), (q_cos, q_sin) = sh.rope.k, sh.rope.q
        w_kv = [sb("a_w_kv_" + n, [P, KC, KVH, 2 * HD], F32R) for n in ("hi", "lo")]
        w_q = sh.in_turn[:, :].rearrange("p (c g n) -> p c g n", c=KC, g=KVH)
        w_o = sb("a_w_o", [P, QH, DM])
        src = [sb("a_src_" + n, [P, KC, 2 * SEQ], F32R) for n in ("hi", "lo")]
        src_own = sb("a_src_own", [P, KC, SEQ])
        k_rot, k_t2 = (sb("a_" + n, [P, KT, 2, ROPE]) for n in ("k_rot", "k_t2"))
        q_rot, q_t2 = (sb("a_" + n, [P, QT, REP, 2, ROPE]) for n in ("q_rot", "q_t2"))
        sq = sb("a_sq", [P, KT + QT * REP, HD])
        three_halves, soft_scale = sb("a_three_halves", [P, KT + QT * REP]), sb("a_soft_scale", [P, QT * REP])
        ms, rs = sb("a_ms", [P, KT + QT * REP]), sb("a_rs", [P, KT + QT * REP])
        q_scale = sb("a_q_scale", [P, 2, QT * REP])
        k_t, q_t = sb("a_k_t", [P, KT, HD]), sb("a_q_t", [P, QT, REP, HD])
        k_f = [sb("a_k_f_" + n, [P, 2, 2 * SEQ], F32R) for n in ("hi", "lo")]
        q_f = [sb("a_q_f_" + n, [P, 2, REP, SEQ], F32R) for n in ("hi", "lo")]
        val = [sb("a_val_" + n, [P, 2, KT, HD], F32R) for n in ("hi", "lo")]
        neg_max, bias, total, inv = (sb("a_" + n, [P, QT]) for n in ("neg_max", "bias", "total", "inv"))
        prob = sb("a_prob", [P, 2, QT, 2 * SEQ])
        prob_t = [sb("a_prob_t_" + n, [P, 2, QT, KT, P], F32R) for n in ("hi", "lo")]
        attn_f = sb("a_attn_f", [P, 2, SEQ])
        s = sh.sem
        (src_ready, kv_mm, q_mm, kt_mm, qt_mm, s_mm, p_mm, pv_mm, wo_mm) = (s("a_" + n) for n in (
            "src_ready", "kv_mm", "q_mm", "kt_mm", "qt_mm", "s_mm", "p_mm", "pv_mm", "wo_mm"))
        (k_sq, kv_read, q_sq, k_turned, q_turned, exp_done, p_turned, attn_read) = (s("a_" + n) for n in (
            "k_sq", "kv_read", "q_sq", "k_turned", "q_turned", "exp_done", "p_turned", "attn_read"))
        (k_parts, q_parts, seeded, q_rs_done, bias_done, scaled, y_read, v_link, p_link) = (s("a_" + n) for n in (
            "k_parts", "q_parts", "seeded", "q_rs_done", "bias_done", "scaled", "y_read", "v_link", "p_link"))
        k_rot_done, q_rot_done, g_link, q_read = s("a_k_rot_done"), s("a_q_rot_done"), s("a_g_link"), s("a_q_read")
        const = s("a_const")
        kv_loaded, o_loaded, w_split = (s("a_" + n) for n in ("kv_loaded", "o_loaded", "w_split"))
        (val_hi, val_split, k_hi, q_hi, p_hi) = (s("a_" + n) for n in ("val_hi", "val_split", "k_hi", "q_hi", "p_hi"))
        kv_raw = prob[:, :, :, :].rearrange("p a t n -> p (a t n)")
        norm = PostNorm(sh, "a", parts=True)
        psum = sh.psum
        SCORE, TURN, PV, OUT, PROJ = 0, 2, 4, 5, 6
        proj = psum[:, PROJ:PROJ + 2, :]
        kv_psum = proj.rearrange("p b (t n) -> p (b t) n", t=2)
        proj_flat = proj.rearrange("p b n -> p (b n)")

        def over_batches(eng, body):
            body(0, True, False)
            with eng.Fori(1, BATCH - 1) as b:
                body(b, False, False)
            body(BATCH - 1, False, True)

        def plan(last):
            for kvh in range(KVH):
                for j in range(REP):
                    yield kvh, j, not (last and kvh == KVH - 1)

        block = ctx.enter_context(nc.Block())

        @block.sync
        def _(sp):
            sp.dma_start(kv_raw, io["a_w_kv"].rearrange("p c g n -> p (c g n)")).then_inc(kv_loaded, 16)
            sp.dma_start(w_o[:, :, :], io["a_w_o"]).then_inc(o_loaded, 16)

        @block.gpsimd
        def _(pool):
            def take_source(b):
                context = sh.ctx_feat[:, :, bass.ds(b, 1), :].rearrange("p c a n -> p c (a n)")
                own = bass.ds(SEQ * b, SEQ)
                pool.tensor_copy(src_own[:, :, :], sh.x_feat[:, :, own]).then_inc(src_ready, 1)
                pool.tensor_copy(src[0][:, :, 0:SEQ], context).then_inc(src_ready, 1)
                pool.tensor_copy(src[0][:, :, SEQ:2 * SEQ], sh.x_hi[:, :, own]).then_inc(src_ready, 1)
                pool.wait_ge(src_ready, 5 * b + 2)
                pool.tensor_copy(src[1][:, :, SEQ:2 * SEQ], sh.x_lo[:, :, own]).then_inc(src_ready, 1)
                pool.tensor_tensor(src[1][:, :, 0:SEQ], context, src[0][:, :, 0:SEQ], ALU.subtract).then_inc(src_ready, 1)

            def keys(g):
                pool.wait_ge(k_parts, g + 1)
                pool.tensor_tensor(k_rot[:, :, :, :], k_rot[:, :, :, :], k_t2[:, :, :, :], ALU.add).then_inc(g_link, 1)

            def factors(g, slot):
                link = Link(pool, p_link)
                link.n = (2 + 4 * NEWTON) * g
                tmp = sh.tmp(KT + QT * REP)[0]
                pool.wait_ge(seeded, g + 1)
                for _ in range(NEWTON):
                    link(pool.tensor_tensor(tmp, rs[:, :], rs[:, :], ALU.mult))
                    link(pool.tensor_tensor(tmp, tmp, ms[:, :], ALU.mult))
                    link(pool.tensor_tensor(tmp, tmp, three_halves[:, :], ALU.add))
                    link(pool.tensor_tensor(rs[:, :], rs[:, :], tmp, ALU.mult))
                link(pool.tensor_tensor(q_scale[:, slot, :], rs[:, KT:KT + QT * REP], soft_scale[:, :], ALU.mult))
                pool.sem_inc(q_rs_done, 1)
                k_rs = rs[:, 0:KT]
                pool.wait_ge(g_link, g + 1)
                flat = k_rot[:, :, :, :].rearrange("p t a n -> p t (a n)")
                link.mark(pool.tensor_tensor(flat, flat, k_rs.unsqueeze(2).broadcast_to([P, KT, HD]), ALU.mult))
                link.wait()
                pool.sem_inc(k_rot_done, 1)

            def queries(g):
                pool.wait_ge(q_parts, g + 1)
                pool.tensor_tensor(q_rot[:, :, :, :, :].rearrange("p t h a n -> p (t h a n)"),
                                   q_rot[:, :, :, :, :].rearrange("p t h a n -> p (t h a n)"),
                                   q_t2[:, :, :, :, :].rearrange("p t h a n -> p (t h a n)"), ALU.add).then_inc(q_rot_done, 1)

            pool.memset(three_halves[:, :], 1.5).then_inc(const, 1)
            pool.memset(soft_scale[:, :], HD ** -0.5).then_inc(const, 1)
            pool.wait_ge(const, 2)
            take_source(0)
            queries(0)
            keys(0)
            factors(0, 0)

            def body(b, first, last):
                for kvh, j, more in plan(last):
                    if not more:
                        continue
                    g = KVH * b + kvh + 1
                    if kvh == KVH - 1 and j == 0:
                        pool.wait_ge(kv_mm, g)
                        take_source(b + 1)
                    if j == 0:
                        queries(g)
                    if j == 1:
                        keys(g)
                        factors(g, (kvh + 1) % 2)
            over_batches(pool, body)
            norm.gpsimd(pool)

        @block.tensor
        def _(pe):
            pe.sem_inc(p_mm, 2 * QT)
            pe.sem_inc(pv_mm, 1)

            def project_kv(g, kvh, b):
                pe.wait_ge(src_ready, 5 * b + 5)
                pe.wait_ge(q_read, g + 1)
                for t in range(KT):
                    for c in range(KC):
                        mm = split_products(pe, kv_psum[:, t, :], [x[:, c, t * P:(t + 1) * P] for x in src],
                                            [w[:, c, kvh, :] for w in w_kv], c == 0, c == KC - 1)
                mm.then_inc(kv_mm, 1)

            def project_q(g, kvh, b):
                pe.wait_ge(src_ready, 5 * b + 1)
                wait_beyond_start(pe, k_turned, g)
                for t in range(QT):
                    for c in range(KC):
                        mm = pe.matmul(psum[:, PROJ + t, :], src_own[:, c, t * P:(t + 1) * P], w_q[:, c, kvh, :], start=c == 0, stop=c == KC - 1)
                mm.then_inc(q_mm, 1)

            def turn_k(g):
                pe.wait_ge(k_rot_done, g + 1)
                pe.wait_ge(q_turned, g + 1)
                for t in range(KT):
                    mm = pe.transpose(proj_flat[:, t * P:(t + 1) * P], k_rot[:, t, :, :].rearrange("p a n -> p (a n)"), sh.ident[:, :])
                mm.then_inc(kt_mm, 1)

            def turn_q(g):
                pe.wait_ge(q_rot_done, g + 1)
                pe.wait_ge(val_split, g + 1)
                for h in range(REP):
                    for t in range(QT):
                        at = (h * QT + t) * P
                        mm = pe.transpose(proj_flat[:, at:at + P], q_rot[:, t, h, :, :].rearrange("p a n -> p (a n)"), sh.ident[:, :])
                mm.then_inc(qt_mm, 1)

            def scores(n, g, slot, h):
                if h == 0:
                    pe.wait_ge(k_turned, g + 1)
                    pe.wait_ge(q_turned, g + 1)
                for t in range(QT):
                    pe.wait_ge(exp_done, QT * n + t + 1)
                    split_products(pe, psum[:, SCORE + t, :], [q[:, slot, h, t * P:(t + 1) * P] for q in q_f],
                                   [x[:, slot, :] for x in k_f], True, True).then_inc(s_mm, 1)

            def turn_probs(n, p):
                for t in range(QT):
                    pe.wait_ge(scaled, QT * n + t + 1)
                    pe.wait_ge(p_turned, QT * n + t + 1)
                    for c in range(KT):
                        mm = pe.transpose(psum[:, TURN + t, c * P:(c + 1) * P], prob[:, p, t, c * P:(c + 1) * P], sh.ident[:, :])
                    mm.then_inc(p_mm, 1)

            def values(n, slot, p):
                pe.wait_ge(p_turned, QT * n + 2 * QT)
                pe.wait_ge(attn_read, n + 1)
                for c in range(KT):
                    mm = split_products(pe, psum[:, PV, 0:SEQ], [x[:, slot, c, :] for x in val],
                                        [x[:, p, :, c, :] for x in prob_t], c == 0, c == KT - 1)
                mm.then_inc(pv_mm, 1)

            def output(n, m, b):
                pe.wait_ge(attn_read, n + 2)
                if m == 0 and not (isinstance(b, int) and b == 0):
                    pe.wait_ge(y_read, b)
                for t in range(QT):
                    mm = pe.matmul(psum[:, OUT, t * DM:(t + 1) * DM], attn_f[:, m % 2, t * P:(t + 1) * P], w_o[:, m, :],
                                   start=m == 0 and t == 0, stop=m == QH - 1, skip_group_check=True)
                mm.then_inc(wo_mm, 1)

            project_q(0, 0, 0)
            pe.wait_ge(w_split, 2)
            project_kv(0, 0, 0)
            turn_q(0)
            turn_k(0)
            pe.wait_ge(o_loaded, 16)

            def body(b, first, last):
                for kvh, j, more in plan(last):
                    m = REP * kvh + j
                    n, g = QH * b + m, KVH * b + kvh
                    nb, nk = (b, kvh + 1) if kvh < KVH - 1 else (b + 1, 0)
                    scores(n, g, kvh % 2, j)
                    if m >= 2 or not first:
                        values(n - 2, (m - 2) // REP % 2, m % 2)
                    if more and j == 2:
                        turn_q(g + 1)
                    if more and j == 3:
                        turn_k(g + 1)
                    if m >= 1 or not first:
                        turn_probs(n - 1, (m - 1) % 2)
                    if more and j == 0:
                        project_q(g + 1, nk, nb)
                    if more and j == 1:
                        project_kv(g + 1, nk, nb)
                    if m >= 3 or not first:
                        output(n - 3, (m - 3) % QH, b)
            over_batches(pe, body)
            n, m = QH * BATCH, QH
            values(n - 2, (m - 2) // REP % 2, m % 2)
            turn_probs(n - 1, (m - 1) % 2)
            output(n - 3, m - 3, BATCH)
            values(n - 1, (m - 1) // REP % 2, (m - 1) % 2)
            output(n - 2, m - 2, BATCH)
            output(n - 1, m - 1, BATCH)
            norm.tensor(pe)

        @block.scalar
        def _(act):
            act.sem_inc(exp_done, QT)
            act.sem_inc(attn_read, 1)

            def squares(x, n):
                return act.activation(sq[:, n, :], x, ACT.Square, accum_out=ms[:, n:n + 1])

            def keys(g):
                act.wait_ge(kv_mm, g + 1)
                if not (isinstance(g, int) and g == 0):
                    act.wait_ge(k_parts, g)
                    act.wait_ge(k_sq, g)
                act.activation(k_t[:, :, :], kv_psum[:, :, 0:HD], ACT.Copy).then_inc(kv_read, 1)
                act.wait_ge(kv_read, g + 1)
                wait_beyond_start(act, q_rs_done, g)
                for t in range(KT):
                    ins = squares(k_t[:, t, :], t)
                ins.then_inc(k_sq, 1)

            def values(g, slot):
                if not (isinstance(g, int) and g == 0):
                    act.wait_ge(pv_mm, REP * (g - 1) + 1)
                act.wait_ge(kv_mm, g + 1)
                act.activation(val[0][:, slot, :, :], kv_psum[:, :, HD:2 * HD], ACT.Copy).then_inc(val_hi, 1)

            def queries(g):
                act.wait_ge(q_mm, g + 1)
                wait_beyond_start(act, q_parts, g)
                act.activation(q_t[:, :, :, :].rearrange("p t h n -> p (t h n)"), proj_flat, ACT.Copy).then_inc(q_read, 1)
                act.wait_ge(q_read, g + 1)
                for n in range(QT * REP):
                    ins = squares(q_t[:, n // REP, n % REP, :], KT + n)
                ins.then_inc(q_sq, 1)

            def keys_turned(g, slot):
                act.wait_ge(kt_mm, g + 1)
                act.activation(k_f[0][:, slot, :], proj_flat[:, 0:2 * SEQ], ACT.Copy).then_inc(k_hi, 1)

            def queries_turned(g, slot):
                act.wait_ge(qt_mm, g + 1)
                act.activation(q_f[0][:, slot, :, :].rearrange("p h n -> p (h n)"), proj_flat, ACT.Copy).then_inc(q_hi, 1)

            def probs_turned(n, t, p):
                act.wait_ge(p_mm, QT * n + t + 1 + 2 * QT)
                wait_beyond_start(act, pv_mm, n)
                act.activation(prob_t[0][:, p, t, :, :].rearrange("p c n -> p (c n)"), psum[:, TURN + t, :], ACT.Copy).then_inc(p_hi, 1)

            def exps(n, t, slot, h, p):
                act.wait_ge(bias_done, QT * n + t + 1)
                act.wait_ge(p_mm, QT * n + QT)
                act.activation(prob[:, p, t, :], psum[:, SCORE + t, :], ACT.Exp, bias=bias[:, t:t + 1],
                               scale=q_scale[:, slot, t * REP + h:t * REP + h + 1], accum_out=total[:, t:t + 1]).then_inc(exp_done, 1)

            def attended(n, m):
                act.wait_ge(pv_mm, n + 2)
                if not isinstance(n, int) or n >= 2:
                    act.wait_ge(wo_mm, n - 1)
                act.activation(attn_f[:, m % 2, :], psum[:, PV, 0:SEQ], ACT.Copy).then_inc(attn_read, 1)

            w_hi = w_kv[0][:, :, :, :].rearrange("p c g n -> p (c g n)")
            act.wait_ge(kv_loaded, 16)
            act.activation(w_hi, kv_raw, ACT.Copy).then_inc(w_split, 1)
            queries(0)
            keys(0)
            values(0, 0)
            queries_turned(0, 0)
            keys_turned(0, 0)

            def body(b, first, last):
                for kvh, j, more in plan(last):
                    m = REP * kvh + j
                    n, g, nxt = QH * b + m, KVH * b + kvh, (kvh + 1) % 2
                    for t in range(QT):
                        exps(n, t, kvh % 2, j, m % 2)
                    if more and j == 3:
                        keys_turned(g + 1, nxt)
                    if m >= 2 or not first:
                        attended(n - 2, (m - 2) % QH)
                    if m >= 1 or not first:
                        for t in range(QT):
                            probs_turned(n - 1, t, (m - 1) % 2)
                    if more and j == 0:
                        queries(g + 1)
                    if more and j == 1:
                        keys(g + 1)
                        values(g + 1, nxt)
                    if more and j == 2:
                        queries_turned(g + 1, nxt)
            over_batches(act, body)
            n = QH * BATCH - 1
            attended(n - 1, 0)
            for t in range(QT):
                probs_turned(n, t, 1)
            attended(n, 1)
            norm.scalar(act)

        @block.vector
        def _(v):
            link = Link(v, v_link)
            v.sem_inc(p_turned, QT)

            def keys(g, b, slot):
                v.wait_ge(kv_read, g + 1)
                wait_beyond_start(v, kt_mm, g)
                x = k_t[:, :, :].rearrange("p t (a n) -> p t a n", a=2)
                cos, sin = (tab[:, bass.ds(KT * b, KT), :, :] for tab in (k_cos, k_sin))
                link.mark(v.tensor_tensor(k_rot[:, :, :, :], x, cos, ALU.mult))
                for half in range(2):
                    link.mark(v.tensor_tensor(k_t2[:, :, half, :], x[:, :, 1 - half, :], sin[:, :, half, :], ALU.mult))
                link.wait()
                v.sem_inc(k_parts, 1)

            def values(g, slot):
                v.wait_ge(val_hi, g + 1)
                v.tensor_tensor(val[1][:, slot, :, :], kv_psum[:, :, HD:2 * HD], val[0][:, slot, :, :], ALU.subtract).then_inc(val_split, 1)

            def queries(g, b, slot):
                v.wait_ge(q_read, g + 1)
                wait_beyond_start(v, qt_mm, g)
                for t in range(QT):
                    x = q_t[:, t, :, :].rearrange("p h (a n) -> p h a n", a=2)
                    cos, sin = (tab[:, bass.ds(QT * b + t, 1), :, :] for tab in (q_cos, q_sin))
                    link.mark(v.tensor_tensor(q_rot[:, t, :, :, :], x, cos.broadcast_to([P, REP, 2, ROPE]), ALU.mult))
                    for half in range(2):
                        link.mark(v.tensor_tensor(q_t2[:, t, :, half, :], x[:, :, 1 - half, :],
                                                  sin[:, :, half, :].broadcast_to([P, REP, ROPE]), ALU.mult))
                link.wait()
                v.sem_inc(q_parts, 1)

            def seeds(g):
                v.wait_ge(k_sq, g + 1)
                v.wait_ge(q_sq, g + 1)
                wait_beyond_start(v, k_rot_done, g)
                link(v.tensor_scalar(ms[:, :], ms[:, :], 1.0 / HD, 1e-6, ALU.mult, ALU.add))
                rsqrt_seed(v, link, rs[:, :], ms[:, :], sh.tmp(KT + QT * REP)[1])
                link(v.tensor_scalar(ms[:, :], ms[:, :], -0.5, None, ALU.mult))
                v.sem_inc(seeded, 1)

            def maxima(n, g, slot, h):
                if h == 0:
                    v.wait_ge(q_rs_done, g + 1)
                for t in range(QT):
                    v.wait_ge(s_mm, QT * n + t + 1)
                    link(v.tensor_reduce(neg_max[:, t:t + 1], psum[:, SCORE + t, :], AX.X, ALU.max, negate=True))
                    v.tensor_tensor(bias[:, t:t + 1], neg_max[:, t:t + 1], q_scale[:, slot, t * REP + h:t * REP + h + 1],
                                    ALU.mult).then_inc(bias_done, 1)

            def scale_probs(n, p):
                for t in range(QT):
                    v.wait_ge(exp_done, QT * n + t + 1 + QT)
                    link(v.reciprocal(inv[:, t:t + 1], total[:, t:t + 1]))
                    v.tensor_scalar(prob[:, p, t, :], prob[:, p, t, :], inv[:, t:t + 1], None, ALU.mult).then_inc(scaled, 1)

            def keys_turned(g, slot):
                v.wait_ge(k_hi, g + 1)
                v.tensor_tensor(k_f[1][:, slot, :], proj_flat[:, 0:2 * SEQ], k_f[0][:, slot, :], ALU.subtract).then_inc(k_turned, 1)

            def queries_turned(g, slot):
                v.wait_ge(q_hi, g + 1)
                v.tensor_tensor(q_f[1][:, slot, :, :].rearrange("p h n -> p (h n)"), proj_flat,
                                q_f[0][:, slot, :, :].rearrange("p h n -> p (h n)"), ALU.subtract).then_inc(q_turned, 1)

            def probs_turned(n, t, p):
                v.wait_ge(p_hi, QT * n + t + 1)
                v.tensor_tensor(prob_t[1][:, p, t, :, :].rearrange("p c n -> p (c n)"), psum[:, TURN + t, :],
                                prob_t[0][:, p, t, :, :].rearrange("p c n -> p (c n)"), ALU.subtract).then_inc(p_turned, 1)

            def residual(b):
                v.wait_ge(wo_mm, QH * (b + 1))
                for t in range(QT):
                    x = sh.x_tok[:, bass.ds(QT * b + t, 1), :].rearrange("p a n -> p (a n)")
                    link(v.tensor_tensor(x, x, psum[:, OUT, t * DM:(t + 1) * DM], ALU.add))
                v.sem_inc(y_read, 1)

            w_hi, w_lo = (w[:, :, :, :].rearrange("p c g n -> p (c g n)") for w in w_kv)
            v.wait_ge(w_split, 1)
            v.tensor_tensor(w_lo, kv_raw, w_hi, ALU.subtract).then_inc(w_split, 1)
            queries(0, 0, 0)
            keys(0, 0, 0)
            values(0, 0)
            seeds(0)
            queries_turned(0, 0)
            keys_turned(0, 0)

            def body(b, first, last):
                for kvh, j, more in plan(last):
                    m = REP * kvh + j
                    n, g, nxt = QH * b + m, KVH * b + kvh, (kvh + 1) % 2
                    nb = b if kvh < KVH - 1 else b + 1
                    if m == 3 and not first:
                        residual(b - 1)
                    maxima(n, g, kvh % 2, j)
                    scale_probs(n, m % 2)
                    if more and j == 3:
                        keys_turned(g + 1, nxt)
                    if m >= 1 or not first:
                        for t in range(QT):
                            probs_turned(n - 1, t, (m - 1) % 2)
                    if more and j == 0:
                        queries(g + 1, nb, nxt)
                    if more and j == 1:
                        keys(g + 1, nb, nxt)
                        values(g + 1, nxt)
                        seeds(g + 1)
                    if more and j == 2:
                        queries_turned(g + 1, nxt)

            body(0, True, False)
            first = link.n
            per_seq = 2 * QT * QH + KVH * (3 + 3 * QT + 4) + QT
            with v.Fori(1, BATCH - 1) as b:
                link.base, link.n = first + per_seq * (b - 1), 0
                body(b, False, False)
                assert link.n == per_seq
            link.base, link.n = 0, first + per_seq * (BATCH - 2)
            body(BATCH - 1, False, True)
            for t in range(QT):
                probs_turned(QH * BATCH - 1, t, 1)
            residual(BATCH - 1)
            v.wait_ge(y_read, BATCH)
            v.sem_inc(norm.y_ready, NT)
            norm.vector(v, add=IN_PLACE)
NSH = ISH // IM
NV = NE + NSH
IC = 2
IP = IM // IC


def stage_moe(nc, sh, io):
    with ExitStack() as ctx:
        def sb(name, shape, dt=F32):
            return ctx.enter_context(nc.sbuf_tensor(name, shape, dt))

        w_r = sb("x_w_r", [P, KC, NE + 1])
        w_gu, w_dn = sb("x_w_gu", [P, 2, KC, 2 * IM]), sb("x_w_dn", [IP, 2, IC, DM])
        gu = [sb("x_gu_" + n, [P, 2, KC, 2 * IM], F32R) for n in ("hi", "lo")]
        dn = [sb("x_dn_" + n, [IP, 2, IC, DM], F32R) for n in ("hi", "lo")]
        logit, shifted = sb("x_logit", [P, NT, NE + 1]), sb("x_shifted", [P, NT, NE])
        neg_max, total = sb("x_neg_max", [P, NT]), sb("x_total", [P, NT])
        prob, top, hit = sb("x_prob", [P, NT, NE]), sb("x_top", [P, NT, 8]), sb("x_hit", [P, NT, NE])
        top_at, top_at_f = sb("x_top_at", [P, NT, 8], U32), sb("x_top_at_f", [P, NT, 2])
        expert, expert_f = sb("x_expert", [P, NE], I32), sb("x_expert_f", [P, NE])
        share = sb("x_share", [P, NT, NV])
        zeros = sb("x_zeros", [P, 512])
        silu, hid = sb("x_silu", [P, 2, IM]), sb("x_hid", [P, 2, IM])
        hid_f = [sb("x_hid_f_" + n, [IP, 2, IC, P], F32R) for n in ("hi", "lo")]
        s = sh.sem
        r_loaded, const, r_mm, r_act, v_link = (s("x_" + n) for n in ("r_loaded", "const", "r_mm", "r_act", "v_link"))
        shifted_done, logit_ready = s("x_shifted_done"), s("x_logit_ready")
        gu_loaded = [s(f"x_gu_loaded{i}") for i in range(2)]
        dn_loaded = [s(f"x_dn_loaded{i}") for i in range(2)]
        gu_mm, ht_mm, dn_mm, silu_done, ht_read, hid_done, stored = (s("x_" + n) for n in (
            "gu_mm", "ht_mm", "dn_mm", "silu_done", "ht_read", "hid_done", "stored"))
        ht_hi, w_link, gu_split, dn_split = s("x_ht_hi"), s("x_w_link"), s("x_gu_split"), s("x_dn_split")
        norm = PostNorm(sh, "x")
        psum = sh.psum
        TURN = 2 * NT
        block = ctx.enter_context(nc.Block())

        @block.sync
        def _(sp):
            sp.dma_start(w_r[:, :, :], io["x_w_r"]).then_inc(r_loaded, 16)

            def load(v, slot, first):
                if not first:
                    sp.wait_ge(gu_split, v - 1)
                sp.dma_start(w_gu[:, slot, :, :], io["x_w_gu"][bass.ds(v, 1), :, :, :].rearrange("a p c n -> p (a c) n")).then_inc(gu_loaded[slot], 16)
                if not first:
                    sp.wait_ge(dn_split, v - 1)
                sp.dma_start(w_dn[:, slot, :, :], io["x_w_dn"][bass.ds(v, 1), :, :, :].rearrange("a p c n -> p (a c) n")).then_inc(dn_loaded[slot], 16)

            load(0, 0, True)
            load(1, 1, True)
            with sp.Fori(1, NV // 2) as r:
                for slot in range(2):
                    load(2 * r + slot, slot, False)
            if sh.out is not None:
                for t in range(NT):
                    sp.wait_ge(norm.normed, t + 1)
                    sp.dma_start(sh.out[t * P:(t + 1) * P, :], sh.x_tok[:, t, :]).then_inc(stored, 16)
                sp.wait_ge(stored, 16 * NT)

        @block.gpsimd
        def _(pool):
            pool.memset(zeros[:, :], 0.0).then_inc(const, 1)
            pool.iota(expert[:, :], pattern=[[1, NE]], base=0, channel_multiplier=0).then_inc(const, 1)
            pool.wait_ge(const, 2)
            pool.tensor_copy(expert_f[:, :], expert[:, :]).then_inc(const, 1)
            link = Link(pool, w_link)

            def split_weights(v, slot, first):
                for raw, parts, loaded, used, done in ((w_gu, gu, gu_loaded, gu_mm, gu_split), (w_dn, dn, dn_loaded, dn_mm, dn_split)):
                    link.n = 2 * v + (raw is w_dn)
                    pool.wait_ge(loaded[slot], 8 * (v - slot) + 16)
                    if not first:
                        pool.wait_ge(used, NT * (v - 1))
                    whole = raw[:, slot, :, :].rearrange("p c n -> p (c n)")
                    ones = sh.ones[0:whole.shape[0], 0:1].broadcast_to(whole.shape)
                    link(pool.tensor_tensor(parts[0][:, slot, :, :].rearrange("p c n -> p (c n)"), whole, ones, ALU.mult))
                    pool.tensor_tensor(parts[1][:, slot, :, :], raw[:, slot, :, :], parts[0][:, slot, :, :],
                                       ALU.subtract).then_inc(done, 1)

            split_weights(0, 0, True)
            split_weights(1, 1, True)
            with pool.Fori(1, NV // 2) as r:
                for slot in range(2):
                    split_weights(2 * r + slot, slot, False)

        @block.tensor
        def _(pe):
            pe.wait_ge(r_loaded, 16)
            for t in range(NT):
                for c in range(KC):
                    mm = pe.matmul(psum[:, 0, t * 16:t * 16 + NE + 1], sh.x_feat[:, c, t * P:(t + 1) * P], w_r[:, c, :],
                                   start=c == 0, stop=c == KC - 1)
            mm.then_inc(r_mm, 1)
            pe.wait_ge(const, 1)
            for bank in range(4, 8):
                pe.matmul(psum[:, bank, :], sh.ident[:, :], zeros[:, :], start=True, stop=False, skip_group_check=True)
            pe.wait_ge(logit_ready, 1)

            def expert_of(u, j):
                return (u - j) // NT + j // NT

            def step(u, j, exists):
                if exists(0):
                    if j % NT == 0:
                        pe.wait_ge(gu_split, expert_of(u, j) + 1)
                    if exists(2):
                        pe.wait_ge(hid_done, u - 1)
                    t = j % NT
                    for c in range(KC):
                        mm = split_products(pe, psum[:, j % 2, 0:2 * IM], [x[:, c, t * P:(t + 1) * P] for x in (sh.x_hi, sh.x_lo)],
                                            [w[:, j // NT, c, :] for w in gu], c == 0, c == KC - 1)
                    mm.then_inc(gu_mm, 1)
                if exists(1):
                    pe.wait_ge(hid_done, u)
                    if exists(3):
                        pe.wait_ge(ht_read, u - 2)
                    for c in range(IC):
                        mm = pe.transpose(psum[0:IP, 2 + (j - 1) % 2, c * P:(c + 1) * P], hid[:, (j - 1) % 2, c * IP:(c + 1) * IP], sh.ident[:, :])
                    mm.then_inc(ht_mm, 1)
                if exists(2):
                    jj = (j - 2) % TURN
                    t, slot = jj % NT, jj // NT
                    if t == 0:
                        pe.wait_ge(dn_split, expert_of(u - 2, jj) + 1)
                    pe.wait_ge(ht_read, u - 1)
                    for c in range(IC):
                        mm = split_products(pe, psum[:, 4 + t // 2, (t % 2) * DM:(t % 2 + 1) * DM], [x[:, j % 2, c, :] for x in hid_f],
                                            [w[:, slot, c, :] for w in dn], False, False, skip_group_check=True)
                    mm.then_inc(dn_mm, 1)
            pipeline(pe, NV * NT, TURN, step, 2)

        @block.scalar
        def _(act):
            act.wait_ge(shifted_done, 1)
            act.activation(shifted[:, :, :], shifted[:, :, :], ACT.Exp).then_inc(r_act, 1)
            act.activation(share[:, :, NE:NV], logit[:, :, NE:NE + 1].broadcast_to([P, NT, NSH]), ACT.Sigmoid).then_inc(r_act, 1)

            def step(u, j, exists):
                if exists(0):
                    act.wait_ge(gu_mm, u + 1)
                    if exists(2):
                        act.wait_ge(hid_done, u - 1)
                    act.activation(silu[:, j % 2, :], psum[:, j % 2, 0:IM], ACT.Silu).then_inc(silu_done, 1)
                if exists(1):
                    act.wait_ge(ht_mm, u)
                    if exists(3):
                        act.wait_ge(dn_mm, u - 2)
                    act.activation(hid_f[0][:, (j - 1) % 2, :, :].rearrange("p c n -> p (c n)"), psum[0:IP, 2 + (j - 1) % 2, 0:IC * P],
                                   ACT.Copy).then_inc(ht_hi, 1)
            pipeline(act, NV * NT, TURN, step, 1)

        @block.vector
        def _(v):
            link = Link(v, v_link)
            wide = lambda ap, n=NE: ap.unsqueeze(2).broadcast_to([P, NT, n])
            v.wait_ge(r_mm, 1)
            v.tensor_copy(logit[:, :, :], psum[:, 0, 0:16 * NT].rearrange("p (t n) -> p t n", t=NT)[:, :, 0:NE + 1]).then_inc(logit_ready, 1)
            v.wait_ge(logit_ready, 1)
            link(v.tensor_reduce(neg_max[:, :], logit[:, :, 0:NE], AX.X, ALU.max, negate=True))
            v.tensor_tensor(shifted[:, :, :], logit[:, :, 0:NE], wide(neg_max[:, :]), ALU.add).then_inc(shifted_done, 1)
            v.wait_ge(r_act, 1)
            link(v.tensor_reduce(total[:, :], shifted[:, :, :], AX.X, ALU.add))
            link(v.reciprocal(total[:, :], total[:, :]))
            link(v.tensor_tensor(prob[:, :, :], shifted[:, :, :], wide(total[:, :]), ALU.mult))
            for t in range(NT):
                link.mark(v.max(top[:, t, :], prob[:, t, :]))
            link.wait()
            for t in range(NT):
                link.mark(v.max_index(top_at[:, t, :], top[:, t, :], prob[:, t, :]))
            link.wait()
            link(v.tensor_copy(top_at_f[:, :, :], top_at[:, :, 0:2]))
            link(v.tensor_tensor(total[:, :], top[:, :, 0], top[:, :, 1], ALU.add))
            link(v.reciprocal(total[:, :], total[:, :]))
            v.wait_ge(const, 3)
            for n, out in enumerate((share[:, :, 0:NE], hit[:, :, :])):
                link(v.tensor_tensor(out, expert_f[:, :].unsqueeze(1).broadcast_to([P, NT, NE]), wide(top_at_f[:, :, n]), ALU.is_equal))
                link(v.tensor_tensor(out, out, wide(top[:, :, n]), ALU.mult))
            link(v.tensor_tensor(share[:, :, 0:NE], share[:, :, 0:NE], hit[:, :, :], ALU.add))
            link(v.tensor_tensor(share[:, :, 0:NE], share[:, :, 0:NE], wide(total[:, :]), ALU.mult))
            v.wait_ge(r_act, 2)

            def step(u, j, exists):
                if exists(0):
                    e = (u - j) // NT + j // NT
                    v.wait_ge(silu_done, u + 1)
                    if exists(2):
                        v.wait_ge(ht_mm, u - 1)
                    v.scalar_tensor_tensor(out=hid[:, j % 2, :], in0=silu[:, j % 2, :], scalar=share[:, j % NT, bass.ds(e, 1)],
                                           in1=psum[:, j % 2, IM:2 * IM], op0=ALU.mult, op1=ALU.mult).then_inc(hid_done, 1)
                if exists(1):
                    v.wait_ge(ht_hi, u)
                    v.tensor_tensor(hid_f[1][:, (j - 1) % 2, :, :].rearrange("p c n -> p (c n)"), psum[0:IP, 2 + (j - 1) % 2, 0:IC * P],
                                    hid_f[0][:, (j - 1) % 2, :, :].rearrange("p c n -> p (c n)"), ALU.subtract).then_inc(ht_read, 1)
            pipeline(v, NV * NT, TURN, step, 1)
            v.wait_ge(dn_mm, NV * NT)
            v.sem_inc(norm.y_ready, NT)
            norm.vector(v, add=lambda t: v.tensor_tensor(
                sh.x_tok[:, t, :], sh.x_tok[:, t, :], psum[:, 4 + t // 2, (t % 2) * DM:(t % 2 + 1) * DM], ALU.add))




STAGES = [stage_mamba, stage_token_experts, stage_thought, stage_ssd, stage_attention, stage_moe]


def run_stage(nc, stage, sh, io):
    before = nc.snapshot_sems()
    stage(nc, sh, io)
    nc.clear_and_free_semaphores(nc.allocated_since(before))
    nc.all_engine_barrier()


def build(nc, io, out):
    with ExitStack() as ctx:
        sh = Shared(nc, ctx, out.rearrange("b s d -> (b s) d"))
        for stage in STAGES:
            run_stage(nc, stage, sh, io)


def chunked(a):
    return np.ascontiguousarray(a.reshape(-1, P, a.shape[-1]).transpose(1, 0, 2))


def lay_out(i):
    g = {}
    x = i["x"].reshape(TOK, DM)
    g["x_tok"] = chunked(x)
    g["x_feat"] = chunked(x.T)
    g["m_w_in"] = chunked(i["L0_attn_W_in"])
    g["m_w_x"] = chunked(i["L0_attn_W_x"])
    g["m_w_dt"] = i["L0_attn_W_dt"]
    g["m_w_out"] = chunked(i["L0_attn_W_out"])
    per = lambda a: chunked(a.reshape(a.shape[0], -1)).reshape(P, -1)
    g["m_small"] = np.concatenate([per(i["L0_attn_" + n]) for n in ("conv_w", "conv_b", "b_dt", "A_log", "D")], axis=1)
    g["ctx_feat"] = i["ctx_2048"].transpose(2, 0, 1).reshape(KC, P, BATCH, SEQ).transpose(1, 0, 2, 3)
    g["token_ids"] = i["itok_BxS_13_99985"].reshape(1, TOK)
    ff = lambda n: i["L0_ffn_" + n]
    g["f_small"] = np.concatenate([per(ff(n)) for n in (
        "in_gamma", "in_beta", "pn_gamma", "pn_beta", "agg_b", "d1_b", "d2_b", "bc_b", "gate_b")], axis=1)
    for n in ("agg_w", "d1_w", "d2_w", "bc_w", "gate_w"):
        g["f_" + n] = chunked(ff(n))
    g["f_out_g"], g["f_out_b"] = ff("out_gamma").reshape(1, DM), ff("out_beta").reshape(1, DM)
    w = i["L1_attn_in_proj_w"].T
    feature_tiles = lambda a: a.reshape(KC, P, -1, P).transpose(2, 1, 0, 3)
    hid_gate = np.stack([feature_tiles(w[:, SI:2 * SI]), feature_tiles(w[:, :SI])], axis=2)
    g["s_w_in"] = hid_gate.reshape(NF, P, 2 * KC * P)
    g["s_w_bc"] = feature_tiles(w[:, 2 * SI:2 * SI + NB * P])
    g["s_w_dt"] = chunked(w[:, 2 * SI + NB * P:])
    g["s_head"] = np.stack([i["L1_attn_dt_bias"], i["L1_attn_A_log"]], axis=1)
    g["s_conv"] = chunked(np.concatenate([i["L1_attn_conv_w"][:, 0, :], i["L1_attn_conv_b"][:, None]], axis=1))
    g["s_norm_w"] = per(i["L1_attn_norm_w"])
    g["s_d"] = i["L1_attn_D"].reshape(1, SH)
    g["s_w_out"] = i["L1_attn_out_proj_w"].T.reshape(NF, P, DM)
    g["r_pos"] = np.concatenate([i["pos_BxS2"], i["itok_BxS_4096_4607"]], axis=1).reshape(BATCH * KT, P).T
    freq = (1.0 / np.float32(10000.0) ** (np.arange(0, HD, 2, dtype=np.float32) / HD)).astype(np.float32)
    g["r_rows"] = np.concatenate([freq, i["L1_xattn_q_norm_w"], i["L1_xattn_k_norm_w"]]).reshape(1, 5 * ROPE)[:, None, :][0]
    xa = lambda n: chunked(i["L1_xattn_" + n].T)
    g["a_w_kv"] = np.concatenate([xa("Wk").reshape(P, KC, KVH, HD), xa("Wv").reshape(P, KC, KVH, HD)], axis=3)
    g["a_w_q"] = xa("Wq").reshape(P, KC, KVH, REP * HD)
    g["a_w_o"] = xa("Wo")
    rows = np.concatenate([i["L1_ffn_router_weight"], i["L1_ffn_shared_gate_w"]], axis=0)
    g["x_w_r"] = chunked(rows.T)
    shared = lambda n: i["L1_ffn_" + n].reshape(NSH, IM, DM)
    gu = np.concatenate([i["L1_ffn_gate_up_proj"],
                         np.concatenate([shared("sh_gate_w"), shared("sh_up_w")], axis=1)], axis=0)
    g["x_w_gu"] = gu.transpose(0, 2, 1).reshape(NV, KC, P, 2 * IM).transpose(0, 2, 1, 3)
    dn = np.concatenate([i["L1_ffn_down_proj"], i["L1_ffn_sh_down_w"].reshape(DM, NSH, IM).transpose(1, 0, 2)], axis=0)
    g["x_w_dn"] = dn.transpose(0, 2, 1).reshape(NV, IC, IP, DM).transpose(0, 2, 1, 3)
    return {name: np.ascontiguousarray(a) for name, a in g.items()}


def kernel(**inputs):
    import concourse.bacc as bacc
    from concourse.bass_utils import run_bass_kernel_spmd

    nc = bacc.Bacc("TRN2", target_bir_lowering=False, num_devices=1)
    arrays = {f"in_{n}": a for n, a in lay_out({n: np.asarray(a) for n, a in inputs.items()}).items()}
    io = {n[3:]: nc.dram_tensor(n, a.shape, mybir.dt.from_np(a.dtype), kind="ExternalInput").ap() for n, a in arrays.items()}
    out = nc.dram_tensor("out", (BATCH, SEQ, DM), F32, kind="ExternalOutput").ap()
    build(nc, io, out)
    return run_bass_kernel_spmd(nc, [arrays], core_ids=[0]).results[0]["out"]
```
